# Optimizing a Trainium2 kernel written in Bass

```python
import numpy as np
import jax
import jax.numpy as jnp

def _softmax(x, axis=-1):
    return jax.nn.softmax(x, axis=axis)

def _gelu(x):
    return jax.nn.gelu(x, approximate=True)

def _silu(x):
    return jax.nn.silu(x)

def _sigmoid(x):
    return jax.nn.sigmoid(x)

def _layernorm(x, axis=-1, eps=1e-05):
    m = jnp.mean(x, axis=axis, keepdims=True)
    v = jnp.var(x, axis=axis, keepdims=True)
    return (x - m) / jnp.sqrt(v + eps)

def _scatter_add(tgt, idx, src, axis=0):
    return tgt.at[idx].add(src)

def _segment_sum(src, seg, n):
    return jax.ops.segment_sum(src, seg, n)
kernel_name = 'mk_vit_tower_d2_tok_img1024_r4_6803d2'

def setup_inputs(seed: int=0):
    np.random.seed(seed)
    _w = jnp.asarray

    def _rec_inputs():
        import jax
        import jax.numpy as jnp
        _rk = jax.random.key(seed)
        x = -0.000348323 + 0.999952 * jax.random.normal(jax.random.fold_in(_rk, 1), (16, 3, 96, 96), jnp.float32)
        return x
    x = _rec_inputs()

    def _L0_tok_setup():
        import jax, jax.numpy as jnp
        import numpy as np
        from jax import lax
        PATCH = 16
        key = jax.random.key(seed)
        k1, k2 = jax.random.split(key)
        B, C, IMG, HID = (32, 3, 96, 256)
        inputs = jax.random.normal(k1, (B, C, IMG, IMG), dtype=jnp.float32)
        flat = C * PATCH * PATCH
        W = jax.random.normal(k2, (flat, HID), dtype=jnp.float32) / np.sqrt(flat)
        return {'inputs': inputs, 'W': W}
    _L0_tok_all = _L0_tok_setup()
    _L0_tok_in = {k: v for k, v in _L0_tok_all.items() if k in ('W',)}
    del _L0_tok_all

    def _L0_attn_setup():
        import jax, jax.numpy as jnp
        import numpy as np
        B, S, H, L = (4, 512, 256, 4)
        CLAMP_LO, CLAMP_HI = (1e-08, 1.0 - 1e-08)
        LN_EPS = 1e-05

        def _linear_scan(a, b):

            def combine(left, right):
                al, bl = left
                ar, br = right
                return (ar * al, ar * bl + br)
            _, h = jax.lax.associative_scan(combine, (a, b), axis=1)
            return h

        def _mingru(x, Wz, bz, Wh, bh):
            z = jax.nn.sigmoid(jnp.einsum('bsi,hi->bsh', x, Wz) + bz)
            h_tilde = jnp.tanh(jnp.einsum('bsi,hi->bsh', x, Wh) + bh)
            a = jnp.clip(1.0 - z, CLAMP_LO, CLAMP_HI)
            return _linear_scan(a, z * h_tilde)

        def _layernorm(x, gamma, beta):
            mu = jnp.mean(x, axis=-1, keepdims=True)
            var = jnp.mean(jnp.square(x - mu), axis=-1, keepdims=True)
            return (x - mu) * jax.lax.rsqrt(var + LN_EPS) * gamma + beta

        def _stack(x, Wz, bz, Wh, bh, gamma, beta):
            h = x
            for i in range(L):
                h_new = _mingru(h, Wz[i], bz[i], Wh[i], bh[i])
                if i > 0:
                    h_new = h_new + h
                h = _layernorm(h_new, gamma, beta)
            return h
        key = jax.random.key(seed)
        ks = jax.random.split(key, 13)
        s = 1.0 / np.sqrt(H)
        u = lambda k, shape: jax.random.uniform(k, shape, jnp.float32, -s, s)
        return {'x': jax.random.normal(ks[0], (B, S, H), jnp.float32), 'fwd_Wz': u(ks[1], (L, H, H)), 'fwd_bz': u(ks[2], (L, H)), 'fwd_Wh': u(ks[3], (L, H, H)), 'fwd_bh': u(ks[4], (L, H)), 'bwd_Wz': u(ks[5], (L, H, H)), 'bwd_bz': u(ks[6], (L, H)), 'bwd_Wh': u(ks[7], (L, H, H)), 'bwd_bh': u(ks[8], (L, H)), 'fusion_W': u(ks[9], (H, 2 * H)), 'fusion_b': u(ks[10], (H,)), 'ln_gamma': jnp.ones((H,), jnp.float32), 'ln_beta': jnp.zeros((H,), jnp.float32)}
    _L0_attn_all = _L0_attn_setup()
    _L0_attn_in = {k: v for k, v in _L0_attn_all.items() if k in ('fwd_Wz', 'fwd_bz', 'fwd_Wh', 'fwd_bh', 'bwd_Wz', 'bwd_bz', 'bwd_Wh', 'bwd_bh', 'fusion_W', 'fusion_b', 'ln_gamma', 'ln_beta')}
    del _L0_attn_all

    def _L0_ffn_setup():
        import jax, jax.numpy as jnp
        import numpy as np
        TOP_K = 2
        key = jax.random.key(seed)
        k1, k2, k3, k4 = jax.random.split(key, 4)
        B, S, H, I, E = (2, 512, 256, 1024, 8)
        return {'hidden_states': jax.random.normal(k1, (B, S, H), jnp.float32), 'gate_w': jax.random.normal(k2, (E, H), jnp.float32) * 0.02, 'gate_up_proj': jax.random.normal(k3, (E, 2 * I, H), jnp.float32) * 0.02, 'down_proj': jax.random.normal(k4, (E, H, I), jnp.float32) * 0.02}
    _L0_ffn_all = _L0_ffn_setup()
    _L0_ffn_in = {k: v for k, v in _L0_ffn_all.items() if k in ('gate_w', 'gate_up_proj', 'down_proj')}
    del _L0_ffn_all

    def _L1_attn_setup():
        import jax, jax.numpy as jnp
        import numpy as np
        MAX_LR = 0.01
        NS_A, NS_B, NS_C = (3.4445, -4.775, 2.0315)

        def newtonschulz5(G, steps=5, eps=1e-07):
            transpose = G.shape[-2] > G.shape[-1]
            X = jnp.swapaxes(G, -2, -1) if transpose else G
            X = X / (jnp.linalg.norm(X, axis=(-2, -1), keepdims=True) + eps)
            for _ in range(steps):
                A = X @ jnp.swapaxes(X, -2, -1)
                Bm = NS_B * A + NS_C * (A @ A)
                X = NS_A * X + Bm @ X
            return jnp.swapaxes(X, -2, -1) if transpose else X

        def _reference_tuple_inner(tokens, wq, wk, wv, wo, w_lr, w_target, w_gates, rms_w):
            N = tokens.shape[1]
            scale = wq.shape[-1] ** (-0.5)
            eps = jnp.finfo(tokens.dtype).eps
            t = tokens * jax.lax.rsqrt(jnp.mean(tokens * tokens, -1, keepdims=True) + eps) * rms_w
            gates = jnp.swapaxes(jax.nn.sigmoid(t @ w_gates), -2, -1)[..., None]
            q = jnp.einsum('bnd,hde->bhne', t, wq)
            k = jnp.einsum('bnd,hde->bhne', t, wk)
            v = jnp.einsum('bnd,hde->bhne', t, wv)
            score = jnp.einsum('bhie,bhje->bhij', q, k) * scale
            causal_mask = jnp.triu(jnp.ones((N, N), bool), 1)
            score = jnp.where(causal_mask, -jnp.finfo(score.dtype).max, score)
            attn = jax.nn.softmax(score, axis=-1)
            out = jnp.einsum('bhij,bhje->bhie', attn, v) * gates
            pred_values = jnp.einsum('bhne,hed->bnd', out, wo)
            tv = t[:, 1:] @ w_target
            tv = (tv - tv.mean(-1, keepdims=True)) * jax.lax.rsqrt(tv.var(-1, keepdims=True) + 1e-05)
            ts = t[:, :-1]
            pv = pred_values[:, :-1]
            o = out[:, :, :-1]
            g = gates[:, :, :-1]
            a = attn[:, :, :-1, :-1]
            qs, ks_, vs = (q[:, :, :-1], k[:, :, :-1], v[:, :, :-1])
            lrs = jax.nn.sigmoid(ts @ w_lr) * MAX_LR
            lr, mlr = (lrs[..., 0], lrs[..., 1])
            error = tv - pv
            dout = jnp.einsum('bnd,hed->bhne', error, wo)
            du = dout * g
            delta = jnp.sum(dout * o, -1, keepdims=True)
            dv = jnp.einsum('bhij,bhie->bhje', a, du)
            dattn = jnp.einsum('bhje,bhie->bhij', vs, du)
            dscore = scale * a * (dattn - delta)
            dq = jnp.einsum('bhje,bhij->bhie', ks_, dscore)
            dk = jnp.einsum('bhie,bhij->bhje', qs, dscore)
            t_qk = ts * lr[..., None]
            t_v = ts * mlr[..., None]
            o_wo = o * mlr[:, None, :, None]
            dwq = jnp.einsum('bhie,bid->bhde', dq, t_qk)
            dwk = jnp.einsum('bhje,bjd->bhde', dk, t_qk)
            dwv = jnp.einsum('bhje,bjd->bhde', dv, t_v)
            dwo = jnp.einsum('bnd,bhne->bhed', error, o_wo)
            dwv = newtonschulz5(dwv)
            dwo = newtonschulz5(dwo)
            return (pred_values, dwq, dwk, dwv, dwo)
        key = jax.random.key(seed)
        ks = jax.random.split(key, 9)
        B, N, D, H, DH = (4, 256, 256, 8, 64)
        s = D ** (-0.5)
        return {'tokens': jax.random.normal(ks[0], (B, N, D), jnp.float32), 'wq': jax.random.normal(ks[1], (H, D, DH), jnp.float32) * s, 'wk': jax.random.normal(ks[2], (H, D, DH), jnp.float32) * s, 'wv': jax.random.normal(ks[3], (H, D, DH), jnp.float32) * s, 'wo': jax.random.normal(ks[4], (H, DH, D), jnp.float32) * s, 'w_lr': jax.random.normal(ks[5], (D, 2), jnp.float32) * 0.02, 'w_target': jax.random.normal(ks[6], (D, D), jnp.float32) * 0.02, 'w_gates': jax.random.normal(ks[7], (D, H), jnp.float32) * 0.02, 'rms_w': jnp.ones((D,), jnp.float32)}
    _L1_attn_all = _L1_attn_setup()
    _L1_attn_in = {k: v for k, v in _L1_attn_all.items() if k in ('wq', 'wk', 'wv', 'wo', 'w_lr', 'w_target', 'w_gates', 'rms_w')}
    del _L1_attn_all

    def _L1_ffn_setup():
        import jax, jax.numpy as jnp
        import numpy as np
        LN_EPS = 1e-05

        def layer_norm(x, g, b):
            mu = jnp.mean(x, axis=-1, keepdims=True)
            var = jnp.mean(jnp.square(x - mu), axis=-1, keepdims=True)
            return (x - mu) * jax.lax.rsqrt(var + LN_EPS) * g + b

        def ternary_quant(w):
            scale = 1.0 / jnp.clip(jnp.mean(jnp.abs(w)), 1e-05)
            wq = jnp.clip(jnp.round(w * scale), -1.0, 1.0) / scale
            return w + jax.lax.stop_gradient(wq - w)
        key = jax.random.key(seed)
        ks = jax.random.split(key, 3)
        dim, hidden = (256, 1024)
        B, S = (8, 256)
        x = jax.random.normal(ks[0], (B, S, dim), dtype=jnp.float32)
        w1 = jax.random.normal(ks[1], (hidden, dim), dtype=jnp.float32) * 0.02
        w2 = jax.random.normal(ks[2], (dim, hidden), dtype=jnp.float32) * 0.02
        return {'x': x, 'ln1_g': jnp.ones((dim,), jnp.float32), 'ln1_b': jnp.zeros((dim,), jnp.float32), 'w1': w1, 'b1': jnp.zeros((hidden,), jnp.float32), 'ln2_g': jnp.ones((hidden,), jnp.float32), 'ln2_b': jnp.zeros((hidden,), jnp.float32), 'w2': w2, 'b2': jnp.zeros((dim,), jnp.float32)}
    _L1_ffn_all = _L1_ffn_setup()
    _L1_ffn_in = {k: v for k, v in _L1_ffn_all.items() if k in ('ln1_g', 'ln1_b', 'w1', 'b1', 'ln2_g', 'ln2_b', 'w2', 'b2')}
    del _L1_ffn_all
    return {'x': x, 'L0_tok_W': _L0_tok_in['W'], 'L0_attn_fwd_Wz': _L0_attn_in['fwd_Wz'], 'L0_attn_fwd_bz': _L0_attn_in['fwd_bz'], 'L0_attn_fwd_Wh': _L0_attn_in['fwd_Wh'], 'L0_attn_fwd_bh': _L0_attn_in['fwd_bh'], 'L0_attn_bwd_Wz': _L0_attn_in['bwd_Wz'], 'L0_attn_bwd_bz': _L0_attn_in['bwd_bz'], 'L0_attn_bwd_Wh': _L0_attn_in['bwd_Wh'], 'L0_attn_bwd_bh': _L0_attn_in['bwd_bh'], 'L0_attn_fusion_W': _L0_attn_in['fusion_W'], 'L0_attn_fusion_b': _L0_attn_in['fusion_b'], 'L0_attn_ln_gamma': _L0_attn_in['ln_gamma'], 'L0_attn_ln_beta': _L0_attn_in['ln_beta'], 'L0_ffn_gate_w': _L0_ffn_in['gate_w'], 'L0_ffn_gate_up_proj': _L0_ffn_in['gate_up_proj'], 'L0_ffn_down_proj': _L0_ffn_in['down_proj'], 'L1_attn_wq': _L1_attn_in['wq'], 'L1_attn_wk': _L1_attn_in['wk'], 'L1_attn_wv': _L1_attn_in['wv'], 'L1_attn_wo': _L1_attn_in['wo'], 'L1_attn_w_lr': _L1_attn_in['w_lr'], 'L1_attn_w_target': _L1_attn_in['w_target'], 'L1_attn_w_gates': _L1_attn_in['w_gates'], 'L1_attn_rms_w': _L1_attn_in['rms_w'], 'L1_ffn_ln1_g': _L1_ffn_in['ln1_g'], 'L1_ffn_ln1_b': _L1_ffn_in['ln1_b'], 'L1_ffn_w1': _L1_ffn_in['w1'], 'L1_ffn_b1': _L1_ffn_in['b1'], 'L1_ffn_ln2_g': _L1_ffn_in['ln2_g'], 'L1_ffn_ln2_b': _L1_ffn_in['ln2_b'], 'L1_ffn_w2': _L1_ffn_in['w2'], 'L1_ffn_b2': _L1_ffn_in['b2']}

def reference(x, L0_tok_W, L0_attn_fwd_Wz, L0_attn_fwd_bz, L0_attn_fwd_Wh, L0_attn_fwd_bh, L0_attn_bwd_Wz, L0_attn_bwd_bz, L0_attn_bwd_Wh, L0_attn_bwd_bh, L0_attn_fusion_W, L0_attn_fusion_b, L0_attn_ln_gamma, L0_attn_ln_beta, L0_ffn_gate_w, L0_ffn_gate_up_proj, L0_ffn_down_proj, L1_attn_wq, L1_attn_wk, L1_attn_wv, L1_attn_wo, L1_attn_w_lr, L1_attn_w_target, L1_attn_w_gates, L1_attn_rms_w, L1_ffn_ln1_g, L1_ffn_ln1_b, L1_ffn_w1, L1_ffn_b1, L1_ffn_ln2_g, L1_ffn_ln2_b, L1_ffn_w2, L1_ffn_b2):
    import jax
    import jax.numpy as jnp

    def _L0_tok_ref(inputs, W):
        import jax, jax.numpy as jnp
        import numpy as np
        from jax import lax
        PATCH = 16
        B, C, H, Wimg = inputs.shape
        patches = lax.conv_general_dilated_patches(inputs, filter_shape=[PATCH, PATCH], window_strides=[PATCH, PATCH], padding='VALID', dimension_numbers=('NCHW', 'HWIO', 'NCHW'))
        patches = patches.reshape(B, -1, C * PATCH * PATCH)
        return jnp.einsum('bnf,fh->bnh', patches, W)

    def _L0_attn_ref(x, fwd_Wz, fwd_bz, fwd_Wh, fwd_bh, bwd_Wz, bwd_bz, bwd_Wh, bwd_bh, fusion_W, fusion_b, ln_gamma, ln_beta):
        import jax, jax.numpy as jnp
        import numpy as np
        B, S, H, L = (4, 512, 256, 4)
        CLAMP_LO, CLAMP_HI = (1e-08, 1.0 - 1e-08)
        LN_EPS = 1e-05

        def _linear_scan(a, b):

            def combine(left, right):
                al, bl = left
                ar, br = right
                return (ar * al, ar * bl + br)
            _, h = jax.lax.associative_scan(combine, (a, b), axis=1)
            return h

        def _mingru(x, Wz, bz, Wh, bh):
            z = jax.nn.sigmoid(jnp.einsum('bsi,hi->bsh', x, Wz) + bz)
            h_tilde = jnp.tanh(jnp.einsum('bsi,hi->bsh', x, Wh) + bh)
            a = jnp.clip(1.0 - z, CLAMP_LO, CLAMP_HI)
            return _linear_scan(a, z * h_tilde)

        def _layernorm(x, gamma, beta):
            mu = jnp.mean(x, axis=-1, keepdims=True)
            var = jnp.mean(jnp.square(x - mu), axis=-1, keepdims=True)
            return (x - mu) * jax.lax.rsqrt(var + LN_EPS) * gamma + beta

        def _stack(x, Wz, bz, Wh, bh, gamma, beta):
            h = x
            for i in range(L):
                h_new = _mingru(h, Wz[i], bz[i], Wh[i], bh[i])
                if i > 0:
                    h_new = h_new + h
                h = _layernorm(h_new, gamma, beta)
            return h
        h_fwd = _stack(x, fwd_Wz, fwd_bz, fwd_Wh, fwd_bh, ln_gamma, ln_beta)
        h_bwd = _stack(jnp.flip(x, axis=1), bwd_Wz, bwd_bz, bwd_Wh, bwd_bh, ln_gamma, ln_beta)
        h_bwd = jnp.flip(h_bwd, axis=1)
        h_comb = jnp.concatenate([h_fwd, h_bwd], axis=-1)
        return jnp.einsum('bsi,hi->bsh', h_comb, fusion_W) + fusion_b

    def _L0_ffn_ref(hidden_states, gate_w, gate_up_proj, down_proj):
        import jax, jax.numpy as jnp
        import numpy as np
        TOP_K = 2
        B, S, H = hidden_states.shape
        E = gate_w.shape[0]
        x = hidden_states.reshape(-1, H)
        T = x.shape[0]
        probs = jax.nn.softmax(x @ gate_w.T, axis=-1)
        w, idx = jax.lax.top_k(probs, TOP_K)
        w = w / jnp.sum(w, axis=-1, keepdims=True)
        combine = jnp.zeros((T, E), x.dtype).at[jnp.arange(T)[:, None], idx].add(w)

        def step(acc, inputs):
            gup, dn, ce = inputs
            g, u = jnp.split(x @ gup.T, 2, axis=-1)
            acc = acc + ce[:, None] * (jax.nn.silu(g) * u @ dn.T)
            return (acc, None)
        out, _ = jax.lax.scan(step, jnp.zeros_like(x), (gate_up_proj, down_proj, combine.T))
        return out.reshape(B, S, H)

    def _L1_attn_ref(tokens, wq, wk, wv, wo, w_lr, w_target, w_gates, rms_w):
        import jax, jax.numpy as jnp
        import numpy as np
        MAX_LR = 0.01
        NS_A, NS_B, NS_C = (3.4445, -4.775, 2.0315)

        def newtonschulz5(G, steps=5, eps=1e-07):
            transpose = G.shape[-2] > G.shape[-1]
            X = jnp.swapaxes(G, -2, -1) if transpose else G
            X = X / (jnp.linalg.norm(X, axis=(-2, -1), keepdims=True) + eps)
            for _ in range(steps):
                A = X @ jnp.swapaxes(X, -2, -1)
                Bm = NS_B * A + NS_C * (A @ A)
                X = NS_A * X + Bm @ X
            return jnp.swapaxes(X, -2, -1) if transpose else X

        def _reference_tuple_inner(tokens, wq, wk, wv, wo, w_lr, w_target, w_gates, rms_w):
            N = tokens.shape[1]
            scale = wq.shape[-1] ** (-0.5)
            eps = jnp.finfo(tokens.dtype).eps
            t = tokens * jax.lax.rsqrt(jnp.mean(tokens * tokens, -1, keepdims=True) + eps) * rms_w
            gates = jnp.swapaxes(jax.nn.sigmoid(t @ w_gates), -2, -1)[..., None]
            q = jnp.einsum('bnd,hde->bhne', t, wq)
            k = jnp.einsum('bnd,hde->bhne', t, wk)
            v = jnp.einsum('bnd,hde->bhne', t, wv)
            score = jnp.einsum('bhie,bhje->bhij', q, k) * scale
            causal_mask = jnp.triu(jnp.ones((N, N), bool), 1)
            score = jnp.where(causal_mask, -jnp.finfo(score.dtype).max, score)
            attn = jax.nn.softmax(score, axis=-1)
            out = jnp.einsum('bhij,bhje->bhie', attn, v) * gates
            pred_values = jnp.einsum('bhne,hed->bnd', out, wo)
            tv = t[:, 1:] @ w_target
            tv = (tv - tv.mean(-1, keepdims=True)) * jax.lax.rsqrt(tv.var(-1, keepdims=True) + 1e-05)
            ts = t[:, :-1]
            pv = pred_values[:, :-1]
            o = out[:, :, :-1]
            g = gates[:, :, :-1]
            a = attn[:, :, :-1, :-1]
            qs, ks_, vs = (q[:, :, :-1], k[:, :, :-1], v[:, :, :-1])
            lrs = jax.nn.sigmoid(ts @ w_lr) * MAX_LR
            lr, mlr = (lrs[..., 0], lrs[..., 1])
            error = tv - pv
            dout = jnp.einsum('bnd,hed->bhne', error, wo)
            du = dout * g
            delta = jnp.sum(dout * o, -1, keepdims=True)
            dv = jnp.einsum('bhij,bhie->bhje', a, du)
            dattn = jnp.einsum('bhje,bhie->bhij', vs, du)
            dscore = scale * a * (dattn - delta)
            dq = jnp.einsum('bhje,bhij->bhie', ks_, dscore)
            dk = jnp.einsum('bhie,bhij->bhje', qs, dscore)
            t_qk = ts * lr[..., None]
            t_v = ts * mlr[..., None]
            o_wo = o * mlr[:, None, :, None]
            dwq = jnp.einsum('bhie,bid->bhde', dq, t_qk)
            dwk = jnp.einsum('bhje,bjd->bhde', dk, t_qk)
            dwv = jnp.einsum('bhje,bjd->bhde', dv, t_v)
            dwo = jnp.einsum('bnd,bhne->bhed', error, o_wo)
            dwv = newtonschulz5(dwv)
            dwo = newtonschulz5(dwo)
            return (pred_values, dwq, dwk, dwv, dwo)
        return _reference_tuple_inner(tokens, wq, wk, wv, wo, w_lr, w_target, w_gates, rms_w)[0]

    def _L1_ffn_ref(x, ln1_g, ln1_b, w1, b1, ln2_g, ln2_b, w2, b2):
        import jax, jax.numpy as jnp
        import numpy as np
        LN_EPS = 1e-05

        def layer_norm(x, g, b):
            mu = jnp.mean(x, axis=-1, keepdims=True)
            var = jnp.mean(jnp.square(x - mu), axis=-1, keepdims=True)
            return (x - mu) * jax.lax.rsqrt(var + LN_EPS) * g + b

        def ternary_quant(w):
            scale = 1.0 / jnp.clip(jnp.mean(jnp.abs(w)), 1e-05)
            wq = jnp.clip(jnp.round(w * scale), -1.0, 1.0) / scale
            return w + jax.lax.stop_gradient(wq - w)
        h = layer_norm(x, ln1_g, ln1_b)
        h = jnp.einsum('bsd,hd->bsh', h, ternary_quant(w1)) + b1
        h = jax.nn.gelu(h, approximate=False)
        h = layer_norm(h, ln2_g, ln2_b)
        out = jnp.einsum('bsh,dh->bsd', h, ternary_quant(w2)) + b2
        return out
    h = _L0_tok_ref(x, L0_tok_W)
    h = h + _L0_attn_ref(_layernorm(h, axis=-1), L0_attn_fwd_Wz, L0_attn_fwd_bz, L0_attn_fwd_Wh, L0_attn_fwd_bh, L0_attn_bwd_Wz, L0_attn_bwd_bz, L0_attn_bwd_Wh, L0_attn_bwd_bh, L0_attn_fusion_W, L0_attn_fusion_b, L0_attn_ln_gamma, L0_attn_ln_beta)
    h = h + _L0_ffn_ref(_layernorm(h, axis=-1), L0_ffn_gate_w, L0_ffn_gate_up_proj, L0_ffn_down_proj)
    h = h + _L1_attn_ref(_layernorm(h, axis=-1), L1_attn_wq, L1_attn_wk, L1_attn_wv, L1_attn_wo, L1_attn_w_lr, L1_attn_w_target, L1_attn_w_gates, L1_attn_rms_w)
    h = h + _L1_ffn_ref(_layernorm(h, axis=-1), L1_ffn_ln1_g, L1_ffn_ln1_b, L1_ffn_w1, L1_ffn_b1, L1_ffn_ln2_g, L1_ffn_ln2_b, L1_ffn_w2, L1_ffn_b2)
    return h

_drawn_inputs = setup_inputs


def setup_inputs(seed=0):
    import zlib

    import numpy as np

    out = dict(_drawn_inputs(seed))
    spreads = {'L0_attn_ln_gamma': (1.0, 0.2),
     'L0_attn_ln_beta': (0.0, 0.1),
     'L1_attn_rms_w': (1.0, 0.2),
     'L1_ffn_ln1_g': (1.0, 0.2),
     'L1_ffn_ln1_b': (0.0, 0.337),
     'L1_ffn_b1': (0.0, 0.1),
     'L1_ffn_ln2_g': (1.0, 0.2),
     'L1_ffn_ln2_b': (0.0, 0.305),
     'L1_ffn_b2': (0.0, 0.1)}
    factors = {'L0_attn_fwd_bz': 8.0,
     'L0_attn_bwd_bz': 7.663,
     'L0_ffn_gate_w': 3.842,
     'L0_ffn_gate_up_proj': 3.364,
     'L0_ffn_down_proj': 3.358}
    for name, (base, spread) in spreads.items():
        noise = np.random.default_rng([zlib.crc32(name.encode()), seed]).standard_normal(out[name].shape)
        drawn = base * np.exp(spread * noise) if base else spread * noise
        out[name] = jnp.asarray(drawn.astype(out[name].dtype))
    for name, factor in factors.items():
        out[name] = (out[name] * factor).astype(out[name].dtype)
    return out
```

```python
from contextlib import ExitStack

import concourse.bass as bass
from concourse import mybir

F32 = mybir.dt.float32
F32R = mybir.dt.float32r
ALU = mybir.AluOpType
ACT = mybir.ActivationFunctionType
AX_X = mybir.AxisListType.X

P = 128
B, S = 16, 36
T = B * S
H = 256
KH = H // P
NT = T // 2
TT = 96
JT = NT // TT
FLAT = 768
KF = FLAT // P
L = 4
UNITS = 4
STEPS = L * UNITS
E = 8
I = 1024
KI = I // P
HEADS, DH = 8, 64
AT = 2 * S
NAT = T // AT
EPS = 1e-5
RMS_EPS = 1.1920928955078125e-07
MASKED = -1e30

V_BZ, V_BH, V_GAM, V_BET, V_FB, V_RMS = 0, 16, 32, 34, 36, 38
V_L1G, V_L1B, V_B1, V_GB2, V_B2, V_N = 40, 42, 44, 52, 68, 70

LN_IN = 0
LN_GRU = 2
LN_MOE = 18
LN_ATT = 20
LN_MLP = 22
LN_ALL = 24


def tower(nc, patches, w_tok, w_gru, w_fus, vecs, w_gate, w_up, w_down, w_qkv, w_gates, w_o, w_1, w_2, out):
    with ExitStack() as ctx:
        def sb(name, shape, dt=F32):
            return ctx.enter_context(nc.sbuf_tensor(name, shape, dt))

        def sem(name):
            return ctx.enter_context(nc.semaphore(name))

        bank = ctx.enter_context(nc.psum_tensor("bank", [P, 8, 512], F32))

        xp = sb("xp", [P, KF, T])
        wt = sb("wt", [P, KF, H])
        wg = sb("wg", [P, L, 2, 2, KH, H])
        wf = sb("wf", [P, 4, H])
        vec = sb("vec", [P, V_N])
        wr = sb("wr", [P, KH, E])
        wqkv = sb("wqkv", [P, KH, 3 * HEADS * DH])
        wga = sb("wga", [P, KH, HEADS])
        wo = sb("wo", [P, 4, H])
        wup = [sb(f"wup{i}", [P, KH, 2 * I]) for i in range(2)]
        wdn2 = sb("wdn2", [P, 2, KI, H])
        wdn = [wdn2[:, i] for i in range(2)]
        ident = sb("ident", [P, P])
        ones = sb("ones", [P, P])
        mean_h = sb("mean_h", [P, 1])
        mean_i = sb("mean_i", [P, 1])
        half_neg = sb("half_neg", [P, JT])
        nbz = sb("nbz", [P, 16])
        cmask = sb("cmask", [AT, AT])
        ranks = sb("ranks", [P, E])
        h = sb("h", [P, KH, T])
        xn = sb("xn", [P, KH, T])
        zz = [sb(f"zz{i}", [P, KH, NT]) for i in range(2)]
        aa = [sb(f"aa{i}", [P, KH, NT]) for i in range(2)]
        tt = [sb(f"tt{i}", [P, KH, NT]) for i in range(2)]
        gru_y = sb("gru_y", [P, UNITS, KH, NT])
        gru_x = sb("gru_x", [P, UNITS, KH, NT])
        yy = [gru_y[:, i] for i in range(UNITS)]
        xx = [gru_x[:, i] for i in range(UNITS)]
        sq = [sb(f"sq{i}", [P, KH, NT]) for i in range(2)]
        stat = sb("stat", [TT, 6])
        msq = sb("msq", [TT, 3])
        var = sb("var", [TT, 3])
        ve = sb("ve", [TT, 3])
        rm = [sb(f"rm{i}", [TT, 6]) for i in range(2)]

        s_load = {n: sem("s_load_" + n) for n in
                  ("xp", "wt", "wg0", "wg1", "wg2", "wg3", "wf", "vec", "wr", "wqkv", "wga", "wo", "w1", "w2")}
        s_up = [sem(f"s_up{i}") for i in range(2)]; s_dn = [sem(f"s_dn{i}") for i in range(2)]
        s_const = sem("s_const")
        s_vconst = sem("s_vconst")
        s_tok = sem("s_tok")
        s_h0 = sem("s_h0")
        s_sq = sem("s_sq")
        s_st = sem("s_st")
        s_ve = sem("s_ve")
        s_pow = sem("s_pow")
        s_rm = sem("s_rm")
        s_bc = sem("s_bc")
        s_norm = sem("s_norm")
        s_aff = sem("s_aff")
        s_zmm = sem("s_zmm"); s_hmm = sem("s_hmm")
        s_gz = sem("s_gz"); s_gt = sem("s_gt")
        s_clip = sem("s_clip"); s_edge = sem("s_edge")
        s_y = sem("s_y")
        s_fus = sem("s_fus"); s_hf = sem("s_hf")
        s_v = sem("s_v")

        chain = [0]

        def link(dve, ins):
            chain[0] += 1
            ins.then_inc(s_v, 1)
            dve.wait_ge(s_v, chain[0])

        def both(x):
            return x[:].rearrange("p k t -> p (k t)")

        def unit(s):
            return s // UNITS, s % UNITS, s % 2, (s % UNITS) // 2

        def half(n):
            return slice(n * NT, (n + 1) * NT)

        def ln_source(i):
            if LN_GRU <= i < LN_MOE:
                return yy[(i - LN_GRU) % UNITS]
            return h[:, :, half(i % 2)]

        def ln_target(i):
            if LN_GRU <= i < LN_MOE:
                return yy[(i - LN_GRU) % UNITS]
            return xn[:, :, half(i % 2)]

        def affine_count(i):
            return max(0, min(i + 1, LN_MOE) - LN_GRU) + max(0, i + 1 - LN_ATT)

        mx1 = sb("mx1", [TT, 6, 1]); keys = sb("keys", [TT, 6, E]); pr = sb("pr", [TT, 6, E]); eq = sb("eq", [TT, 6, E])
        sel = sb("sel", [TT, 2, 6, E]); top = sb("top", [TT, 2, 6]); den = sb("den", [TT, 6]); comb = sb("comb", [TT, 6, E])
        cb = wg[:].rearrange("p l d g k n -> p (l d g k n)")[:, 0:E * T].rearrange("p (e t) -> p e t", t=T)
        sg = [sb(f"sg{i}", [P, NT]) for i in range(2)]
        gt = [sb(f"gt{i}", [P, NT]) for i in range(2)]
        act = [x[:].rearrange("p u k t -> p (u k) t") for x in (gru_x, gru_y)]
        s_logit = sem("s_logit"); s_max = sem("s_max"); s_exp = sem("s_exp"); s_comb = sem("s_comb")
        s_cbp = sem("s_cbp"); s_cb = sem("s_cb")
        s_gu = sem("s_gu"); s_sig = sem("s_sig"); s_act = sem("s_act"); s_down = sem("s_down"); s_add = sem("s_add")

        qt = act[0].rearrange("p k t -> p (k t)").rearrange("p (m t) -> p m t", t=T)
        kt = act[1].rearrange("p k t -> p (k t)").rearrange("p (m t) -> p m t", t=T)
        vt = wdn2[0:AT].rearrange("p i k n -> p (i k n)").rearrange("p (t n) -> p t n", t=NAT)
        ot = xp[:, 0:4, :]
        gex = sb("gex", [AT, NAT, HEADS])
        sc = [sb(f"sc{i}", [AT, HEADS, AT]) for i in range(2)]
        pt = [sb(f"pt{i}", [AT, HEADS, AT]) for i in range(2)]
        rmax = sb("rmax", [AT, HEADS]); rsum = sb("rsum", [AT, HEADS]); rden = sb("rden", [AT, HEADS])
        s_qk = sem("s_qk"); s_qkc = sem("s_qkc"); s_vg = sem("s_vg"); s_vgc = sem("s_vgc"); s_ge = sem("s_ge")
        s_sc = sem("s_sc"); s_sm = sem("s_sm"); s_scf = sem("s_scf"); s_ex = sem("s_ex"); s_pn = sem("s_pn")
        s_ptp = sem("s_ptp"); s_pt = sem("s_pt"); s_o = sem("s_o"); s_oc = sem("s_oc")
        s_wo = sem("s_wo"); s_ha = sem("s_ha")

        q1 = sb("q1", [P, KH, I], F32R)
        q2 = sb("q2", [P, KI, H], F32R)
        w1 = wup[1][:, 0, :].rearrange("p (k n) -> p k n", k=KH)
        w2 = wup[1][:, 1, :].rearrange("p (k n) -> p k n", k=KI)
        qtmp = wup[0]
        asum = sb("asum", [P, 2]); ws = sb("ws", [P, 2]); wsi = sb("wsi", [P, 2])
        xh = sb("xh", [P, KH, NT], F32R); xl = sb("xl", [P, KH, NT], F32R)
        gy = xp[:, 0:4, :].rearrange("p k t -> p (k t)").rearrange("p (k t) -> p k t", t=NT)
        gsq = act[0]
        yh = [sb(f"yh{i}", [P, NT], F32R) for i in range(2)]
        yl = [sb(f"yl{i}", [P, NT], F32R) for i in range(2)]
        vh = sb("vh", [P, KI, 2], F32R); vl = sb("vl", [P, KI, 2], F32R)
        gb = sb("gb", [P, KH, 2])
        oc = wt[0:TT]
        s_abs = sem("s_abs"); s_absp = sem("s_absp"); s_q1 = sem("s_q1"); s_q2 = sem("s_q2")
        s_xs = sem("s_xs"); s_u = sem("s_u"); s_gel = sem("s_gel"); s_gsq = sem("s_gsq"); s_ys = sem("s_ys")
        s_w2 = sem("s_w2"); s_st2 = sem("s_st2"); s_ve2 = sem("s_ve2"); s_pow2 = sem("s_pow2"); s_rm2 = sem("s_rm2")
        s_bc2 = sem("s_bc2"); s_fin = sem("s_fin"); s_gbp = sem("s_gbp"); s_tr = sem("s_tr"); s_trc = sem("s_trc"); s_out = sem("s_out")

        block = ctx.enter_context(nc.Block())

        @block.sync
        def _(sp):
            sp.dma_start(wt[:], w_tok.rearrange("(k p) n -> p k n", p=P)).then_inc(s_load["wt"], 16)
            sp.dma_start(xp[:], patches.rearrange("(k p) n -> p k n", p=P)).then_inc(s_load["xp"], 16)
            sp.dma_start(vec[:], vecs).then_inc(s_load["vec"], 16)
            for l in range(L):
                sp.dma_start(wg[:, l], w_gru[l].rearrange("d g (k p) n -> p d g k n", p=P)).then_inc(s_load[f"wg{l}"], 16)
            sp.dma_start(wf[:], w_fus.rearrange("(k p) n -> p k n", p=P)).then_inc(s_load["wf"], 16)
            sp.dma_start(wr[:], w_gate.rearrange("(k p) n -> p k n", p=P)).then_inc(s_load["wr"], 16)
            for i in range(2):
                sp.dma_start(wup[i][:], w_up[i].rearrange("(k p) n -> p k n", p=P)).then_inc(s_up[i], 16)
                sp.dma_start(wdn[i], w_down[i].rearrange("(k p) n -> p k n", p=P)).then_inc(s_dn[i], 16)
            sp.dma_start(wqkv[:], w_qkv.rearrange("(k p) n -> p k n", p=P)).then_inc(s_load["wqkv"], 16)
            sp.dma_start(wga[:], w_gates.rearrange("(k p) n -> p k n", p=P)).then_inc(s_load["wga"], 16)
            sp.dma_start(wo[:], w_o.rearrange("(k p) n -> p k n", p=P)).then_inc(s_load["wo"], 16)
            with sp.Fori(1, E // 2) as pair:
                for i in range(2):
                    sp.wait_ge(s_down, pair * 4 + (2 * i - 2))
                    sp.dma_start(wup[i][:], w_up[pair * 2 + i].rearrange("(k p) n -> p k n", p=P)).then_inc(s_up[i], 16)
                    sp.dma_start(wdn[i], w_down[pair * 2 + i].rearrange("(k p) n -> p k n", p=P)).then_inc(s_dn[i], 16)
            sp.wait_ge(s_down, 2 * E)
            sp.dma_start(w1, w_1.rearrange("(k p) n -> p k n", p=P)).then_inc(s_load["w1"], 16)
            sp.dma_start(w2, w_2.rearrange("(k p) n -> p k n", p=P)).then_inc(s_load["w2"], 16)
            for j in range(6):
                sp.wait_ge(s_trc, j + 1)
                sp.dma_start(out[j * TT:(j + 1) * TT, :], oc[:, j, :]).then_inc(s_out, 16)
            sp.wait_ge(s_out, 16 * 6)

        @block.gpsimd
        def _(pool):
            pool.memset(ident[:], 0.0).then_inc(s_const, 1)
            pool.memset(cmask[:], MASKED).then_inc(s_const, 1)
            pool.memset(half_neg[:], -0.5).then_inc(s_const, 1)
            pool.iota(ranks[:], pattern=[[-1, E]], base=E, channel_multiplier=0,
                      allow_small_or_imprecise_dtypes=True).then_inc(s_const, 1)
            pool.wait_ge(s_const, 4)
            pool.affine_select(out=ident[:], in_=ident[:], compare_op=ALU.not_equal, fill=1.0, base=0,
                               pattern=[[-1, P]], channel_multiplier=1).then_inc(s_const, 1)
            pool.affine_select(out=cmask[:], in_=cmask[:], compare_op=ALU.is_gt, fill=0.0, base=0,
                               pattern=[[1, AT]], channel_multiplier=-1).then_inc(s_const, 1)
            pool.wait_ge(s_const, 6)
            pool.affine_select(out=cmask[:, 0:S], in_=cmask[:, 0:S], compare_op=ALU.is_gt, fill=MASKED, base=S,
                               pattern=[[0, S]], channel_multiplier=-1).then_inc(s_const, 1)

            def power(i):
                pool.wait_ge(s_ve, i + 1)
                if i >= 2:
                    pool.wait_ge(s_bc, i - 1)
                pool.tensor_tensor(rm[i % 2][:, 0:3], ve[:], half_neg[0:TT, :], ALU.pow).then_inc(s_pow, 1)

            for i in range(LN_GRU):
                power(i)
            for s in range(STEPS + 1):
                if s >= 1:
                    power(LN_GRU + s - 1)
                if s < STEPS:
                    d, y = s % 2, aa[s % 2]
                    first = 0 if d == 0 else S - 1
                    pool.wait_ge(s_clip, s + 1)
                    pool.memset(both(y)[:, first::S], 0.0).then_inc(s_edge, 1)
            for i in range(LN_MOE, LN_ALL):
                power(i)
            for n in range(2):
                pool.wait_ge(s_ve2, n + 1)
                pool.tensor_tensor(rm[n][:, 0:3], ve[:], half_neg[0:TT, :], ALU.pow).then_inc(s_pow2, 1)

        @block.tensor
        def _(pe):
            def ln_sums(i):
                y = ln_source(i)
                pe.wait_ge(s_sq, i + 1)
                if i >= 1:
                    pe.wait_ge(s_rm, i)
                for c, src in enumerate((y, sq[i % 2])):
                    for j in range(JT):
                        for k in range(KH):
                            last = pe.matmul(bank[0:TT, 4, c * JT + j:c * JT + j + 1],
                                             src[:, k, j * TT:(j + 1) * TT], mean_h[:],
                                             start=(k == 0), stop=(k == KH - 1))
                last.then_inc(s_st, 1)

            def ln_spread(i):
                pe.wait_ge(s_rm, i + 1)
                if i >= 1:
                    pe.wait_ge(s_norm, i)
                for c in range(2):
                    for j in range(JT):
                        last = pe.matmul(bank[:, 5 + c, j * TT:(j + 1) * TT],
                                         rm[i % 2][:, c * JT + j:c * JT + j + 1].broadcast_to([TT, P]),
                                         ident[0:TT, 0:TT], start=True, stop=True)
                last.then_inc(s_bc, 1)

            pe.wait_ge(s_load["wt"], 16)
            pe.wait_ge(s_load["xp"], 16)
            for n in range(2):
                for m in range(KH):
                    for k in range(KF):
                        last = pe.matmul(bank[:, 2 * n + m, 0:NT], wt[:, k, m * P:(m + 1) * P],
                                         xp[:, k, half(n)], start=(k == 0), stop=(k == KF - 1))
                    last.then_inc(s_tok, 1)
            pe.wait_ge(s_const, 7)
            pe.wait_ge(s_vconst, 4)
            for i in range(LN_GRU):
                ln_sums(i)
                ln_spread(i)

            for s in range(STEPS + 2):
                if s < STEPS:
                    l, u, d, n = unit(s)
                    if l == 0:
                        pe.wait_ge(s_norm, n + 1)
                    else:
                        pe.wait_ge(s_aff, s - UNITS + 1)
                    if u == 0:
                        pe.wait_ge(s_load[f"wg{l}"], 16)
                    for g, (done, free) in enumerate(((s_zmm, s_gz), (s_hmm, s_gt))):
                        if s >= 1:
                            pe.wait_ge(free, s)
                        for m in range(KH):
                            for k in range(KH):
                                src = xn[:, k, half(n)] if l == 0 else xx[u][:, k, :]
                                last = pe.matmul(bank[:, 2 * g + m, 0:NT], wg[:, l, d, g, k, m * P:(m + 1) * P], src,
                                                 start=(k == 0), stop=(k == KH - 1))
                        last.then_inc(done, 1)
                if 1 <= s <= STEPS:
                    ln_sums(LN_GRU + s - 1)
                if s >= 2:
                    ln_spread(LN_GRU + s - 2)

            pe.wait_ge(s_load["wf"], 16)
            pe.wait_ge(s_gz, STEPS)
            pe.wait_ge(s_gt, STEPS)
            for n in range(2):
                pe.wait_ge(s_aff, STEPS - UNITS + 2 * n + 2)
                for m in range(KH):
                    for k in range(4):
                        last = pe.matmul(bank[:, 2 * n + m, 0:NT], wf[:, k, m * P:(m + 1) * P],
                                         xx[2 * n + k // 2][:, k % 2, :], start=(k == 0), stop=(k == 3))
                last.then_inc(s_fus, 1)

            for n in range(2):
                ln_sums(LN_MOE + n)
                ln_spread(LN_MOE + n)
            pe.wait_ge(s_load["wr"], 16)
            pe.wait_ge(s_norm, LN_MOE + 2)
            for j in range(6):
                for k in range(KH):
                    last = pe.matmul(bank[0:TT, 7, j * E:(j + 1) * E], xn[:, k, j * TT:(j + 1) * TT], wr[:, k, :],
                                     start=(k == 0), stop=(k == KH - 1))
            last.then_inc(s_logit, 1)
            pe.wait_ge(s_comb, 1)
            for e in range(E):
                for n in range(2):
                    q = 2 * e + n
                    if q >= 2:
                        pe.wait_ge(s_cb, q - 1)
                    for j in range(JT):
                        last = pe.matmul(bank[:, 5 + n, j * TT:(j + 1) * TT],
                                         comb[:, n * JT + j, e:e + 1].broadcast_to([TT, P]),
                                         ident[0:TT, 0:TT], start=True, stop=True)
                    last.then_inc(s_cbp, 1)

            def up(pair, q):
                i, n = q // 2, q % 2
                if n == 0:
                    pe.wait_ge(s_up[i], pair * 16 + 16)
                if q == 0:
                    pe.wait_ge(s_act, pair * 32)if not isinstance(pair, int) or pair else None
                for m in range(KI):
                    if q * KI + m >= 2 or not isinstance(pair, int):
                        pe.wait_ge(s_act, pair * 32 + q * KI + m - 1)
                    for g in range(2):
                        for k in range(KH):
                            last = pe.matmul(bank[:, 2 * g + m % 2, 0:NT],
                                             wup[i][:, k, g * I + m * P:g * I + (m + 1) * P],
                                             xn[:, k, half(n)], start=(k == 0), stop=(k == KH - 1))
                    last.then_inc(s_gu, 1)

            def down(pair, q):
                i, n = q // 2, q % 2
                if n == 0:
                    pe.wait_ge(s_dn[i], pair * 16 + 16)
                pe.wait_ge(s_act, pair * 32 + (q + 1) * KI)
                if q >= 1 or not isinstance(pair, int):
                    pe.wait_ge(s_add, pair * 4 + q)
                for m in range(KH):
                    for k in range(KI):
                        last = pe.matmul(bank[:, 4 + 3 * m, 0:NT], wdn[i][:, k, m * P:(m + 1) * P],
                                         act[n][:, k, :], start=(k == 0), stop=(k == KI - 1))
                last.then_inc(s_down, 1)

            pe.wait_ge(s_max, 1)
            up(0, 0)
            for q in range(1, 4):
                up(0, q)
                down(0, q - 1)
            down(0, 3)
            with pe.Fori(1, E // 2) as pair:
                up(pair, 0)
                for q in range(1, 4):
                    up(pair, q)
                    down(pair, q - 1)
                down(pair, 3)

            pe.wait_ge(s_add, 2 * E)
            for n in range(2):
                ln_sums(LN_ATT + n)
                ln_spread(LN_ATT + n)
            pe.wait_ge(s_load["wqkv"], 16)
            pe.wait_ge(s_load["wga"], 16)
            pe.wait_ge(s_act, 4 * E * KI // 2)
            pe.wait_ge(s_aff, affine_count(LN_ATT + 1))
            for q in range(16):
                if q >= 4:
                    pe.wait_ge(s_qkc, q - 3)
                c, m, n = q // 8, q % 8 // 2, q % 2
                for k in range(KH):
                    last = pe.matmul(bank[:, q % 4, 0:NT], wqkv[:, k, c * 512 + m * P:c * 512 + (m + 1) * P],
                                     xn[:, k, half(n)], start=(k == 0), stop=(k == KH - 1))
                last.then_inc(s_qk, 1)
            pe.wait_ge(s_qkc, 16)
            for t in range(NAT):
                if t >= 2:
                    pe.wait_ge(s_vgc, t - 1)
                for k in range(KH):
                    pe.matmul(bank[0:AT, 2 * (t % 2), :], xn[:, k, t * AT:(t + 1) * AT], wqkv[:, k, 1024:1536],
                              start=(k == 0), stop=(k == KH - 1))
                for k in range(KH):
                    last = pe.matmul(bank[0:AT, 2 * (t % 2) + 1, 0:HEADS], xn[:, k, t * AT:(t + 1) * AT], wga[:, k, :],
                                     start=(k == 0), stop=(k == KH - 1))
                last.then_inc(s_vg, 1)
            pe.wait_ge(s_vgc, NAT)
            pe.wait_ge(s_ge, NAT)

            def scores(t):
                if t >= 1:
                    pe.wait_ge(s_sm, t)
                for e in range(HEADS):
                    r = slice(64 * (e % 2), 64 * (e % 2) + 64)
                    last = pe.matmul(bank[0:AT, e % 2, (e // 2) * AT:(e // 2 + 1) * AT],
                                     qt[r, e // 2, t * AT:(t + 1) * AT], kt[r, e // 2, t * AT:(t + 1) * AT],
                                     start=True, stop=True)
                last.then_inc(s_sc, 1)

            def values(t):
                pe.wait_ge(s_pn, t + 1)
                if t >= 1:
                    pe.wait_ge(s_pt, t)
                for e in range(HEADS):
                    last = pe.transpose(bank[0:AT, 2 + e // 4, (e % 4) * AT:(e % 4 + 1) * AT],
                                        sc[t % 2][:, e, :], ident[0:AT, 0:AT])
                last.then_inc(s_ptp, 1)
                pe.wait_ge(s_pt, t + 1)
                if t >= 1:
                    pe.wait_ge(s_oc, t)
                for e in range(HEADS):
                    r = slice(64 * (e % 2), 64 * (e % 2) + 64)
                    last = pe.matmul(bank[r, 4, (e // 2) * AT:(e // 2 + 1) * AT], vt[:, t, e * DH:(e + 1) * DH],
                                     pt[t % 2][:, (e % 2) * 4 + e // 2, :], start=True, stop=True)
                last.then_inc(s_o, 1)

            scores(0)
            for t in range(1, NAT):
                scores(t)
                values(t - 1)
            values(NAT - 1)
            pe.wait_ge(s_load["wo"], 16)
            pe.wait_ge(s_oc, NAT)
            for n in range(2):
                for m in range(KH):
                    for k in range(4):
                        last = pe.matmul(bank[:, 2 * n + m, 0:NT], wo[:, k, m * P:(m + 1) * P],
                                         ot[:, k, half(n)], start=(k == 0), stop=(k == 3))
                last.then_inc(s_wo, 1)

            pe.wait_ge(s_abs, 2)
            pe.matmul(bank[:, 7, 0:2], ones[:], asum[:], start=True, stop=True).then_inc(s_absp, 1)
            for n in range(2):
                ln_sums(LN_MLP + n)
                ln_spread(LN_MLP + n)
            pe.wait_ge(s_q2, 1)
            pe.wait_ge(s_q1, 1)
            for m in range(KH):
                for k in range(KI):
                    for part in (vh, vl):
                        last = pe.matmul(bank[:, 7, 2 * m:2 * m + 2], q2[:, k, m * P:(m + 1) * P], part[:, k, :],
                                         start=(k == 0 and part is vh), stop=(k == KI - 1 and part is vl))
            last.then_inc(s_gbp, 1)
            for n in range(2):
                def hidden(m):
                    pe.wait_ge(s_xs, n + 1)
                    if n * KI + m >= 2:
                        pe.wait_ge(s_gel, n * KI + m - 1)
                    for k in range(KH):
                        for part in (xh, xl):
                            last = pe.matmul(bank[:, m % 2, 0:NT], q1[:, k, m * P:(m + 1) * P], part[:, k, :],
                                             start=(k == 0 and part is xh), stop=(k == KH - 1 and part is xl))
                    last.then_inc(s_u, 1)

                def outward(k):
                    pe.wait_ge(s_ys, n * KI + k + 1)
                    if n >= 1 and k == 0:
                        pe.wait_ge(s_fin, n)
                    for m in range(KH):
                        for part in (yh[k % 2], yl[k % 2]):
                            last = pe.matmul(bank[:, 2 + m, 0:NT], q2[:, k, m * P:(m + 1) * P], part[:],
                                             start=(k == 0 and part is yh[k % 2]),
                                             stop=(k == KI - 1 and part is yl[k % 2]))
                    last.then_inc(s_w2, 1)
                hidden(0)
                for k in range(KI):
                    if k + 1 < KI:
                        hidden(k + 1)
                    outward(k)
                pe.wait_ge(s_gsq, (n + 1) * KI)
                for c, src in enumerate((gy, gsq)):
                    for j in range(JT):
                        for k in range(KI):
                            last = pe.matmul(bank[0:TT, 4, c * JT + j:c * JT + j + 1],
                                             src[:, k, j * TT:(j + 1) * TT], mean_i[:],
                                             start=(k == 0), stop=(k == KI - 1))
                last.then_inc(s_st2, 1)
                pe.wait_ge(s_rm2, n + 1)
                for c in range(2):
                    for j in range(JT):
                        last = pe.matmul(bank[:, 5 + c, j * TT:(j + 1) * TT],
                                         rm[n][:, c * JT + j:c * JT + j + 1].broadcast_to([TT, P]),
                                         ident[0:TT, 0:TT], start=True, stop=True)
                last.then_inc(s_bc2, 1)
            for n in range(2):
                pe.wait_ge(s_fin, n + 1)
                for j in range(JT):
                    t = n * JT + j
                    if t >= 2:
                        pe.wait_ge(s_trc, t - 1)
                    for m in range(KH):
                        last = pe.transpose(bank[0:TT, t % 2, m * P:(m + 1) * P],
                                            h[:, m, t * TT:(t + 1) * TT], ident[:])
                    last.then_inc(s_tr, 1)

        @block.scalar
        def _(sc_):
            def squares(i, ready):
                sc_.wait_ge(*ready)
                if i >= 2:
                    sc_.wait_ge(s_st, i - 1)
                sc_.activation(sq[i % 2][:], ln_source(i), ACT.Square).then_inc(s_sq, 1)

            def affine(i, gain, shift):
                sc_.wait_ge(s_norm, i + 1)
                for m in range(KH):
                    if LN_GRU <= i < LN_MOE:
                        src, dst = yy[(i - LN_GRU) % UNITS][:, m, :], xx[(i - LN_GRU) % UNITS][:, m, :]
                    else:
                        src = dst = xn[:, m, half(i % 2)]
                    last = sc_.activation(dst, src, ACT.Identity, scale=vec[:, gain + m:gain + m + 1],
                                          bias=vec[:, shift + m:shift + m + 1] if shift is not None else 0.0)
                last.then_inc(s_aff, 1)

            for i in range(2):
                squares(i, (s_h0, 2 * i + 2))
            sc_.wait_ge(s_load["vec"], 16)
            sc_.wait_ge(s_vconst, 5)
            for s in range(STEPS + 2):
                if s < STEPS:
                    l, u, d, n = unit(s)
                    if s >= 2:
                        sc_.wait_ge(s_y, s - 1)
                    sc_.wait_ge(s_zmm, s + 1)
                    c = (l * 2 + d) * 2
                    for m in range(KH):
                        sc_.activation(aa[s % 2][:, m, :], bank[:, m, 0:NT], ACT.Sigmoid, scale=-1.0,
                                       bias=nbz[:, c + m:c + m + 1])
                        last = sc_.activation(zz[s % 2][:, m, :], bank[:, m, 0:NT], ACT.Sigmoid,
                                              bias=vec[:, V_BZ + c + m:V_BZ + c + m + 1])
                    last.then_inc(s_gz, 1)
                    sc_.wait_ge(s_hmm, s + 1)
                    for m in range(KH):
                        last = sc_.activation(tt[s % 2][:, m, :], bank[:, 2 + m, 0:NT], ACT.Tanh,
                                              bias=vec[:, V_BH + c + m:V_BH + c + m + 1])
                    last.then_inc(s_gt, 1)
                if s >= 2:
                    affine(LN_GRU + s - 2, V_GAM, V_BET)
                if s < STEPS:
                    squares(LN_GRU + s, (s_y, s + 1))
            for n in range(2):
                squares(LN_MOE + n, (s_hf, n + 1))
            sc_.wait_ge(s_max, 2)
            sc_.activation(pr[:], pr[:], ACT.Exp).then_inc(s_exp, 1)
            for q in range(2 * E):
                sc_.wait_ge(s_cbp, q + 1)
                sc_.activation(cb[:, q // 2, half(q % 2)], bank[:, 5 + q % 2, 0:NT], ACT.Copy).then_inc(s_cb, 1)
            def gate(count, r, first):
                sc_.wait_ge(s_gu, count)
                if not first:
                    sc_.wait_ge(s_act, count - 2)
                sc_.activation(sg[r % 2][:], bank[:, r % 2, 0:NT], ACT.Sigmoid).then_inc(s_sig, 1)
            for r in range(32):
                gate(r + 1, r, r < 2)
            with sc_.Fori(1, E // 2) as pair:
                for r in range(32):
                    gate(pair * 32 + r + 1, r, False)
            for n in range(2):
                squares(LN_ATT + n, (s_add, 2 * E - 1 + n))
            for n in range(2):
                affine(LN_ATT + n, V_RMS, None)
            for q in range(16):
                c, m, n = q // 8, q % 8 // 2, q % 2
                sc_.wait_ge(s_qk, q + 1)
                sc_.activation((qt, kt)[c][:, m, half(n)], bank[:, q % 4, 0:NT], ACT.Copy,
                               scale=DH ** -0.5 if c == 0 else 1.0).then_inc(s_qkc, 1)
            for t in range(NAT):
                sc_.wait_ge(s_vg, t + 1)
                sc_.activation(gex[:, t, :], bank[0:AT, 2 * (t % 2) + 1, 0:HEADS], ACT.Exp, scale=-1.0).then_inc(s_ge, 1)
                sc_.activation(vt[:, t, :], bank[0:AT, 2 * (t % 2), :], ACT.Copy).then_inc(s_vgc, 1)
            for t in range(NAT + 1):
                if t < NAT:
                    sc_.wait_ge(s_scf, t + 1)
                    sc_.activation(sc[t % 2][:], sc[t % 2][:], ACT.Exp).then_inc(s_ex, 1)
                if t >= 1:
                    sc_.wait_ge(s_ptp, t)
                    if t >= 3:
                        sc_.wait_ge(s_o, t - 2)
                    sc_.activation(pt[(t - 1) % 2][:].rearrange("p (b e) t -> p b (e t)", b=2),
                                   bank[0:AT, 2:4, 0:4 * AT], ACT.Copy).then_inc(s_pt, 1)
            sc_.wait_ge(s_load["w1"], 16)
            sc_.wait_ge(s_load["w2"], 16)
            sc_.wait_ge(s_down, 2 * E)
            sc_.activation(qtmp[:, 0, :], w1.rearrange("p k n -> p (k n)"), ACT.Abs,
                           accum_out=asum[:, 0:1]).then_inc(s_abs, 1)
            sc_.activation(qtmp[:, 1, :], w2.rearrange("p k n -> p (k n)"), ACT.Abs,
                           accum_out=asum[:, 1:2]).then_inc(s_abs, 1)
            for n in range(2):
                squares(LN_MLP + n, (s_ha, n + 1))
            for n in range(2):
                affine(LN_MLP + n, V_L1G, V_L1B)
            for n in range(2):
                for m in range(KI):
                    q = n * KI + m
                    sc_.wait_ge(s_u, q + 1)
                    if n and m == 0:
                        sc_.wait_ge(s_st2, n)
                    sc_.activation(gy[:, m, :], bank[:, m % 2, 0:NT], ACT.Gelu, scale=wsi[:, 0:1],
                                   bias=vec[:, V_B1 + m:V_B1 + m + 1]).then_inc(s_gel, 1)
                    sc_.wait_ge(s_gel, q + 1)
                    sc_.activation(gsq[:, m, :], gy[:, m, :], ACT.Square).then_inc(s_gsq, 1)
            for t in range(6):
                sc_.wait_ge(s_tr, t + 1)
                sc_.activation(oc[:, t, :], bank[0:TT, t % 2, 0:H], ACT.Copy).then_inc(s_trc, 1)

        @block.vector
        def _(dve):
            dve.memset(ones[:], 1.0).then_inc(s_vconst, 1)
            dve.memset(mean_h[:], 1.0 / H).then_inc(s_vconst, 1)
            dve.memset(mean_i[:], 1.0 / I).then_inc(s_vconst, 1)
            dve.memset(stat[:], 0.0).then_inc(s_vconst, 1)
            dve.wait_ge(s_load["vec"], 16)
            dve.tensor_scalar(nbz[:], vec[:, V_BZ:V_BZ + 16], -1.0, None, ALU.mult).then_inc(s_vconst, 1)

            def variance(sums, a, b, done, eps_sem):
                dve.wait_ge(*sums)
                link(dve, dve.tensor_copy(stat[:], bank[0:TT, 4, 0:6]))
                link(dve, dve.tensor_tensor(msq[:], stat[:, 0:3], stat[:, 0:3], ALU.mult))
                link(dve, dve.tensor_tensor(var[:], stat[:, 3:6], msq[:], ALU.subtract))
                if a == 1.0:
                    dve.tensor_scalar(ve[:], var[:], 0.0, b, ALU.max, ALU.add).then_inc(eps_sem, 1)
                else:
                    link(dve, dve.tensor_scalar(var[:], var[:], 0.0, a, ALU.max, ALU.mult))
                    dve.tensor_scalar(ve[:], var[:], b, None, ALU.add).then_inc(eps_sem, 1)

            def ln_var(i):
                e2 = {LN_ATT: RMS_EPS, LN_MLP: EPS}.get(i - i % 2)
                if e2 is None:
                    variance((s_st, i + 1), 1.0, EPS, None, s_ve)
                else:
                    variance((s_st, i + 1), 1.0 + e2, e2 * EPS, None, s_ve)

            def ln_root(i):
                dve.wait_ge(s_pow, i + 1)
                dve.tensor_tensor(rm[i % 2][:, 3:6], stat[:, 0:3], rm[i % 2][:, 0:3], ALU.mult).then_inc(s_rm, 1)

            def ln_norm(i):
                dve.wait_ge(s_bc, i + 1)
                src, dst = ln_source(i), ln_target(i)
                link(dve, dve.tensor_tensor(dst, src, bank[:, 5:6, 0:NT].broadcast_to([P, KH, NT]), ALU.mult))
                dve.tensor_tensor(dst, dst, bank[:, 6:7, 0:NT].broadcast_to([P, KH, NT]),
                                  ALU.subtract).then_inc(s_norm, 1)

            for n in range(2):
                for m in range(KH):
                    dve.wait_ge(s_tok, 2 * n + m + 1)
                    dve.tensor_copy(h[:, m, half(n)], bank[:, 2 * n + m, 0:NT]).then_inc(s_h0, 1)
            for i in range(LN_GRU):
                ln_var(i)
                ln_root(i)
                ln_norm(i)

            for s in range(STEPS + 2):
                if 1 <= s <= STEPS:
                    ln_var(LN_GRU + s - 1)
                if s >= 2:
                    ln_norm(LN_GRU + s - 2)
                if 1 <= s <= STEPS:
                    ln_root(LN_GRU + s - 1)
                if s < STEPS:
                    l, u, d, n = unit(s)
                    z, a, t, y = zz[s % 2], aa[s % 2], tt[s % 2], yy[u]
                    dve.wait_ge(s_gz, s + 1)
                    dve.tensor_scalar(a[:], a[:], 1e-8, 1.0, ALU.max, ALU.min).then_inc(s_clip, 1)
                    dve.wait_ge(s_gt, s + 1)
                    link(dve, dve.tensor_tensor(z[:], z[:], t[:], ALU.mult))
                    dve.wait_ge(s_edge, s + 1)
                    if s >= 4:
                        dve.wait_ge(s_aff, s - 3)
                    to = y if l == 0 else t
                    rev = slice(None) if d == 0 else slice(None, None, -1)
                    scan = dve.tensor_tensor_scan(both(to)[:, rev], both(a)[:, rev], both(z)[:, rev], 0.0,
                                                  ALU.mult, ALU.add)
                    if l == 0:
                        scan.then_inc(s_y, 1)
                    else:
                        link(dve, scan)
                        dve.tensor_tensor(y, t[:], xx[u], ALU.add).then_inc(s_y, 1)

            for n in range(2):
                dve.wait_ge(s_fus, n + 1)
                for m in range(KH):
                    last = dve.scalar_tensor_tensor(out=h[:, m, half(n)], in0=bank[:, 2 * n + m, 0:NT],
                                                    scalar=vec[:, V_FB + m:V_FB + m + 1], in1=h[:, m, half(n)],
                                                    op0=ALU.add, op1=ALU.add)
                last.then_inc(s_hf, 1)
            for n in range(2):
                ln_var(LN_MOE + n)
                ln_root(LN_MOE + n)
                ln_norm(LN_MOE + n)

            def over(x):
                return x.broadcast_to([TT, 6, E])
            lg = bank[0:TT, 7, 0:6 * E].rearrange("p (j e) -> p j e", e=E)
            dve.wait_ge(s_logit, 1)
            link(dve, dve.tensor_reduce(mx1[:], lg, AX_X, ALU.max))
            dve.tensor_tensor(pr[:], lg, over(mx1[:]), ALU.subtract).then_inc(s_max, 2)
            dve.wait_ge(s_exp, 1)
            link(dve, dve.tensor_reduce(mx1[:], pr[:], AX_X, ALU.add))
            link(dve, dve.reciprocal(mx1[:], mx1[:]))
            link(dve, dve.tensor_tensor(pr[:], pr[:], over(mx1[:]), ALU.mult))
            dve.wait_ge(s_const, 7)
            rk = ranks[0:TT, :].rearrange("p (o e) -> p o e", o=1).broadcast_to([TT, 6, E])
            for c in range(2):
                link(dve, dve.tensor_reduce(top[:, c, :], pr[:], AX_X, ALU.max))
                tc = top[:, c, :].rearrange("p (j o) -> p j o", o=1)
                link(dve, dve.tensor_tensor(eq[:], pr[:], over(tc), ALU.is_equal))
                link(dve, dve.tensor_tensor(keys[:], eq[:], rk, ALU.mult))
                link(dve, dve.tensor_reduce(mx1[:], keys[:], AX_X, ALU.max))
                link(dve, dve.tensor_tensor(sel[:, c], keys[:], over(mx1[:]), ALU.is_equal))
                link(dve, dve.scalar_tensor_tensor(out=pr[:], in0=sel[:, c], scalar=-2.0, in1=pr[:],
                                                   op0=ALU.mult, op1=ALU.add))
            link(dve, dve.tensor_tensor(den[:], top[:, 0, :], top[:, 1, :], ALU.add))
            link(dve, dve.reciprocal(den[:], den[:]))
            for c in range(2):
                link(dve, dve.tensor_tensor(top[:, c, :], top[:, c, :], den[:], ALU.mult))
                link(dve, dve.tensor_tensor(sel[:, c], sel[:, c],
                                            over(top[:, c, :].rearrange("p (j o) -> p j o", o=1)), ALU.mult))
            dve.tensor_tensor(comb[:], sel[:, 0], sel[:, 1], ALU.add).then_inc(s_comb, 1)
            dve.wait_ge(s_cb, 2 * E)

            before_loop = chain[0]
            per_pair = [0]

            def activate(pair, r):
                q, m = r // KI, r % KI
                dve.wait_ge(s_sig, pair * 32 + r + 1)
                dve.tensor_tensor(gt[r % 2][:], bank[:, r % 2, 0:NT], sg[r % 2][:], ALU.mult).then_inc(s_v, 1)
                per_pair[0] += 1
                dve.wait_ge(s_v, pair * per_all + before_loop + per_pair[0])
                if q >= 2 and m == 0:
                    dve.wait_ge(s_down, pair * 4 + q - 1)
                dve.tensor_tensor(act[q % 2][:, m, :], bank[:, 2 + r % 2, 0:NT], gt[r % 2][:], ALU.mult).then_inc(s_act, 1)

            def gather(pair, q):
                i, n = q // 2, q % 2
                dve.wait_ge(s_down, pair * 4 + q + 1)
                cbe = cb[:, pair * 2 + i, half(n)]
                dve.tensor_tensor(zz[0][:, 0, :], bank[:, 4, 0:NT], cbe, ALU.mult).then_inc(s_v, 1)
                dve.tensor_tensor(zz[0][:, 1, :], bank[:, 7, 0:NT], cbe, ALU.mult).then_inc(s_v, 1)
                per_pair[0] += 2
                dve.wait_ge(s_v, pair * per_all + before_loop + per_pair[0])
                dve.tensor_tensor(h[:, :, half(n)], h[:, :, half(n)], zz[0][:], ALU.add).then_inc(s_add, 1)

            def experts(pair):
                per_pair[0] = 0
                for q in range(4):
                    for m in range(KI):
                        activate(pair, q * KI + m)
                    if q >= 1:
                        gather(pair, q - 1)
                gather(pair, 3)
                assert per_pair[0] == per_all

            per_all = 4 * (KI + 2)
            experts(0)
            with dve.Fori(1, E // 2) as pair:
                experts(pair)
            chain[0] = before_loop + (E // 2) * per_all

            for n in range(2):
                ln_var(LN_ATT + n)
                ln_root(LN_ATT + n)
                ln_norm(LN_ATT + n)

            def softmax_in(t):
                dve.wait_ge(s_sc, t + 1)
                if t >= 2:
                    dve.wait_ge(s_ptp, t - 1)
                x = sc[t % 2]
                for b in range(2):
                    last = dve.tensor_tensor(x[:, 4 * b:4 * b + 4, :],
                                             bank[0:AT, b, 0:4 * AT].rearrange("p (e t) -> p e t", e=4),
                                             cmask[:].rearrange("p (o t) -> p o t", o=1).broadcast_to([AT, 4, AT]),
                                             ALU.add)
                    last.then_inc(s_v, 1)
                    chain[0] += 1
                dve.wait_ge(s_v, chain[0])
                dve.tensor_reduce(rmax[:], x[:], AX_X, ALU.max).then_inc(s_sm, 1)
                dve.wait_ge(s_sm, t + 1)
                dve.tensor_tensor(x[:], x[:], rmax[:].rearrange("p (e o) -> p e o", o=1).broadcast_to([AT, HEADS, AT]),
                                  ALU.subtract).then_inc(s_scf, 1)

            def softmax_out(t):
                x = sc[t % 2]
                dve.wait_ge(s_ex, t + 1)
                link(dve, dve.tensor_reduce(rsum[:], x[:], AX_X, ALU.add))
                link(dve, dve.scalar_tensor_tensor(out=rden[:], in0=gex[:, t, :], scalar=1.0, in1=rsum[:],
                                                   op0=ALU.add, op1=ALU.mult))
                link(dve, dve.reciprocal(rden[:], rden[:]))
                dve.tensor_tensor(x[:], x[:], rden[:].rearrange("p (e o) -> p e o", o=1).broadcast_to([AT, HEADS, AT]),
                                  ALU.mult).then_inc(s_pn, 1)

            def keep_out(t):
                dve.wait_ge(s_o, t + 1)
                dve.tensor_copy(ot[:, :, t * AT:(t + 1) * AT],
                                bank[:, 4, 0:4 * AT].rearrange("p (e t) -> p e t", e=4)).then_inc(s_oc, 1)

            softmax_in(0)
            for t in range(NAT):
                if t + 1 < NAT:
                    softmax_in(t + 1)
                softmax_out(t)
                if t >= 1:
                    keep_out(t - 1)
            keep_out(NAT - 1)
            for n in range(2):
                dve.wait_ge(s_wo, n + 1)
                dve.tensor_tensor(h[:, :, half(n)], bank[:, 2 * n:2 * n + 2, 0:NT], h[:, :, half(n)],
                                  ALU.add).then_inc(s_ha, 1)

            dve.wait_ge(s_absp, 1)
            link(dve, dve.tensor_scalar(wsi[:], bank[:, 7, 0:2], 1.0 / (H * I), 1e-5, ALU.mult, ALU.max))
            link(dve, dve.reciprocal(ws[:], wsi[:]))
            link(dve, dve.reciprocal(wsi[:], ws[:]))
            for c, (w, q, done) in enumerate(((w1, q1, s_q1), (w2, q2, s_q2))):
                flat = w.rearrange("p k n -> p (k n)")
                dve.wait_ge(s_absp, 1)
                dve.tensor_scalar(qtmp[:, 0, :], flat, ws[:, c:c + 1], -0.5, ALU.mult, ALU.is_lt).then_inc(s_v, 1)
                dve.tensor_scalar(qtmp[:, 1, :], flat, ws[:, c:c + 1], 0.5, ALU.mult, ALU.is_gt).then_inc(s_v, 1)
                chain[0] += 2
                dve.wait_ge(s_v, chain[0])
                ins = dve.tensor_tensor(q[:].rearrange("p k n -> p (k n)"), qtmp[:, 1, :], qtmp[:, 0, :], ALU.subtract)
                link(dve, ins)
                if c == 0:
                    dve.tensor_copy(msq[:], var[:]).then_inc(done, 1)
            gbv = vec[:, V_GB2:V_GB2 + 16].rearrange("p (k c) -> p k c", c=2)
            link(dve, dve.tensor_copy(vh[:], gbv))
            dve.tensor_tensor(vl[:], gbv, vh[:].bitcast(F32), ALU.subtract).then_inc(s_q2, 1)

            for n in range(2):
                ln_var(LN_MLP + n)
                ln_root(LN_MLP + n)
                ln_norm(LN_MLP + n)
            dve.wait_ge(s_gbp, 1)
            link(dve, dve.tensor_scalar(gb[:], bank[:, 7, 0:4].rearrange("p (m c) -> p m c", c=2), wsi[:, 1:2],
                                        None, ALU.mult))
            for m in range(KH):
                link(dve, dve.tensor_tensor(gb[:, m, 1:2], gb[:, m, 1:2], vec[:, V_B2 + m:V_B2 + m + 1], ALU.add))
            for n in range(2):
                dve.wait_ge(s_aff, affine_count(LN_MLP + n))
                if n:
                    dve.wait_ge(s_u, n * KI)
                link(dve, dve.tensor_copy(xh[:], xn[:, :, half(n)]))
                dve.tensor_tensor(xl[:], xn[:, :, half(n)], xh[:].bitcast(F32), ALU.subtract).then_inc(s_xs, 1)
                for k in range(KI):
                    q = n * KI + k
                    dve.wait_ge(s_gel, q + 1)
                    if q >= 2:
                        dve.wait_ge(s_w2, q - 1)
                    g2 = vec[:, V_GB2 + 2 * k:V_GB2 + 2 * k + 1]
                    link(dve, dve.tensor_scalar(yh[k % 2][:], gy[:, k, :], g2, None, ALU.mult))
                    dve.scalar_tensor_tensor(out=yl[k % 2][:], in0=gy[:, k, :], scalar=g2, in1=yh[k % 2][:].bitcast(F32),
                                             op0=ALU.mult, op1=ALU.subtract).then_inc(s_ys, 1)
                variance((s_st2, n + 1), 1.0, EPS, None, s_ve2)
                dve.wait_ge(s_pow2, n + 1)
                dve.tensor_tensor(rm[n][:, 3:6], stat[:, 0:3], rm[n][:, 0:3], ALU.mult).then_inc(s_rm2, 1)
                dve.wait_ge(s_w2, (n + 1) * KI)
                dve.wait_ge(s_bc2, n + 1)
                tmp, tmp2 = zz[0], zz[1]
                link(dve, dve.tensor_copy(tmp2[:, 0, :], bank[:, 5, 0:NT]))
                link(dve, dve.scalar_tensor_tensor(out=tmp[:], in0=bank[:, 2:4, 0:NT], scalar=wsi[:, 1:2],
                                                   in1=tmp2[:, 0:1, :].broadcast_to([P, KH, NT]), op0=ALU.mult, op1=ALU.mult))
                for m in range(KH):
                    link(dve, dve.tensor_scalar(tmp2[:, m, :], bank[:, 6, 0:NT], gb[:, m, 0:1], gb[:, m, 1:2],
                                                ALU.mult, ALU.subtract))
                link(dve, dve.tensor_tensor(tmp[:], tmp[:], tmp2[:], ALU.subtract))
                dve.tensor_tensor(h[:, :, half(n)], h[:, :, half(n)], tmp[:], ALU.add).then_inc(s_fin, 1)


def kernel(**inputs):
    import numpy as np
    import concourse.bacc as bacc
    from concourse.bass_utils import run_bass_kernel_spmd

    a = {k: np.asarray(v) for k, v in inputs.items()}
    c = np.ascontiguousarray
    px = a["x"].reshape(B, 3, 6, 16, 6, 16).transpose(0, 1, 3, 5, 2, 4).reshape(T, FLAT)

    def cols(v):
        return v.reshape(-1, P).T

    gru = np.stack([np.stack([a[f"L0_attn_{d}_W{g}"] for g in "zh"], 1) for d in ("fwd", "bwd")], 1)
    bias = [np.stack([a["L0_attn_fwd_b" + g], a["L0_attn_bwd_b" + g]], 1) for g in "zh"]
    gb2 = np.stack([cols(a["L1_ffn_ln2_g"]), cols(a["L1_ffn_ln2_b"])], 2).reshape(P, 16)
    vecs = np.concatenate([cols(bias[0]), cols(bias[1]), cols(a["L0_attn_ln_gamma"]), cols(a["L0_attn_ln_beta"]),
                           cols(a["L0_attn_fusion_b"]), cols(a["L1_attn_rms_w"]), cols(a["L1_ffn_ln1_g"]),
                           cols(a["L1_ffn_ln1_b"]), cols(a["L1_ffn_b1"]), gb2, cols(a["L1_ffn_b2"])], 1)
    qkv = np.concatenate([a[f"L1_attn_w{n}"].transpose(1, 0, 2).reshape(H, HEADS * DH) for n in "qkv"], 1)
    arrays = {
        "patches": px.T, "w_tok": a["L0_tok_W"], "w_gru": gru.transpose(0, 1, 2, 4, 3),
        "w_fus": a["L0_attn_fusion_W"].T, "vecs": vecs, "w_gate": a["L0_ffn_gate_w"].T,
        "w_up": a["L0_ffn_gate_up_proj"].transpose(0, 2, 1), "w_down": a["L0_ffn_down_proj"].transpose(0, 2, 1),
        "w_qkv": qkv, "w_gates": a["L1_attn_w_gates"][:, [0, 2, 4, 6, 1, 3, 5, 7]], "w_o": a["L1_attn_wo"].reshape(HEADS * DH, H),
        "w_1": a["L1_ffn_w1"].T, "w_2": a["L1_ffn_w2"].T,
    }
    arrays = {k: c(v) for k, v in arrays.items()}
    nc = bacc.Bacc("TRN2", target_bir_lowering=False, num_devices=1)
    args = [nc.dram_tensor(k, v.shape, mybir.dt.from_np(v.dtype), kind="ExternalInput").ap() for k, v in arrays.items()]
    out = nc.dram_tensor("tower_out", (T, H), F32, kind="ExternalOutput").ap()
    tower(nc, *args, out)
    r = run_bass_kernel_spmd(nc, [arrays], core_ids=[0])
    return r.results[0]["tower_out"].reshape(B, S, H)
```

```python
from contextlib import ExitStack

import concourse.bass as bass
from concourse import mybir

F32 = mybir.dt.float32
F32R = mybir.dt.float32r
ALU = mybir.AluOpType
ACT = mybir.ActivationFunctionType
AX_X = mybir.AxisListType.X

P = 128
B, S = 16, 36
T = B * S
H = 256
KH = H // P
NT = T // 2
TT = 96
JT = NT // TT
FLAT = 768
KF = FLAT // P
L = 4
UNITS = 4
STEPS = L * UNITS
E = 8
I = 1024
KI = I // P
HEADS, DH = 8, 64
AT = 2 * S
NAT = T // AT
EPS = 1e-5
RMS_EPS = 1.1920928955078125e-07
MASKED = -1e30
C = 192
CT = C // TT
PASSES = T // C
NP = E // 2

V_BZ, V_BH, V_GAM, V_BET, V_FB, V_RMS = 0, 16, 32, 34, 36, 38
V_L1G, V_L1B, V_B1, V_GB2, V_B2, V_N = 40, 42, 44, 52, 68, 70

LN_IN = 0
LN_GRU = 2
LN_MOE = 18
LN_ATT = 20
LN_MLP = 22
LN_ALL = 24


def tower(nc, patches, w_tok, w_gru, w_fus, vecs, w_gate, w_up, w_down, w_qkv, w_gates, w_o, w_1, w_2, out):
    with ExitStack() as ctx:
        def sb(name, shape, dt=F32):
            return ctx.enter_context(nc.sbuf_tensor(name, shape, dt))

        def sem(name):
            return ctx.enter_context(nc.semaphore(name))

        bank = ctx.enter_context(nc.psum_tensor("bank", [P, 8, 512], F32))

        xp = sb("xp", [P, KF, T])
        wt = sb("wt", [P, KF, H])
        wg = sb("wg", [P, L, 2, 2, KH, H])
        wf = sb("wf", [P, 4, H])
        vec = sb("vec", [P, V_N])
        wr = sb("wr", [P, KH, E])
        wqkv = xp[:].rearrange("p k t -> p (k t)")[:, 0:KH * 3 * HEADS * DH].rearrange("p (k n) -> p k n", k=KH)
        wga = sb("wga", [P, KH, HEADS])
        wo = wt[:, 0:4, :]
        wup = [sb(f"wup{i}", [P, KH, 2 * I]) for i in range(2)]
        wdn2 = sb("wdn2", [P, 2, KI, H])
        wdn = [wdn2[:, i] for i in range(2)]
        ident = sb("ident", [P, P])
        ones = sb("ones", [P, P])
        mean_h = sb("mean_h", [P, 1])
        mean_i = sb("mean_i", [P, 1])
        half_neg = sb("half_neg", [P, JT])
        nbz = sb("nbz", [P, 16])
        cmask = sb("cmask", [AT, AT])
        ranks = sb("ranks", [P, E])
        h = sb("h", [P, KH, T])
        xn = sb("xn", [P, KH, T])
        zz = [sb(f"zz{i}", [P, KH, NT]) for i in range(2)]
        aa = [sb(f"aa{i}", [P, KH, NT]) for i in range(2)]
        tt = [sb(f"tt{i}", [P, KH, NT]) for i in range(2)]
        gru_y = sb("gru_y", [P, UNITS, KH, NT])
        gru_x = sb("gru_x", [P, UNITS, KH, NT])
        yy = [gru_y[:, i] for i in range(UNITS)]
        xx = [gru_x[:, i] for i in range(UNITS)]
        sq = [sb(f"sq{i}", [P, KH, NT]) for i in range(2)]
        stat = sb("stat", [TT, 6])
        msq = sb("msq", [TT, 3])
        var = sb("var", [TT, 3])
        ve = sb("ve", [TT, 3])
        rm = [sb(f"rm{i}", [TT, 6]) for i in range(2)]

        s_load = {n: sem("s_load_" + n) for n in
                  ("xp", "wt", "wg0", "wg1", "wg2", "wg3", "wf", "vec", "wr", "wqkv", "wga", "wo", "w1", "w2")}
        s_const = sem("s_const")
        s_vconst = sem("s_vconst")
        s_tok = sem("s_tok")
        s_h0 = sem("s_h0")
        s_sq = sem("s_sq")
        s_st = sem("s_st")
        s_ve = sem("s_ve")
        s_pow = sem("s_pow")
        s_rm = sem("s_rm")
        s_bc = sem("s_bc")
        s_norm = sem("s_norm")
        s_aff = sem("s_aff")
        s_zmm = sem("s_zmm"); s_hmm = sem("s_hmm")
        s_gz = sem("s_gz"); s_gt = sem("s_gt")
        s_clip = sem("s_clip"); s_edge = sem("s_edge")
        s_y = sem("s_y")
        s_fus = sem("s_fus"); s_hf = sem("s_hf")
        s_v = sem("s_v")

        chain = [0]

        def link(dve, ins):
            chain[0] += 1
            ins.then_inc(s_v, 1)
            dve.wait_ge(s_v, chain[0])

        def both(x):
            return x[:].rearrange("p k t -> p (k t)")

        def unit(s):
            return s // UNITS, s % UNITS, s % 2, (s % UNITS) // 2

        def half(n):
            return slice(n * NT, (n + 1) * NT)

        def ln_source(i):
            if LN_GRU <= i < LN_MOE:
                return yy[(i - LN_GRU) % UNITS]
            return h[:, :, half(i % 2)]

        def ln_target(i):
            if LN_GRU <= i < LN_MOE:
                return yy[(i - LN_GRU) % UNITS]
            return xn[:, :, half(i % 2)]

        def affine_count(i):
            return max(0, min(i + 1, LN_MOE) - LN_GRU) + max(0, i + 1 - LN_ATT)

        wgf = wg[:].rearrange("p l d g k n -> p (l d g k n)")
        rkb = wgf[:, 0:E * T].rearrange("p (e t) -> p e t", t=T)
        act = [x[:].rearrange("p u k t -> p (u k t)")[:, 0:KI * C].rearrange("p (k t) -> p k t", t=C)
               for x in (gru_x, gru_y)]
        xg = [x[:].rearrange("p k t -> p (k t)")[:, 0:KH * C].rearrange("p (k t) -> p k t", t=C) for x in tt]
        mx1 = sb("mx1", [TT, 6, 1]); keys = sb("keys", [TT, 6, E]); pr = sb("pr", [TT, 6, E]); eq = sb("eq", [TT, 6, E])
        sel = sb("sel", [TT, 2, 6, E]); top = sb("top", [TT, 2, 6]); den = sb("den", [TT, 6]); comb = sb("comb", [TT, 6, E])
        msk = sb("msk", [TT, 6, E]); pre = sb("pre", [TT, 6, E]); rk = sb("rk", [TT, 6, E], F32R)
        combs = sb("combs", [TT, 6, E, 2], F32R)
        before = sb("before", [TT, TT])
        slot_row = sb("slot_row", [TT, T])
        slot_col = sb("slot_col", [TT, PASSES * CT])
        rmx = sb("rmx", [TT, 1]); rone = sb("rone", [1, 1]); flag = sb("flag", [1, 1], mybir.dt.int32)
        identr = sb("identr", [TT, TT], F32R)
        arena = sb("arena", [P, 8704], F32R)
        G = [arena[0:TT, i * 1152:(i + 1) * 1152].rearrange("p (j c) -> p j c", c=C) for i in range(2)]
        Sm = [arena[0:TT, 2304 + i * 1152:2304 + (i + 1) * 1152].rearrange("p (u t) -> p u t", t=T) for i in range(2)]
        xth = arena[0:TT, 4608:6144].rearrange("p (j n) -> p j n", n=H)
        xtl = arena[0:TT, 6144:7680].rearrange("p (j n) -> p j n", n=H)
        ywh = arena[0:TT, 7680:8192].rearrange("p (u n) -> p u n", n=H)
        ywl = arena[0:TT, 8192:8704].rearrange("p (u n) -> p u n", n=H)
        cur = [sb(f"cur{i}", [TT, 6, 2], F32R) for i in range(2)]
        wsl2 = [sb(f"wsl{i}", [TT, CT, 2]) for i in range(2)]; wsum = sb("wsum", [TT, CT])
        zero16 = sb("zero16", [P, NT], mybir.dt.bfloat16)
        sg = [sb(f"sg{i}", [P, C]) for i in range(2)]
        gt = [sb(f"gt{i}", [P, C]) for i in range(2)]
        s_logit = sem("s_logit"); s_max = sem("s_max"); s_exp = sem("s_exp"); s_msk = sem("s_msk"); s_rank = sem("s_rank")
        s_rmx = sem("s_rmx"); s_rmt = sem("s_rmt"); s_flag = sem("s_flag"); s_rk = sem("s_rk")
        s_rbp = sem("s_rbp"); s_rb = sem("s_rb"); s_xtp = sem("s_xtp"); s_xt = sem("s_xt"); s_add = sem("s_add")
        NAMES = ("g", "s", "gath", "xg", "gu", "sig", "act", "dmm", "yw", "scat")
        ps = [{n: sem(f"s_{n}_{c}") for n in NAMES} for c in range(PASSES)]
        s_upw = [[sem(f"s_upw{c}{i}") for i in range(2)] for c in range(PASSES)]
        s_dnw = [[sem(f"s_dnw{c}{i}") for i in range(2)] for c in range(PASSES)]
        s_vact = [sem(f"s_vact{c}") for c in range(PASSES)]
        s_vy = [sem(f"s_vy{c}") for c in range(PASSES)]

        qt, kt = [x[:].rearrange("p u k t -> p (u k t)").rearrange("p (m t) -> p m t", t=T) for x in (gru_x, gru_y)]
        vt = wdn2[0:AT].rearrange("p i k n -> p (i k n)").rearrange("p (t n) -> p t n", t=NAT)
        ot = wgf[:, 4 * T:8 * T].rearrange("p (m t) -> p m t", t=T)
        gex = sb("gex", [AT, NAT, HEADS])
        sc, pt = [[x[0:AT].rearrange("p k t -> p (k t)").rearrange("p (e t) -> p e t", t=AT) for x in b]
                  for b in (zz, aa)]
        rmax = sb("rmax", [AT, HEADS]); rsum = sb("rsum", [AT, HEADS]); rden = sb("rden", [AT, HEADS])
        s_qk = sem("s_qk"); s_qkc = sem("s_qkc"); s_vg = sem("s_vg"); s_vgc = sem("s_vgc"); s_ge = sem("s_ge")
        s_sc = sem("s_sc"); s_sm = sem("s_sm"); s_scf = sem("s_scf"); s_ex = sem("s_ex"); s_pn = sem("s_pn")
        s_ptp = sem("s_ptp"); s_pt = sem("s_pt"); s_o = sem("s_o"); s_oc = sem("s_oc")
        s_wo = sem("s_wo"); s_ha = sem("s_ha")

        q1 = arena[:, 0:2048].rearrange("p (k n) -> p k n", k=KH)
        q2 = arena[:, 2048:4096].rearrange("p (k n) -> p k n", k=KI)
        w1 = wup[1][:, 0, :].rearrange("p (k n) -> p k n", k=KH)
        w2 = wup[1][:, 1, :].rearrange("p (k n) -> p k n", k=KI)
        qtmp = wup[0]
        asum = sb("asum", [P, 2]); ws = sb("ws", [P, 2]); wsi = sb("wsi", [P, 2])
        xh = sb("xh", [P, KH, NT], F32R); xl = sb("xl", [P, KH, NT], F32R)
        gy = wgf[:, 0:4 * T].rearrange("p (k t) -> p k t", t=NT)
        gsq = gru_x[:].rearrange("p u k t -> p (u k) t")
        yh = [sb(f"yh{i}", [P, NT], F32R) for i in range(2)]
        yl = [sb(f"yl{i}", [P, NT], F32R) for i in range(2)]
        vh = sb("vh", [P, KI, 2], F32R); vl = sb("vl", [P, KI, 2], F32R)
        gb = sb("gb", [P, KH, 2])
        oc = wgf[0:TT, 8 * T:8 * T + 6 * H].rearrange("p (t n) -> p t n", n=H)
        s_abs = sem("s_abs"); s_absp = sem("s_absp"); s_q1 = sem("s_q1"); s_q2 = sem("s_q2")
        s_xs = sem("s_xs"); s_u = sem("s_u"); s_gel = sem("s_gel"); s_gsq = sem("s_gsq"); s_ys = sem("s_ys")
        s_w2 = sem("s_w2"); s_st2 = sem("s_st2"); s_ve2 = sem("s_ve2"); s_pow2 = sem("s_pow2"); s_rm2 = sem("s_rm2")
        s_bc2 = sem("s_bc2"); s_fin = sem("s_fin"); s_gbp = sem("s_gbp"); s_tr = sem("s_tr"); s_trc = sem("s_trc"); s_out = sem("s_out")

        block = ctx.enter_context(nc.Block())

        @block.sync
        def _(sp):
            sp.dma_start(wt[:], w_tok.rearrange("(k p) n -> p k n", p=P)).then_inc(s_load["wt"], 16)
            sp.dma_start(xp[:], patches.rearrange("(k p) n -> p k n", p=P)).then_inc(s_load["xp"], 16)
            sp.dma_start(vec[:], vecs).then_inc(s_load["vec"], 16)
            for l in range(L):
                sp.dma_start(wg[:, l], w_gru[l].rearrange("d g (k p) n -> p d g k n", p=P)).then_inc(s_load[f"wg{l}"], 16)
            sp.dma_start(wf[:], w_fus.rearrange("(k p) n -> p k n", p=P)).then_inc(s_load["wf"], 16)
            sp.dma_start(wr[:], w_gate.rearrange("(k p) n -> p k n", p=P)).then_inc(s_load["wr"], 16)
            def experts_load(c):
                for i in range(2):
                    sp.dma_start(wup[i][:], w_up[i].rearrange("(k p) n -> p k n", p=P)).then_inc(s_upw[c][i], 16)
                    sp.dma_start(wdn[i], w_down[i].rearrange("(k p) n -> p k n", p=P)).then_inc(s_dnw[c][i], 16)
                    if c == 0 and i == 0:
                        sp.wait_ge(s_tok, 4)
                        sp.dma_start(wqkv, w_qkv.rearrange("(k p) n -> p k n", p=P)).then_inc(s_load["wqkv"], 16)
                        sp.dma_start(wo, w_o.rearrange("(k p) n -> p k n", p=P)).then_inc(s_load["wo"], 16)
                        sp.dma_start(wga[:], w_gates.rearrange("(k p) n -> p k n", p=P)).then_inc(s_load["wga"], 16)
                with sp.Fori(1, NP) as pair:
                    for i in range(2):
                        sp.wait_ge(ps[c]["gu"], pair * 2 * KI + (i - 1) * KI)
                        sp.dma_start(wup[i][:], w_up[pair * 2 + i].rearrange("(k p) n -> p k n", p=P))\
                          .then_inc(s_upw[c][i], 16)
                        sp.wait_ge(ps[c]["dmm"], pair * 2 + (i - 1))
                        sp.dma_start(wdn[i], w_down[pair * 2 + i].rearrange("(k p) n -> p k n", p=P))\
                          .then_inc(s_dnw[c][i], 16)

            experts_load(0)
            sp.wait_ge(s_flag, 1)
            with sp.If(sp.value_load(flag[0:1, 0:1]) > 0):
                for c in range(1, PASSES):
                    sp.wait_ge(ps[c - 1]["scat"], E)
                    experts_load(c)
            sp.wait_ge(s_add, 2)
            sp.dma_start(w1, w_1.rearrange("(k p) n -> p k n", p=P)).then_inc(s_load["w1"], 16)
            sp.dma_start(w2, w_2.rearrange("(k p) n -> p k n", p=P)).then_inc(s_load["w2"], 16)
            for j in range(6):
                sp.wait_ge(s_trc, j + 1)
                sp.dma_start(out[j * TT:(j + 1) * TT, :], oc[:, j, :]).then_inc(s_out, 16)
            sp.wait_ge(s_out, 16 * 6)

        @block.gpsimd
        def _(pool):
            pool.memset(ident[:], 0.0).then_inc(s_const, 1)
            pool.memset(cmask[:], MASKED).then_inc(s_const, 1)
            pool.memset(half_neg[:], -0.5).then_inc(s_const, 1)
            pool.iota(ranks[:], pattern=[[-1, E]], base=E, channel_multiplier=0,
                      allow_small_or_imprecise_dtypes=True).then_inc(s_const, 1)
            pool.memset(before[:], 1.0).then_inc(s_const, 1)
            pool.iota(slot_row[:], pattern=[[1, T]], base=0, channel_multiplier=0,
                      allow_small_or_imprecise_dtypes=True).then_inc(s_const, 1)
            pool.iota(slot_col[:], pattern=[[TT, PASSES * CT]], base=0, channel_multiplier=1,
                      allow_small_or_imprecise_dtypes=True).then_inc(s_const, 1)
            pool.memset(zero16[:], 0.0).then_inc(s_const, 1)
            pool.wait_ge(s_const, 8)
            pool.affine_select(out=ident[:], in_=ident[:], compare_op=ALU.not_equal, fill=1.0, base=0,
                               pattern=[[-1, P]], channel_multiplier=1).then_inc(s_const, 1)
            pool.affine_select(out=cmask[:], in_=cmask[:], compare_op=ALU.is_gt, fill=0.0, base=0,
                               pattern=[[1, AT]], channel_multiplier=-1).then_inc(s_const, 1)
            pool.affine_select(out=before[:], in_=before[:], compare_op=ALU.is_gt, fill=0.0, base=0,
                               pattern=[[1, TT]], channel_multiplier=-1).then_inc(s_const, 1)
            pool.wait_ge(s_const, 11)
            pool.affine_select(out=cmask[:, 0:S], in_=cmask[:, 0:S], compare_op=ALU.is_gt, fill=MASKED, base=S,
                               pattern=[[0, S]], channel_multiplier=-1).then_inc(s_const, 1)

            def power(i):
                pool.wait_ge(s_ve, i + 1)
                if i >= 2:
                    pool.wait_ge(s_bc, i - 1)
                pool.tensor_tensor(rm[i % 2][:, 0:3], ve[:], half_neg[0:TT, :], ALU.pow).then_inc(s_pow, 1)

            for i in range(LN_GRU):
                power(i)
            for s in range(STEPS + 1):
                if s >= 1:
                    power(LN_GRU + s - 1)
                if s < STEPS:
                    d, y = s % 2, aa[s % 2]
                    first = 0 if d == 0 else S - 1
                    pool.wait_ge(s_clip, s + 1)
                    pool.memset(both(y)[:, first::S], 0.0).then_inc(s_edge, 1)
            for i in range(LN_MOE, LN_ALL):
                power(i)
            for n in range(2):
                pool.wait_ge(s_ve2, n + 1)
                pool.tensor_tensor(rm[n][:, 0:3], ve[:], half_neg[0:TT, :], ALU.pow).then_inc(s_pow2, 1)

        @block.tensor
        def _(pe):
            def ln_sums(i):
                y = ln_source(i)
                pe.wait_ge(s_sq, i + 1)
                if i >= 1:
                    pe.wait_ge(s_rm, i)
                for c, src in enumerate((y, sq[i % 2])):
                    for j in range(JT):
                        for k in range(KH):
                            last = pe.matmul(bank[0:TT, 4, c * JT + j:c * JT + j + 1],
                                             src[:, k, j * TT:(j + 1) * TT], mean_h[:],
                                             start=(k == 0), stop=(k == KH - 1))
                last.then_inc(s_st, 1)

            def ln_spread(i):
                pe.wait_ge(s_rm, i + 1)
                if i >= 1:
                    pe.wait_ge(s_norm, i)
                for c in range(2):
                    for j in range(JT):
                        last = pe.matmul(bank[:, 5 + c, j * TT:(j + 1) * TT],
                                         rm[i % 2][:, c * JT + j:c * JT + j + 1].broadcast_to([TT, P]),
                                         ident[0:TT, 0:TT], start=True, stop=True)
                last.then_inc(s_bc, 1)

            pe.wait_ge(s_load["wt"], 16)
            pe.wait_ge(s_load["xp"], 16)
            for n in range(2):
                for m in range(KH):
                    for k in range(KF):
                        last = pe.matmul(bank[:, 2 * n + m, 0:NT], wt[:, k, m * P:(m + 1) * P],
                                         xp[:, k, half(n)], start=(k == 0), stop=(k == KF - 1))
                    last.then_inc(s_tok, 1)
            pe.wait_ge(s_const, 12)
            pe.wait_ge(s_vconst, 4)
            for i in range(LN_GRU):
                ln_sums(i)
                ln_spread(i)

            for s in range(STEPS + 2):
                if s < STEPS:
                    l, u, d, n = unit(s)
                    if l == 0:
                        pe.wait_ge(s_norm, n + 1)
                    else:
                        pe.wait_ge(s_aff, s - UNITS + 1)
                    if u == 0:
                        pe.wait_ge(s_load[f"wg{l}"], 16)
                    for g, (done, free) in enumerate(((s_zmm, s_gz), (s_hmm, s_gt))):
                        if s >= 1:
                            pe.wait_ge(free, s)
                        for m in range(KH):
                            for k in range(KH):
                                src = xn[:, k, half(n)] if l == 0 else xx[u][:, k, :]
                                last = pe.matmul(bank[:, 2 * g + m, 0:NT], wg[:, l, d, g, k, m * P:(m + 1) * P], src,
                                                 start=(k == 0), stop=(k == KH - 1))
                        last.then_inc(done, 1)
                if 1 <= s <= STEPS:
                    ln_sums(LN_GRU + s - 1)
                if s >= 2:
                    ln_spread(LN_GRU + s - 2)

            pe.wait_ge(s_load["wf"], 16)
            pe.wait_ge(s_gz, STEPS)
            pe.wait_ge(s_gt, STEPS)
            for n in range(2):
                pe.wait_ge(s_aff, STEPS - UNITS + 2 * n + 2)
                for m in range(KH):
                    for k in range(4):
                        last = pe.matmul(bank[:, 2 * n + m, 0:NT], wf[:, k, m * P:(m + 1) * P],
                                         xx[2 * n + k // 2][:, k % 2, :], start=(k == 0), stop=(k == 3))
                last.then_inc(s_fus, 1)

            for n in range(2):
                ln_sums(LN_MOE + n)
                ln_spread(LN_MOE + n)
            pe.wait_ge(s_load["wr"], 16)
            pe.wait_ge(s_norm, LN_MOE + 2)
            for j in range(6):
                for k in range(KH):
                    last = pe.matmul(bank[0:TT, 7, j * E:(j + 1) * E], xn[:, k, j * TT:(j + 1) * TT], wr[:, k, :],
                                     start=(k == 0), stop=(k == KH - 1))
            last.then_inc(s_logit, 1)
            pe.wait_ge(s_msk, 1)
            flat = lambda x: x[:].rearrange("p j e -> p (j e)")
            pe.matmul(bank[0:TT, 7, 0:6 * E], before[:], flat(msk), start=True, stop=False)
            pe.matmul(bank[0:TT, 7, 0:6 * E], ones[0:TT, 0:TT], flat(pre), start=False, stop=True).then_inc(s_rank, 1)
            for j in range(6):
                if j >= 2:
                    pe.wait_ge(s_xt, j - 1)
                for m in range(KH):
                    last = pe.transpose(bank[0:TT, j % 2, m * P:(m + 1) * P], xn[:, m, j * TT:(j + 1) * TT], ident[:])
                last.then_inc(s_xtp, 1)
            pe.wait_ge(s_rk, 1)
            for q in range(2 * E):
                e, n = q // 2, q % 2
                if q >= 2:
                    pe.wait_ge(s_rb, q - 1)
                for j in range(JT):
                    last = pe.matmul(bank[:, 5 + n, j * TT:(j + 1) * TT],
                                     rk[:, n * JT + j, e:e + 1].broadcast_to([TT, P]), identr[:],
                                     start=True, stop=True)
                last.then_inc(s_rbp, 1)
            pe.wait_ge(s_rmx, 1)
            pe.transpose(bank[0:1, 7, 0:TT], rmx[:], ident[0:TT, 0:TT]).then_inc(s_rmt, 1)

            pe.wait_ge(s_xt, 6)
            pe.wait_ge(s_rb, 2 * E)
            for b in range(4):
                pe.matmul(bank[:, b, 0:NT], zero16[:, 0:P], zero16[:], start=True, stop=False, skip_group_check=True)

            def gather(c, x, i):
                pe.wait_ge(ps[c]["g"], x + 1)
                if i != 0 or not isinstance(x, int) or x > 0:
                    pe.wait_ge(ps[c]["xg"], x)
                for m in range(KH):
                    for part in (xth, xtl):
                        for j in range(6):
                            pe.matmul(bank[:, 6, m * C:(m + 1) * C], part[:, j, m * P:(m + 1) * P], G[i][:, j, :],
                                      start=(part is xth and j == 0), stop=(part is xtl and j == 5))
                for u in range(CT):
                    for j in range(6):
                        last = pe.matmul(bank[0:TT, 6, KH * C + 2 * u:KH * C + 2 * u + 2], G[i][:, j, u * TT:(u + 1) * TT],
                                         cur[i][:, j, :], start=(j == 0), stop=(j == 5))
                last.then_inc(ps[c]["gath"], 1)

            def up(c, x, i):
                pe.wait_ge(s_upw[c][i], (x - i) * 8 + 16)
                pe.wait_ge(ps[c]["xg"], x + 1)
                for m in range(KI):
                    if m >= 2 or not (isinstance(x, int) and x == 0):
                        pe.wait_ge(ps[c]["act"], x * KI + m - 1)
                    for g in range(2):
                        for k in range(KH):
                            last = pe.matmul(bank[:, 4 + m % 2, g * 256:g * 256 + C],
                                             wup[i][:, k, g * I + m * P:g * I + (m + 1) * P], xg[i][:, k, :],
                                             start=(k == 0), stop=(k == KH - 1))
                    last.then_inc(ps[c]["gu"], 1)

            def down(c, x, i):
                pe.wait_ge(s_dnw[c][i], (x - i) * 8 + 16)
                pe.wait_ge(ps[c]["act"], (x + 1) * KI)
                if not (isinstance(x, int) and x == 0):
                    pe.wait_ge(ps[c]["yw"], x)
                for u in range(CT):
                    for k in range(KI):
                        last = pe.matmul(bank[0:TT, 7, u * H:(u + 1) * H], act[i][:, k, u * TT:(u + 1) * TT],
                                         wdn[i][:, k, :], start=(k == 0), stop=(k == KI - 1))
                last.then_inc(ps[c]["dmm"], 1)

            def scatter(c, x, i):
                pe.wait_ge(ps[c]["yw"], x + 1)
                pe.wait_ge(ps[c]["s"], x + 1)
                for m in range(KH):
                    for n in range(2):
                        for u in range(CT):
                            for part in (ywh, ywl):
                                last = pe.matmul(bank[:, 2 * m + n, 0:NT], part[:, u, m * P:(m + 1) * P],
                                                 Sm[i][:, u, half(n)], start=False, stop=False, skip_group_check=True)
                last.then_inc(ps[c]["scat"], 1)

            def experts(c):
                gather(c, 0, 0)
                up(c, 0, 0)
                with pe.Fori(0, NP - 1) as pair:
                    x = pair * 2
                    gather(c, x + 1, 1)
                    down(c, x, 0)
                    up(c, x + 1, 1)
                    scatter(c, x, 0)
                    gather(c, x + 2, 0)
                    down(c, x + 1, 1)
                    up(c, x + 2, 0)
                    scatter(c, x + 1, 1)
                gather(c, E - 1, 1)
                down(c, E - 2, 0)
                up(c, E - 1, 1)
                scatter(c, E - 2, 0)
                down(c, E - 1, 1)
                scatter(c, E - 1, 1)

            experts(0)
            pe.wait_ge(s_flag, 1)
            with pe.If(pe.value_load(flag[0:1, 0:1]) > 0):
                for c in range(1, PASSES):
                    experts(c)

            pe.wait_ge(s_add, 2)
            for n in range(2):
                ln_sums(LN_ATT + n)
                ln_spread(LN_ATT + n)
            pe.wait_ge(s_load["wqkv"], 16)
            pe.wait_ge(s_load["wga"], 16)
            pe.wait_ge(s_aff, affine_count(LN_ATT + 1))
            for q in range(16):
                if q >= 4:
                    pe.wait_ge(s_qkc, q - 3)
                c, m, n = q // 8, q % 8 // 2, q % 2
                for k in range(KH):
                    last = pe.matmul(bank[:, q % 4, 0:NT], wqkv[:, k, c * 512 + m * P:c * 512 + (m + 1) * P],
                                     xn[:, k, half(n)], start=(k == 0), stop=(k == KH - 1))
                last.then_inc(s_qk, 1)
            pe.wait_ge(s_qkc, 16)
            for t in range(NAT):
                if t >= 2:
                    pe.wait_ge(s_vgc, t - 1)
                for k in range(KH):
                    pe.matmul(bank[0:AT, 2 * (t % 2), :], xn[:, k, t * AT:(t + 1) * AT], wqkv[:, k, 1024:1536],
                              start=(k == 0), stop=(k == KH - 1))
                for k in range(KH):
                    last = pe.matmul(bank[0:AT, 2 * (t % 2) + 1, 0:HEADS], xn[:, k, t * AT:(t + 1) * AT], wga[:, k, :],
                                     start=(k == 0), stop=(k == KH - 1))
                last.then_inc(s_vg, 1)
            pe.wait_ge(s_vgc, NAT)
            pe.wait_ge(s_ge, NAT)

            def scores(t):
                if t >= 1:
                    pe.wait_ge(s_sm, t)
                for e in range(HEADS):
                    r = slice(64 * (e % 2), 64 * (e % 2) + 64)
                    last = pe.matmul(bank[0:AT, e % 2, (e // 2) * AT:(e // 2 + 1) * AT],
                                     qt[r, e // 2, t * AT:(t + 1) * AT], kt[r, e // 2, t * AT:(t + 1) * AT],
                                     start=True, stop=True)
                last.then_inc(s_sc, 1)

            def values(t):
                pe.wait_ge(s_pn, t + 1)
                if t >= 1:
                    pe.wait_ge(s_pt, t)
                for e in range(HEADS):
                    last = pe.transpose(bank[0:AT, 2 + e // 4, (e % 4) * AT:(e % 4 + 1) * AT],
                                        sc[t % 2][:, e, :], ident[0:AT, 0:AT])
                last.then_inc(s_ptp, 1)
                pe.wait_ge(s_pt, t + 1)
                if t >= 1:
                    pe.wait_ge(s_oc, t)
                for e in range(HEADS):
                    r = slice(64 * (e % 2), 64 * (e % 2) + 64)
                    last = pe.matmul(bank[r, 4, (e // 2) * AT:(e // 2 + 1) * AT], vt[:, t, e * DH:(e + 1) * DH],
                                     pt[t % 2][:, (e % 2) * 4 + e // 2, :], start=True, stop=True)
                last.then_inc(s_o, 1)

            scores(0)
            for t in range(1, NAT):
                scores(t)
                values(t - 1)
            values(NAT - 1)
            pe.wait_ge(s_load["wo"], 16)
            pe.wait_ge(s_oc, NAT)
            for n in range(2):
                for m in range(KH):
                    for k in range(4):
                        last = pe.matmul(bank[:, 2 * n + m, 0:NT], wo[:, k, m * P:(m + 1) * P],
                                         ot[:, k, half(n)], start=(k == 0), stop=(k == 3))
                last.then_inc(s_wo, 1)

            pe.wait_ge(s_abs, 2)
            pe.matmul(bank[:, 7, 0:2], ones[:], asum[:], start=True, stop=True).then_inc(s_absp, 1)
            for n in range(2):
                ln_sums(LN_MLP + n)
                ln_spread(LN_MLP + n)
            pe.wait_ge(s_q2, 1)
            pe.wait_ge(s_q1, 1)
            for m in range(KH):
                for k in range(KI):
                    for part in (vh, vl):
                        last = pe.matmul(bank[:, 7, 2 * m:2 * m + 2], q2[:, k, m * P:(m + 1) * P], part[:, k, :],
                                         start=(k == 0 and part is vh), stop=(k == KI - 1 and part is vl))
            last.then_inc(s_gbp, 1)
            for n in range(2):
                def hidden(m):
                    pe.wait_ge(s_xs, n + 1)
                    if n * KI + m >= 2:
                        pe.wait_ge(s_gel, n * KI + m - 1)
                    for k in range(KH):
                        for part in (xh, xl):
                            last = pe.matmul(bank[:, m % 2, 0:NT], q1[:, k, m * P:(m + 1) * P], part[:, k, :],
                                             start=(k == 0 and part is xh), stop=(k == KH - 1 and part is xl))
                    last.then_inc(s_u, 1)

                def outward(k):
                    pe.wait_ge(s_ys, n * KI + k + 1)
                    if n >= 1 and k == 0:
                        pe.wait_ge(s_fin, n)
                    for m in range(KH):
                        for part in (yh[k % 2], yl[k % 2]):
                            last = pe.matmul(bank[:, 2 + m, 0:NT], q2[:, k, m * P:(m + 1) * P], part[:],
                                             start=(k == 0 and part is yh[k % 2]),
                                             stop=(k == KI - 1 and part is yl[k % 2]))
                    last.then_inc(s_w2, 1)
                hidden(0)
                for k in range(KI):
                    if k + 1 < KI:
                        hidden(k + 1)
                    outward(k)
                pe.wait_ge(s_gsq, (n + 1) * KI)
                for c, src in enumerate((gy, gsq)):
                    for j in range(JT):
                        for k in range(KI):
                            last = pe.matmul(bank[0:TT, 4, c * JT + j:c * JT + j + 1],
                                             src[:, k, j * TT:(j + 1) * TT], mean_i[:],
                                             start=(k == 0), stop=(k == KI - 1))
                last.then_inc(s_st2, 1)
                pe.wait_ge(s_rm2, n + 1)
                for c in range(2):
                    for j in range(JT):
                        last = pe.matmul(bank[:, 5 + c, j * TT:(j + 1) * TT],
                                         rm[n][:, c * JT + j:c * JT + j + 1].broadcast_to([TT, P]),
                                         ident[0:TT, 0:TT], start=True, stop=True)
                last.then_inc(s_bc2, 1)
            for n in range(2):
                pe.wait_ge(s_fin, n + 1)
                for j in range(JT):
                    t = n * JT + j
                    if t >= 2:
                        pe.wait_ge(s_trc, t - 1)
                    for m in range(KH):
                        last = pe.transpose(bank[0:TT, t % 2, m * P:(m + 1) * P],
                                            h[:, m, t * TT:(t + 1) * TT], ident[:])
                    last.then_inc(s_tr, 1)

        @block.scalar
        def _(sc_):
            def squares(i, ready):
                sc_.wait_ge(*ready)
                if i >= 2:
                    sc_.wait_ge(s_st, i - 1)
                sc_.activation(sq[i % 2][:], ln_source(i), ACT.Square).then_inc(s_sq, 1)

            def affine(i, gain, shift):
                sc_.wait_ge(s_norm, i + 1)
                for m in range(KH):
                    if LN_GRU <= i < LN_MOE:
                        src, dst = yy[(i - LN_GRU) % UNITS][:, m, :], xx[(i - LN_GRU) % UNITS][:, m, :]
                    else:
                        src = dst = xn[:, m, half(i % 2)]
                    last = sc_.activation(dst, src, ACT.Identity, scale=vec[:, gain + m:gain + m + 1],
                                          bias=vec[:, shift + m:shift + m + 1] if shift is not None else 0.0)
                last.then_inc(s_aff, 1)

            for i in range(2):
                squares(i, (s_h0, 2 * i + 2))
            sc_.wait_ge(s_load["vec"], 16)
            sc_.wait_ge(s_vconst, 5)
            for s in range(STEPS + 2):
                if s < STEPS:
                    l, u, d, n = unit(s)
                    if s >= 2:
                        sc_.wait_ge(s_y, s - 1)
                    sc_.wait_ge(s_zmm, s + 1)
                    c = (l * 2 + d) * 2
                    for m in range(KH):
                        sc_.activation(aa[s % 2][:, m, :], bank[:, m, 0:NT], ACT.Sigmoid, scale=-1.0,
                                       bias=nbz[:, c + m:c + m + 1])
                        last = sc_.activation(zz[s % 2][:, m, :], bank[:, m, 0:NT], ACT.Sigmoid,
                                              bias=vec[:, V_BZ + c + m:V_BZ + c + m + 1])
                    last.then_inc(s_gz, 1)
                    sc_.wait_ge(s_hmm, s + 1)
                    for m in range(KH):
                        last = sc_.activation(tt[s % 2][:, m, :], bank[:, 2 + m, 0:NT], ACT.Tanh,
                                              bias=vec[:, V_BH + c + m:V_BH + c + m + 1])
                    last.then_inc(s_gt, 1)
                if s >= 2:
                    affine(LN_GRU + s - 2, V_GAM, V_BET)
                if s < STEPS:
                    squares(LN_GRU + s, (s_y, s + 1))
            for n in range(2):
                squares(LN_MOE + n, (s_hf, n + 1))
            sc_.wait_ge(s_max, 2)
            sc_.activation(pr[:], pr[:], ACT.Exp).then_inc(s_exp, 1)
            for q in range(2 * E):
                sc_.wait_ge(s_rbp, q + 1)
                sc_.activation(rkb[:, q // 2, half(q % 2)], bank[:, 5 + q % 2, 0:NT], ACT.Copy).then_inc(s_rb, 1)

            def gathered(c, x, i):
                sc_.wait_ge(ps[c]["gath"], x + 1)
                if not (isinstance(x, int) and x < 2):
                    sc_.wait_ge(ps[c]["gu"], (x - 1) * KI)
                    sc_.wait_ge(ps[c]["yw"], x - 1)
                sc_.activation(wsl2[i][:], bank[0:TT, 6, KH * C:KH * C + 2 * CT].rearrange("p (u c) -> p u c", c=2),
                               ACT.Copy)
                sc_.activation(xg[i], bank[:, 6, 0:KH * C].rearrange("p (k t) -> p k t", t=C), ACT.Copy)\
                   .then_inc(ps[c]["xg"], 1)

            def sigmoids(c, x, i):
                for m in range(KI):
                    sc_.wait_ge(ps[c]["gu"], x * KI + m + 1)
                    if m >= 2 or not (isinstance(x, int) and x == 0):
                        sc_.wait_ge(ps[c]["act"], x * KI + m - 1)
                    sc_.activation(sg[m % 2][:], bank[:, 4 + m % 2, 0:C], ACT.Sigmoid).then_inc(ps[c]["sig"], 1)

            def experts(c):
                gathered(c, 0, 0)
                sigmoids(c, 0, 0)
                with sc_.Fori(0, NP - 1) as pair:
                    for i in (1, 0):
                        gathered(c, pair * 2 + 2 - i, i)
                        sigmoids(c, pair * 2 + 2 - i, i)
                gathered(c, E - 1, 1)
                sigmoids(c, E - 1, 1)

            experts(0)
            sc_.wait_ge(s_flag, 1)
            with sc_.If(sc_.value_load(flag[0:1, 0:1]) > 0):
                for c in range(1, PASSES):
                    sc_.wait_ge(ps[c - 1]["scat"], E)
                    experts(c)
            for n in range(2):
                squares(LN_ATT + n, (s_add, n + 1))
            for n in range(2):
                affine(LN_ATT + n, V_RMS, None)
            for q in range(16):
                c, m, n = q // 8, q % 8 // 2, q % 2
                sc_.wait_ge(s_qk, q + 1)
                sc_.activation((qt, kt)[c][:, m, half(n)], bank[:, q % 4, 0:NT], ACT.Copy,
                               scale=DH ** -0.5 if c == 0 else 1.0).then_inc(s_qkc, 1)
            for t in range(NAT):
                sc_.wait_ge(s_vg, t + 1)
                sc_.activation(gex[:, t, :], bank[0:AT, 2 * (t % 2) + 1, 0:HEADS], ACT.Exp, scale=-1.0).then_inc(s_ge, 1)
                sc_.activation(vt[:, t, :], bank[0:AT, 2 * (t % 2), :], ACT.Copy).then_inc(s_vgc, 1)
            for t in range(NAT + 1):
                if t < NAT:
                    sc_.wait_ge(s_scf, t + 1)
                    sc_.activation(sc[t % 2][:], sc[t % 2][:], ACT.Exp).then_inc(s_ex, 1)
                if t >= 1:
                    sc_.wait_ge(s_ptp, t)
                    if t >= 3:
                        sc_.wait_ge(s_o, t - 2)
                    sc_.activation(pt[(t - 1) % 2][:].rearrange("p (b e) t -> p b (e t)", b=2),
                                   bank[0:AT, 2:4, 0:4 * AT], ACT.Copy).then_inc(s_pt, 1)
            sc_.wait_ge(s_load["w1"], 16)
            sc_.wait_ge(s_load["w2"], 16)
            sc_.activation(qtmp[:, 0, :], w1.rearrange("p k n -> p (k n)"), ACT.Abs,
                           accum_out=asum[:, 0:1]).then_inc(s_abs, 1)
            sc_.activation(qtmp[:, 1, :], w2.rearrange("p k n -> p (k n)"), ACT.Abs,
                           accum_out=asum[:, 1:2]).then_inc(s_abs, 1)
            for n in range(2):
                squares(LN_MLP + n, (s_ha, n + 1))
            for n in range(2):
                affine(LN_MLP + n, V_L1G, V_L1B)
            for n in range(2):
                for m in range(KI):
                    q = n * KI + m
                    sc_.wait_ge(s_u, q + 1)
                    if n and m == 0:
                        sc_.wait_ge(s_st2, n)
                    sc_.activation(gy[:, m, :], bank[:, m % 2, 0:NT], ACT.Gelu, scale=wsi[:, 0:1],
                                   bias=vec[:, V_B1 + m:V_B1 + m + 1]).then_inc(s_gel, 1)
                    sc_.wait_ge(s_gel, q + 1)
                    sc_.activation(gsq[:, m, :], gy[:, m, :], ACT.Square).then_inc(s_gsq, 1)
            for t in range(6):
                sc_.wait_ge(s_tr, t + 1)
                sc_.activation(oc[:, t, :], bank[0:TT, t % 2, 0:H], ACT.Copy).then_inc(s_trc, 1)

        @block.vector
        def _(dve):
            dve.memset(ones[:], 1.0).then_inc(s_vconst, 1)
            dve.memset(mean_h[:], 1.0 / H).then_inc(s_vconst, 1)
            dve.memset(mean_i[:], 1.0 / I).then_inc(s_vconst, 1)
            dve.memset(stat[:], 0.0).then_inc(s_vconst, 1)
            dve.wait_ge(s_load["vec"], 16)
            dve.tensor_scalar(nbz[:], vec[:, V_BZ:V_BZ + 16], -1.0, None, ALU.mult).then_inc(s_vconst, 1)

            def variance(sums, a, b, done, eps_sem):
                dve.wait_ge(*sums)
                link(dve, dve.tensor_copy(stat[:], bank[0:TT, 4, 0:6]))
                link(dve, dve.tensor_tensor(msq[:], stat[:, 0:3], stat[:, 0:3], ALU.mult))
                link(dve, dve.tensor_tensor(var[:], stat[:, 3:6], msq[:], ALU.subtract))
                if a == 1.0:
                    dve.tensor_scalar(ve[:], var[:], 0.0, b, ALU.max, ALU.add).then_inc(eps_sem, 1)
                else:
                    link(dve, dve.tensor_scalar(var[:], var[:], 0.0, a, ALU.max, ALU.mult))
                    dve.tensor_scalar(ve[:], var[:], b, None, ALU.add).then_inc(eps_sem, 1)

            def ln_var(i):
                e2 = {LN_ATT: RMS_EPS, LN_MLP: EPS}.get(i - i % 2)
                if e2 is None:
                    variance((s_st, i + 1), 1.0, EPS, None, s_ve)
                else:
                    variance((s_st, i + 1), 1.0 + e2, e2 * EPS, None, s_ve)

            def ln_root(i):
                dve.wait_ge(s_pow, i + 1)
                dve.tensor_tensor(rm[i % 2][:, 3:6], stat[:, 0:3], rm[i % 2][:, 0:3], ALU.mult).then_inc(s_rm, 1)

            def ln_norm(i):
                dve.wait_ge(s_bc, i + 1)
                src, dst = ln_source(i), ln_target(i)
                link(dve, dve.tensor_tensor(dst, src, bank[:, 5:6, 0:NT].broadcast_to([P, KH, NT]), ALU.mult))
                dve.tensor_tensor(dst, dst, bank[:, 6:7, 0:NT].broadcast_to([P, KH, NT]),
                                  ALU.subtract).then_inc(s_norm, 1)

            for n in range(2):
                for m in range(KH):
                    dve.wait_ge(s_tok, 2 * n + m + 1)
                    dve.tensor_copy(h[:, m, half(n)], bank[:, 2 * n + m, 0:NT]).then_inc(s_h0, 1)
            for i in range(LN_GRU):
                ln_var(i)
                ln_root(i)
                ln_norm(i)

            for s in range(STEPS + 2):
                if 1 <= s <= STEPS:
                    ln_var(LN_GRU + s - 1)
                if s >= 2:
                    ln_norm(LN_GRU + s - 2)
                if 1 <= s <= STEPS:
                    ln_root(LN_GRU + s - 1)
                if s < STEPS:
                    l, u, d, n = unit(s)
                    z, a, t, y = zz[s % 2], aa[s % 2], tt[s % 2], yy[u]
                    dve.wait_ge(s_gz, s + 1)
                    dve.tensor_scalar(a[:], a[:], 1e-8, 1.0, ALU.max, ALU.min).then_inc(s_clip, 1)
                    dve.wait_ge(s_gt, s + 1)
                    link(dve, dve.tensor_tensor(z[:], z[:], t[:], ALU.mult))
                    dve.wait_ge(s_edge, s + 1)
                    if s >= 4:
                        dve.wait_ge(s_aff, s - 3)
                    to = y if l == 0 else t
                    rev = slice(None) if d == 0 else slice(None, None, -1)
                    scan = dve.tensor_tensor_scan(both(to)[:, rev], both(a)[:, rev], both(z)[:, rev], 0.0,
                                                  ALU.mult, ALU.add)
                    if l == 0:
                        scan.then_inc(s_y, 1)
                    else:
                        link(dve, scan)
                        dve.tensor_tensor(y, t[:], xx[u], ALU.add).then_inc(s_y, 1)

            for n in range(2):
                dve.wait_ge(s_fus, n + 1)
                for m in range(KH):
                    last = dve.scalar_tensor_tensor(out=h[:, m, half(n)], in0=bank[:, 2 * n + m, 0:NT],
                                                    scalar=vec[:, V_FB + m:V_FB + m + 1], in1=h[:, m, half(n)],
                                                    op0=ALU.add, op1=ALU.add)
                last.then_inc(s_hf, 1)
            for n in range(2):
                ln_var(LN_MOE + n)
                ln_root(LN_MOE + n)
                ln_norm(LN_MOE + n)

            def over(x):
                return x.broadcast_to([TT, 6, E])
            lg = bank[0:TT, 7, 0:6 * E].rearrange("p (j e) -> p j e", e=E)
            dve.wait_ge(s_logit, 1)
            link(dve, dve.tensor_reduce(mx1[:], lg, AX_X, ALU.max))
            dve.tensor_tensor(pr[:], lg, over(mx1[:]), ALU.subtract).then_inc(s_max, 2)
            dve.wait_ge(s_exp, 1)
            link(dve, dve.tensor_reduce(mx1[:], pr[:], AX_X, ALU.add))
            link(dve, dve.reciprocal(mx1[:], mx1[:]))
            link(dve, dve.tensor_tensor(pr[:], pr[:], over(mx1[:]), ALU.mult))
            dve.wait_ge(s_const, 12)
            prefer = ranks[0:TT, :].rearrange("p (o e) -> p o e", o=1).broadcast_to([TT, 6, E])
            for c in range(2):
                link(dve, dve.tensor_reduce(top[:, c, :], pr[:], AX_X, ALU.max))
                tc = top[:, c, :].rearrange("p (j o) -> p j o", o=1)
                link(dve, dve.tensor_tensor(eq[:], pr[:], over(tc), ALU.is_equal))
                link(dve, dve.tensor_tensor(keys[:], eq[:], prefer, ALU.mult))
                link(dve, dve.tensor_reduce(mx1[:], keys[:], AX_X, ALU.max))
                link(dve, dve.tensor_tensor(sel[:, c], keys[:], over(mx1[:]), ALU.is_equal))
                link(dve, dve.scalar_tensor_tensor(out=pr[:], in0=sel[:, c], scalar=-2.0, in1=pr[:],
                                                   op0=ALU.mult, op1=ALU.add))
            link(dve, dve.tensor_tensor(msk[:], sel[:, 0], sel[:, 1], ALU.add))
            link(dve, dve.memset(pre[:, 0, :], 0.0))
            for j in range(1, 6):
                ins = dve.tensor_tensor(pre[:, j, :], pre[:, j - 1, :], msk[:, j - 1, :], ALU.add)
                link(dve, ins) if j < 5 else ins.then_inc(s_msk, 1)
            link(dve, dve.tensor_tensor(den[:], top[:, 0, :], top[:, 1, :], ALU.add))
            link(dve, dve.reciprocal(den[:], den[:]))
            for c in range(2):
                link(dve, dve.tensor_tensor(top[:, c, :], top[:, c, :], den[:], ALU.mult))
                link(dve, dve.tensor_tensor(sel[:, c], sel[:, c],
                                            over(top[:, c, :].rearrange("p (j o) -> p j o", o=1)), ALU.mult))
            link(dve, dve.tensor_tensor(comb[:], sel[:, 0], sel[:, 1], ALU.add))
            link(dve, dve.tensor_copy(combs[:, :, :, 0], comb[:]))
            link(dve, dve.tensor_tensor(combs[:, :, :, 1], comb[:], combs[:, :, :, 0].bitcast(F32), ALU.subtract))
            link(dve, dve.tensor_copy(identr[:], ident[0:TT, 0:TT]))
            dve.wait_ge(s_rank, 1)
            link(dve, dve.scalar_tensor_tensor(out=keys[:], in0=bank[0:TT, 7, 0:6 * E].rearrange("p (j e) -> p j e", e=E),
                                               scalar=1.0, in1=msk[:], op0=ALU.add, op1=ALU.mult))
            dve.tensor_scalar(rk[:], keys[:], -1.0, None, ALU.add).then_inc(s_rk, 1)
            dve.tensor_reduce(rmx[:], keys[:].rearrange("p j e -> p (j e)"), AX_X, ALU.max).then_inc(s_rmx, 1)
            for j in range(6):
                dve.wait_ge(s_xtp, j + 1)
                link(dve, dve.tensor_copy(xth[:, j, :], bank[0:TT, j % 2, 0:H]))
                dve.tensor_tensor(xtl[:, j, :], bank[0:TT, j % 2, 0:H], xth[:, j, :].bitcast(F32),
                                  ALU.subtract).then_inc(s_xt, 1)
            dve.wait_ge(s_rmt, 1)
            link(dve, dve.tensor_reduce(rone[:], bank[0:1, 7, 0:TT], AX_X, ALU.max))
            dve.tensor_scalar(flag[:], rone[:], float(C) + 0.5, None, ALU.is_gt).then_inc(s_flag, 1)

            dve.wait_ge(s_rb, 2 * E)
            dve.wait_ge(s_rk, 1)

            def matrix_g(c, x, i):
                if not (isinstance(x, int) and x < 2):
                    dve.wait_ge(ps[c]["gath"], x - 1)
                dve.tensor_copy(cur[i][:], combs[:, :, x, :].bitcast(F32))
                dve.tensor_tensor(G[i],
                                  slot_row[:, c * C:(c + 1) * C].rearrange("p (o s) -> p o s", o=1).broadcast_to([TT, 6, C]),
                                  rk[:, :, x].bitcast(F32).rearrange("p (j o) -> p j o", o=1).broadcast_to([TT, 6, C]),
                                  ALU.is_equal).then_inc(ps[c]["g"], 1)

            def matrix_s(c, x, i):
                if not (isinstance(x, int) and x < 2):
                    dve.wait_ge(ps[c]["scat"], x - 1)
                for u in range(CT):
                    last = dve.tensor_scalar(Sm[i][:, u, :], rkb[0:TT, x, :], slot_col[:, c * CT + u:c * CT + u + 1], None,
                                             ALU.is_equal)
                last.then_inc(ps[c]["s"], 1)

            def activate(c, x, i):
                if not (isinstance(x, int) and x < 2):
                    dve.wait_ge(ps[c]["dmm"], x - 1)
                for m in range(KI):
                    dve.wait_ge(ps[c]["sig"], x * KI + m + 1)
                    dve.tensor_tensor(gt[m % 2][:], bank[:, 4 + m % 2, 0:C], sg[m % 2][:], ALU.mult).then_inc(s_vact[c], 1)
                    dve.wait_ge(s_vact[c], x * KI + m + 1)
                    dve.tensor_tensor(act[i][:, m, :], bank[:, 4 + m % 2, 256:256 + C], gt[m % 2][:],
                                      ALU.mult).then_inc(ps[c]["act"], 1)

            def outputs(c, x, i):
                dve.wait_ge(ps[c]["xg"], x + 1)
                dve.tensor_reduce(wsum[:], wsl2[i][:], AX_X, ALU.add).then_inc(s_vy[c], 1)
                dve.wait_ge(s_vy[c], x * (1 + CT) + 1)
                dve.wait_ge(ps[c]["dmm"], x + 1)
                if not (isinstance(x, int) and x == 0):
                    dve.wait_ge(ps[c]["scat"], x)
                for u in range(CT):
                    dve.tensor_scalar(ywh[:, u, :], bank[0:TT, 7, u * H:(u + 1) * H], wsum[:, u:u + 1], None,
                                      ALU.mult).then_inc(s_vy[c], 1)
                for u in range(CT):
                    dve.wait_ge(s_vy[c], x * (1 + CT) + 2 + u)
                    last = dve.scalar_tensor_tensor(out=ywl[:, u, :], in0=bank[0:TT, 7, u * H:(u + 1) * H],
                                                    scalar=wsum[:, u:u + 1], in1=ywh[:, u, :].bitcast(F32),
                                                    op0=ALU.mult, op1=ALU.subtract)
                last.then_inc(ps[c]["yw"], 1)

            def experts(c):
                matrix_g(c, 0, 0)
                matrix_g(c, 1, 1)
                matrix_s(c, 0, 0)
                activate(c, 0, 0)
                with dve.Fori(0, NP - 1) as pair:
                    x = pair * 2
                    for i in range(2):
                        matrix_g(c, x + 2 + i, i)
                        matrix_s(c, x + 1 + i, 1 - i)
                        outputs(c, x + i, i)
                        activate(c, x + 1 + i, 1 - i)
                matrix_s(c, E - 1, 1)
                outputs(c, E - 2, 0)
                activate(c, E - 1, 1)
                outputs(c, E - 1, 1)

            experts(0)
            dve.wait_ge(ps[0]["scat"], E)
            dve.wait_ge(s_flag, 1)
            with dve.If(dve.value_load(flag[0:1, 0:1]) > 0):
                for c in range(1, PASSES):
                    experts(c)
                    dve.wait_ge(ps[c]["scat"], E)
            for n in range(2):
                for m in range(KH):
                    last = dve.tensor_tensor(h[:, m, half(n)], bank[:, 2 * m + n, 0:NT], h[:, m, half(n)], ALU.add)
                last.then_inc(s_add, 1)

            for n in range(2):
                ln_var(LN_ATT + n)
                ln_root(LN_ATT + n)
                ln_norm(LN_ATT + n)

            def softmax_in(t):
                dve.wait_ge(s_sc, t + 1)
                if t >= 2:
                    dve.wait_ge(s_ptp, t - 1)
                x = sc[t % 2]
                for b in range(2):
                    last = dve.tensor_tensor(x[:, 4 * b:4 * b + 4, :],
                                             bank[0:AT, b, 0:4 * AT].rearrange("p (e t) -> p e t", e=4),
                                             cmask[:].rearrange("p (o t) -> p o t", o=1).broadcast_to([AT, 4, AT]),
                                             ALU.add)
                    last.then_inc(s_v, 1)
                    chain[0] += 1
                dve.wait_ge(s_v, chain[0])
                dve.tensor_reduce(rmax[:], x[:], AX_X, ALU.max).then_inc(s_sm, 1)
                dve.wait_ge(s_sm, t + 1)
                dve.tensor_tensor(x[:], x[:], rmax[:].rearrange("p (e o) -> p e o", o=1).broadcast_to([AT, HEADS, AT]),
                                  ALU.subtract).then_inc(s_scf, 1)

            def softmax_out(t):
                x = sc[t % 2]
                dve.wait_ge(s_ex, t + 1)
                link(dve, dve.tensor_reduce(rsum[:], x[:], AX_X, ALU.add))
                link(dve, dve.scalar_tensor_tensor(out=rden[:], in0=gex[:, t, :], scalar=1.0, in1=rsum[:],
                                                   op0=ALU.add, op1=ALU.mult))
                link(dve, dve.reciprocal(rden[:], rden[:]))
                dve.tensor_tensor(x[:], x[:], rden[:].rearrange("p (e o) -> p e o", o=1).broadcast_to([AT, HEADS, AT]),
                                  ALU.mult).then_inc(s_pn, 1)

            def keep_out(t):
                dve.wait_ge(s_o, t + 1)
                dve.tensor_copy(ot[:, :, t * AT:(t + 1) * AT],
                                bank[:, 4, 0:4 * AT].rearrange("p (e t) -> p e t", e=4)).then_inc(s_oc, 1)

            softmax_in(0)
            for t in range(NAT):
                if t + 1 < NAT:
                    softmax_in(t + 1)
                softmax_out(t)
                if t >= 1:
                    keep_out(t - 1)
            keep_out(NAT - 1)
            for n in range(2):
                dve.wait_ge(s_wo, n + 1)
                dve.tensor_tensor(h[:, :, half(n)], bank[:, 2 * n:2 * n + 2, 0:NT], h[:, :, half(n)],
                                  ALU.add).then_inc(s_ha, 1)

            dve.wait_ge(s_absp, 1)
            link(dve, dve.tensor_scalar(wsi[:], bank[:, 7, 0:2], 1.0 / (H * I), 1e-5, ALU.mult, ALU.max))
            link(dve, dve.reciprocal(ws[:], wsi[:]))
            link(dve, dve.reciprocal(wsi[:], ws[:]))
            for c, (w, q, done) in enumerate(((w1, q1, s_q1), (w2, q2, s_q2))):
                flat = w.rearrange("p k n -> p (k n)")
                dve.wait_ge(s_absp, 1)
                dve.tensor_scalar(qtmp[:, 0, :], flat, ws[:, c:c + 1], -0.5, ALU.mult, ALU.is_lt).then_inc(s_v, 1)
                dve.tensor_scalar(qtmp[:, 1, :], flat, ws[:, c:c + 1], 0.5, ALU.mult, ALU.is_gt).then_inc(s_v, 1)
                chain[0] += 2
                dve.wait_ge(s_v, chain[0])
                ins = dve.tensor_tensor(q[:].rearrange("p k n -> p (k n)"), qtmp[:, 1, :], qtmp[:, 0, :], ALU.subtract)
                link(dve, ins)
                if c == 0:
                    dve.tensor_copy(msq[:], var[:]).then_inc(done, 1)
            gbv = vec[:, V_GB2:V_GB2 + 16].rearrange("p (k c) -> p k c", c=2)
            link(dve, dve.tensor_copy(vh[:], gbv))
            dve.tensor_tensor(vl[:], gbv, vh[:].bitcast(F32), ALU.subtract).then_inc(s_q2, 1)

            for n in range(2):
                ln_var(LN_MLP + n)
                ln_root(LN_MLP + n)
                ln_norm(LN_MLP + n)
            dve.wait_ge(s_gbp, 1)
            link(dve, dve.tensor_scalar(gb[:], bank[:, 7, 0:4].rearrange("p (m c) -> p m c", c=2), wsi[:, 1:2],
                                        None, ALU.mult))
            for m in range(KH):
                link(dve, dve.tensor_tensor(gb[:, m, 1:2], gb[:, m, 1:2], vec[:, V_B2 + m:V_B2 + m + 1], ALU.add))
            for n in range(2):
                dve.wait_ge(s_aff, affine_count(LN_MLP + n))
                if n:
                    dve.wait_ge(s_u, n * KI)
                link(dve, dve.tensor_copy(xh[:], xn[:, :, half(n)]))
                dve.tensor_tensor(xl[:], xn[:, :, half(n)], xh[:].bitcast(F32), ALU.subtract).then_inc(s_xs, 1)
                for k in range(KI):
                    q = n * KI + k
                    dve.wait_ge(s_gel, q + 1)
                    if q >= 2:
                        dve.wait_ge(s_w2, q - 1)
                    g2 = vec[:, V_GB2 + 2 * k:V_GB2 + 2 * k + 1]
                    link(dve, dve.tensor_scalar(yh[k % 2][:], gy[:, k, :], g2, None, ALU.mult))
                    dve.scalar_tensor_tensor(out=yl[k % 2][:], in0=gy[:, k, :], scalar=g2, in1=yh[k % 2][:].bitcast(F32),
                                             op0=ALU.mult, op1=ALU.subtract).then_inc(s_ys, 1)
                variance((s_st2, n + 1), 1.0, EPS, None, s_ve2)
                dve.wait_ge(s_pow2, n + 1)
                dve.tensor_tensor(rm[n][:, 3:6], stat[:, 0:3], rm[n][:, 0:3], ALU.mult).then_inc(s_rm2, 1)
                dve.wait_ge(s_w2, (n + 1) * KI)
                dve.wait_ge(s_bc2, n + 1)
                tmp, tmp2 = zz[0], zz[1]
                link(dve, dve.tensor_copy(tmp2[:, 0, :], bank[:, 5, 0:NT]))
                link(dve, dve.scalar_tensor_tensor(out=tmp[:], in0=bank[:, 2:4, 0:NT], scalar=wsi[:, 1:2],
                                                   in1=tmp2[:, 0:1, :].broadcast_to([P, KH, NT]), op0=ALU.mult, op1=ALU.mult))
                for m in range(KH):
                    link(dve, dve.tensor_scalar(tmp2[:, m, :], bank[:, 6, 0:NT], gb[:, m, 0:1], gb[:, m, 1:2],
                                                ALU.mult, ALU.subtract))
                link(dve, dve.tensor_tensor(tmp[:], tmp[:], tmp2[:], ALU.subtract))
                dve.tensor_tensor(h[:, :, half(n)], h[:, :, half(n)], tmp[:], ALU.add).then_inc(s_fin, 1)


def kernel(**inputs):
    import numpy as np
    import concourse.bacc as bacc
    from concourse.bass_utils import run_bass_kernel_spmd

    a = {k: np.asarray(v) for k, v in inputs.items()}
    c = np.ascontiguousarray
    px = a["x"].reshape(B, 3, 6, 16, 6, 16).transpose(0, 1, 3, 5, 2, 4).reshape(T, FLAT)

    def cols(v):
        return v.reshape(-1, P).T

    gru = np.stack([np.stack([a[f"L0_attn_{d}_W{g}"] for g in "zh"], 1) for d in ("fwd", "bwd")], 1)
    bias = [np.stack([a["L0_attn_fwd_b" + g], a["L0_attn_bwd_b" + g]], 1) for g in "zh"]
    gb2 = np.stack([cols(a["L1_ffn_ln2_g"]), cols(a["L1_ffn_ln2_b"])], 2).reshape(P, 16)
    vecs = np.concatenate([cols(bias[0]), cols(bias[1]), cols(a["L0_attn_ln_gamma"]), cols(a["L0_attn_ln_beta"]),
                           cols(a["L0_attn_fusion_b"]), cols(a["L1_attn_rms_w"]), cols(a["L1_ffn_ln1_g"]),
                           cols(a["L1_ffn_ln1_b"]), cols(a["L1_ffn_b1"]), gb2, cols(a["L1_ffn_b2"])], 1)
    qkv = np.concatenate([a[f"L1_attn_w{n}"].transpose(1, 0, 2).reshape(H, HEADS * DH) for n in "qkv"], 1)
    arrays = {
        "patches": px.T, "w_tok": a["L0_tok_W"], "w_gru": gru.transpose(0, 1, 2, 4, 3),
        "w_fus": a["L0_attn_fusion_W"].T, "vecs": vecs, "w_gate": a["L0_ffn_gate_w"].T,
        "w_up": a["L0_ffn_gate_up_proj"].transpose(0, 2, 1), "w_down": a["L0_ffn_down_proj"].transpose(0, 2, 1),
        "w_qkv": qkv, "w_gates": a["L1_attn_w_gates"][:, [0, 2, 4, 6, 1, 3, 5, 7]], "w_o": a["L1_attn_wo"].reshape(HEADS * DH, H),
        "w_1": a["L1_ffn_w1"].T, "w_2": a["L1_ffn_w2"].T,
    }
    arrays = {k: c(v) for k, v in arrays.items()}
    nc = bacc.Bacc("TRN2", target_bir_lowering=False, num_devices=1)
    args = [nc.dram_tensor(k, v.shape, mybir.dt.from_np(v.dtype), kind="ExternalInput").ap() for k, v in arrays.items()]
    out = nc.dram_tensor("tower_out", (T, H), F32, kind="ExternalOutput").ap()
    tower(nc, *args, out)
    r = run_bass_kernel_spmd(nc, [arrays], core_ids=[0])
    return r.results[0]["tower_out"].reshape(B, S, H)
```

```python
from contextlib import ExitStack

import concourse.bass as bass
from concourse import mybir

F32 = mybir.dt.float32
F32R = mybir.dt.float32r
ALU = mybir.AluOpType
ACT = mybir.ActivationFunctionType
AX_X = mybir.AxisListType.X

P = 128
B, S = 16, 36
T = B * S
H = 256
KH = H // P
NT = T // 2
TT = 96
JT = NT // TT
FLAT = 768
KF = FLAT // P
L = 4
UNITS = 4
STEPS = L * UNITS
E = 8
I = 1024
KI = I // P
HEADS, DH = 8, 64
AT = 2 * S
NAT = T // AT
EPS = 1e-5
RMS_EPS = 1.1920928955078125e-07
MASKED = -1e30
C = 192
CT = C // TT
PASSES = T // C
NP = E // 2

V_BZ, V_BH, V_GAM, V_BET, V_FB, V_RMS = 0, 16, 32, 34, 36, 38
V_L1G, V_L1B, V_B1, V_GB2, V_B2, V_N = 40, 42, 44, 52, 68, 70

LN_IN = 0
LN_GRU = 2
LN_MOE = 18
LN_ATT = 20
LN_MLP = 22
LN_OUT = 24
LN_ALL = 24


def tower(nc, patches, w_tok, w_gru, w_fus, vecs, w_gate, w_up, w_down, w_qkv, w_gates, w_o, w_1, w_2, out):
    with ExitStack() as ctx:
        def sb(name, shape, dt=F32):
            return ctx.enter_context(nc.sbuf_tensor(name, shape, dt))

        def sem(name):
            return ctx.enter_context(nc.semaphore(name))

        bank = ctx.enter_context(nc.psum_tensor("bank", [P, 8, 512], F32))

        xp = sb("xp", [P, KF, T])
        wt = sb("wt", [P, KF, H])
        wg = sb("wg", [P, L, 2, 2, KH, H])
        wf = sb("wf", [P, 4, H])
        vec = sb("vec", [P, V_N])
        wr = sb("wr", [P, KH, E])
        wqkv = xp[:].rearrange("p k t -> p (k t)")[:, 0:KH * 3 * HEADS * DH].rearrange("p (k n) -> p k n", k=KH)
        wga = sb("wga", [P, KH, HEADS])
        wo = wt[:, 0:4, :]
        wup = [sb(f"wup{i}", [P, KH, 2 * I]) for i in range(2)]
        wdn2 = sb("wdn2", [P, 2, KI, H])
        wdn = [wdn2[:, i] for i in range(2)]
        ident = sb("ident", [P, P])
        ones = sb("ones", [P, P])
        identr = sb("identr", [TT, TT], F32R)
        cmask4 = sb("cmask4", [AT, 4 * AT], mybir.dt.bfloat16)
        identb = sb("identb", [AT, AT], mybir.dt.bfloat16)
        mean_h = sb("mean_h", [P, 1])
        mean_i = sb("mean_i", [P, 1])
        half_neg = sb("half_neg", [P, JT])
        nbz = sb("nbz", [P, 16])
        cmask = sb("cmask", [AT, AT])
        ranks = sb("ranks", [P, E])
        h = sb("h", [P, KH, T])
        xn = sb("xn", [P, KH, T])
        zz = [sb(f"zz{i}", [P, KH, NT]) for i in range(2)]
        aa = [sb(f"aa{i}", [P, KH, NT]) for i in range(2)]
        tt = [sb(f"tt{i}", [P, KH, NT]) for i in range(2)]
        gru_y = sb("gru_y", [P, UNITS, KH, NT])
        gru_x = sb("gru_x", [P, UNITS, KH, NT])
        yy = [gru_y[:, i] for i in range(UNITS)]
        xx = [gru_x[:, i] for i in range(UNITS)]
        sq = [sb(f"sq{i}", [P, KH, NT]) for i in range(2)]
        stat = [sb(f"stat{i}", [TT, 6]) for i in range(2)]
        msq = [sb(f"msq{i}", [TT, 3]) for i in range(2)]
        var = [sb(f"var{i}", [TT, 3]) for i in range(2)]
        ve = [sb(f"ve{i}", [TT, 3]) for i in range(2)]
        rm = [sb(f"rm{i}", [TT, 6]) for i in range(2)]
        scratch = sb("scratch", [P, max(4 * C, T)])
        ysum = [scratch[:, i * NT:(i + 1) * NT] for i in range(2)]

        s_load = {n: sem("s_load_" + n) for n in
                  ("xp", "wt", "wg0", "wg1", "wg2", "wg3", "wf", "vec", "wr", "wqkv", "wga", "wo", "w1", "w2")}
        s_in = [sem(f"s_in{k}") for k in range(KF)]
        s_const = sem("s_const")
        s_vconst = sem("s_vconst")
        s_tok = sem("s_tok")
        s_h0 = sem("s_h0")
        s_sq = sem("s_sq")
        s_pre = sem("s_pre")
        s_st = sem("s_st")
        s_stc = sem("s_stc")
        s_ve = sem("s_ve")
        s_pow = sem("s_pow")
        s_rm = sem("s_rm")
        s_bc = sem("s_bc")
        s_norm = sem("s_norm")
        s_aff = sem("s_aff")
        s_zmm = sem("s_zmm"); s_hmm = sem("s_hmm")
        s_gz = sem("s_gz"); s_gt = sem("s_gt")
        s_clip = sem("s_clip"); s_edge = sem("s_edge")
        s_y = sem("s_y")
        s_fus = sem("s_fus"); s_hf = sem("s_hf")
        s_v = sem("s_v")

        chain = [0]

        def link(dve, ins):
            chain[0] += 1
            ins.then_inc(s_v, 1)
            dve.wait_ge(s_v, chain[0])

        def bias_column(s):
            l, _, d, _ = unit(s)
            return (l * 2 + d) * 2

        def both(x):
            return x[:].rearrange("p k t -> p (k t)")

        def unit(s):
            return s // UNITS, s % UNITS, s % 2, (s % UNITS) // 2

        def spread_place(i):
            apart = not LN_GRU <= i < LN_MOE and i < LN_OUT and i % 2 == 1
            return [bank[:, b, 0:NT] for b in ((2, 3) if apart else (5, 6))]

        def half(n):
            return slice(n * NT, (n + 1) * NT)

        def ln_source(i):
            if LN_GRU <= i < LN_MOE:
                return yy[(i - LN_GRU) % UNITS]
            return h[:, :, half(i % 2)]

        def ln_target(i):
            if LN_GRU <= i < LN_MOE:
                return yy[(i - LN_GRU) % UNITS]
            return xn[:, :, half(i % 2)]

        def affine_count(i):
            return max(0, min(i + 1, LN_MOE) - LN_GRU) + max(0, i + 1 - LN_ATT)

        wgf = wg[:].rearrange("p l d g k n -> p (l d g k n)")
        rkb = wgf[:, 0:E * T].rearrange("p (e t) -> p e t", t=T)
        act = [x[:].rearrange("p u k t -> p (u k t)")[:, 0:KI * C].rearrange("p (k t) -> p k t", t=C)
               for x in (gru_x, gru_y)]
        xg = [x[:].rearrange("p k t -> p (k t)")[:, 0:KH * C].rearrange("p (k t) -> p k t", t=C) for x in tt]
        mx1 = sb("mx1", [TT, 6, 1]); keys = sb("keys", [TT, 6, E]); pr = sb("pr", [TT, 6, E]); eq = sb("eq", [TT, 6, E])
        sel = sb("sel", [TT, 2, 6, E]); top = sb("top", [TT, 2, 6]); den = sb("den", [TT, 6]); comb = sb("comb", [TT, 6, E])
        msk = sb("msk", [TT, 6, E]); pre = sb("pre", [TT, 6, E]); rk = sb("rk", [TT, 6, E], F32R)
        combs = sb("combs", [TT, 6, E, 2], F32R)
        before = sb("before", [TT, TT])
        slot_row = sb("slot_row", [TT, T])
        slot_col = sb("slot_col", [TT, PASSES * CT])
        rmx = sb("rmx", [TT, 1]); rone = sb("rone", [1, 1]); flag = sb("flag", [1, 1], mybir.dt.int32)
        arena = sb("arena", [P, 8704], F32R)
        G = [arena[0:TT, i * 6 * C:(i + 1) * 6 * C].rearrange("p (j c) -> p j c", c=C) for i in range(2)]
        Sm = [arena[0:TT, 2304 + i * CT * T:2304 + (i + 1) * CT * T].rearrange("p (u t) -> p u t", t=T) for i in range(2)]
        xth = arena[0:TT, 4608:6144].rearrange("p (j n) -> p j n", n=H)
        xtl = arena[0:TT, 6144:7680].rearrange("p (j n) -> p j n", n=H)
        ywh = arena[0:TT, 7680:7680 + CT * H].rearrange("p (u n) -> p u n", n=H)
        ywl = arena[0:TT, 8192:8192 + CT * H].rearrange("p (u n) -> p u n", n=H)
        cur = [sb(f"cur{i}", [TT, 6, 2], F32R) for i in range(2)]
        wsl2 = [sb(f"wsl{i}", [TT, CT, 2]) for i in range(2)]; wsum = sb("wsum", [TT, CT])
        zero16 = sb("zero16", [P, NT], mybir.dt.bfloat16)
        sg, gt = [[scratch[:, (2 * c + i) * C:(2 * c + i + 1) * C] for i in range(2)] for c in range(2)]
        s_logit = sem("s_logit"); s_max = sem("s_max"); s_exp = sem("s_exp"); s_msk = sem("s_msk"); s_rank = sem("s_rank")
        s_rkp = sem("s_rkp"); s_rkt = sem("s_rkt"); s_xh = sem("s_xh")
        rkt = sb("rkt", [E, T], F32R)
        awake = sb("awake", [1, 1])
        TURN_BANKS = (0, 1, 2, 3, 5, 6)
        s_rmx = sem("s_rmx"); s_rmt = sem("s_rmt"); s_flag = sem("s_flag"); s_rk = sem("s_rk")
        s_rbp = sem("s_rbp"); s_rb = [sem(f"s_rb{n}") for n in range(2)]; s_xtp = sem("s_xtp"); s_xt = sem("s_xt"); s_add = sem("s_add")
        NAMES = ("g", "s", "gath", "xg", "gu", "sig", "act", "dmm", "yt", "yp", "yw", "scat")
        down_out = sb("down_out", [P, KH, C])
        ps = [{n: sem(f"s_{n}_{c}") for n in NAMES} for c in range(PASSES)]
        s_upw = [[sem(f"s_upw{c}{i}") for i in range(2)] for c in range(PASSES)]
        s_dnw = [[sem(f"s_dnw{c}{i}") for i in range(2)] for c in range(PASSES)]
        s_vact = [sem(f"s_vact{c}") for c in range(PASSES)]
        s_vy = [sem(f"s_vy{c}") for c in range(PASSES)]

        qt, kt = [x[:].rearrange("p u k t -> p (u k t)").rearrange("p (m t) -> p m t", t=T) for x in (gru_x, gru_y)]
        vt = wdn2[0:AT].rearrange("p i k n -> p (i k n)").rearrange("p (t n) -> p t n", t=NAT)
        ot = wgf[:, 4 * T:8 * T].rearrange("p (m t) -> p m t", t=T)
        gex = sb("gex", [AT, NAT, HEADS])
        sc, pt = [[x[0:AT].rearrange("p k t -> p (k t)").rearrange("p (e t) -> p e t", t=AT) for x in b]
                  for b in (zz + tt[:1], aa)]
        NSC = len(sc)
        rmax = [sb(f"rmax{i}", [AT, HEADS]) for i in range(2)]; rsum = sb("rsum", [AT, HEADS]); rden = sb("rden", [AT, HEADS])
        s_qk = sem("s_qk"); s_qkc = sem("s_qkc"); s_vg = sem("s_vg"); s_vgc = sem("s_vgc"); s_ge = sem("s_ge")
        s_sc = sem("s_sc"); s_sm = sem("s_sm"); s_scf = sem("s_scf"); s_ex = sem("s_ex"); s_pn = sem("s_pn")
        s_ptp = sem("s_ptp"); s_pt = sem("s_pt"); s_o = sem("s_o"); s_oc = sem("s_oc")
        s_wo = sem("s_wo"); s_ha = sem("s_ha")

        q1 = arena[:, 0:2048].rearrange("p (k n) -> p k n", k=KH)
        q2 = arena[:, 2048:4096].rearrange("p (k n) -> p k n", k=KI)
        w1 = wup[1][:, 0, :].rearrange("p (k n) -> p k n", k=KH)
        w2 = wup[1][:, 1, :].rearrange("p (k n) -> p k n", k=KI)
        qtmp = wup[0]
        asum = sb("asum", [P, 2]); ws = sb("ws", [P, 2]); wsi = sb("wsi", [P, 2])
        YB = 4
        xh, xl = [[arena[:, 4096 + (2 * n + c) * KH * NT:4096 + (2 * n + c + 1) * KH * NT]
                   .rearrange("p (k t) -> p k t", t=NT) for n in range(2)] for c in range(2)]
        yh, yl = [[arena[:, 6400 + (2 * b + c) * NT:6400 + (2 * b + c + 1) * NT] for b in range(YB)] for c in range(2)]
        gy = [wgf[:, n * KI * NT:(n + 1) * KI * NT].rearrange("p (k t) -> p k t", t=NT) for n in range(2)]
        gsq = [x[:].rearrange("p u k t -> p (u k) t") for x in (gru_x, gru_y)]
        vh = sb("vh", [P, KI, 2], F32R); vl = sb("vl", [P, KI, 2], F32R)
        gb = sb("gb", [P, KH, 2]); gbn = sb("gbn", [P, KH])
        s_gb = sem("s_gb"); s_mg = sem("s_mg")
        oc = wgf[0:TT, 8 * T:8 * T + 6 * H].rearrange("p (t n) -> p t n", n=H)
        s_acc = sem("s_acc")
        s_accy = sem("s_accy")
        s_abs = sem("s_abs"); s_absp = sem("s_absp"); s_q1 = sem("s_q1"); s_q2 = sem("s_q2")
        s_xs = sem("s_xs"); s_u = sem("s_u"); s_gel = sem("s_gel"); s_gsq = sem("s_gsq"); s_ys = sem("s_ys")
        s_w2 = sem("s_w2"); s_fin = sem("s_fin"); s_gbp = sem("s_gbp"); s_tr = sem("s_tr"); s_trc = sem("s_trc"); s_out = sem("s_out")

        block = ctx.enter_context(nc.Block())

        @block.sync
        def _(sp):
            for k in range(KF):
                sp.dma_start(wt[:, k, :], w_tok[k * P:(k + 1) * P, :]).then_inc(s_in[k], 16)
                sp.dma_start(xp[:, k, :], patches[k * P:(k + 1) * P, :]).then_inc(s_in[k], 16)
            sp.dma_start(vec[:], vecs).then_inc(s_load["vec"], 16)
            for l in range(L):
                sp.dma_start(wg[:, l], w_gru[l].rearrange("d g (k p) n -> p d g k n", p=P)).then_inc(s_load[f"wg{l}"], 16)
            sp.dma_start(wf[:], w_fus.rearrange("(k p) n -> p k n", p=P)).then_inc(s_load["wf"], 16)
            sp.dma_start(wr[:], w_gate.rearrange("(k p) n -> p k n", p=P)).then_inc(s_load["wr"], 16)
            def experts_load(c):
                for i in range(2):
                    sp.dma_start(wup[i][:], w_up[i].rearrange("(k p) n -> p k n", p=P)).then_inc(s_upw[c][i], 16)
                    sp.dma_start(wdn[i], w_down[i].rearrange("(k p) n -> p k n", p=P)).then_inc(s_dnw[c][i], 16)
                    if c == 0 and i == 0:
                        sp.wait_ge(s_tok, 4)
                        sp.dma_start(wqkv, w_qkv.rearrange("(k p) n -> p k n", p=P)).then_inc(s_load["wqkv"], 16)
                        sp.dma_start(wo, w_o.rearrange("(k p) n -> p k n", p=P)).then_inc(s_load["wo"], 16)
                        sp.dma_start(wga[:], w_gates.rearrange("(k p) n -> p k n", p=P)).then_inc(s_load["wga"], 16)
                with sp.Fori(1, NP) as pair:
                    for i in range(2):
                        sp.wait_ge(ps[c]["gu"], pair * 2 * KI + (i - 1) * KI)
                        sp.dma_start(wup[i][:], w_up[pair * 2 + i].rearrange("(k p) n -> p k n", p=P))\
                          .then_inc(s_upw[c][i], 16)
                        sp.wait_ge(ps[c]["dmm"], pair * 2 + (i - 1))
                        sp.dma_start(wdn[i], w_down[pair * 2 + i].rearrange("(k p) n -> p k n", p=P))\
                          .then_inc(s_dnw[c][i], 16)

            experts_load(0)
            sp.wait_ge(s_flag, 1)
            with sp.If(sp.value_load(flag[0:1, 0:1]) > 0):
                for c in range(1, PASSES):
                    sp.wait_ge(ps[c - 1]["scat"], E)
                    experts_load(c)
            sp.wait_ge(s_add, 2)
            sp.dma_start(w1, w_1.rearrange("(k p) n -> p k n", p=P)).then_inc(s_load["w1"], 16)
            sp.dma_start(w2, w_2.rearrange("(k p) n -> p k n", p=P)).then_inc(s_load["w2"], 16)
            for j in range(6):
                sp.wait_ge(s_trc, j + 1)
                sp.dma_start(out[j * TT:(j + 1) * TT, :], oc[:, j, :]).then_inc(s_out, 16)
            sp.wait_ge(s_out, 16 * 6)

        @block.gpsimd
        def _(pool):
            pool.memset(ident[:], 0.0).then_inc(s_const, 1)
            pool.memset(cmask[:], MASKED).then_inc(s_const, 1)
            pool.memset(half_neg[:], -0.5).then_inc(s_const, 1)
            pool.iota(ranks[:], pattern=[[-1, E]], base=E, channel_multiplier=0,
                      allow_small_or_imprecise_dtypes=True).then_inc(s_const, 1)
            pool.memset(before[:], 1.0).then_inc(s_const, 1)
            pool.iota(slot_row[:], pattern=[[1, T]], base=0, channel_multiplier=0,
                      allow_small_or_imprecise_dtypes=True).then_inc(s_const, 1)
            pool.iota(slot_col[:], pattern=[[TT, PASSES * CT]], base=0, channel_multiplier=1,
                      allow_small_or_imprecise_dtypes=True).then_inc(s_const, 1)
            pool.memset(zero16[:], 0.0).then_inc(s_const, 1)
            pool.wait_ge(s_const, 8)
            pool.affine_select(out=ident[:], in_=ident[:], compare_op=ALU.not_equal, fill=1.0, base=0,
                               pattern=[[-1, P]], channel_multiplier=1).then_inc(s_const, 1)
            pool.affine_select(out=cmask[:], in_=cmask[:], compare_op=ALU.is_gt, fill=0.0, base=0,
                               pattern=[[1, AT]], channel_multiplier=-1).then_inc(s_const, 1)
            pool.affine_select(out=before[:], in_=before[:], compare_op=ALU.is_gt, fill=0.0, base=0,
                               pattern=[[1, TT]], channel_multiplier=-1).then_inc(s_const, 1)
            pool.wait_ge(s_const, 11)
            pool.affine_select(out=cmask[:, 0:S], in_=cmask[:, 0:S], compare_op=ALU.is_gt, fill=MASKED, base=S,
                               pattern=[[0, S]], channel_multiplier=-1).then_inc(s_const, 1)

            def power(i):
                pool.wait_ge(s_ve, i + 1)
                if i >= 2:
                    pool.wait_ge(s_bc, i - 1)
                pool.tensor_tensor(rm[i % 2][:, 0:3], ve[i % 2][:], half_neg[0:TT, :], ALU.pow).then_inc(s_pow, 1)

            def add_input(i, ready):
                pool.wait_ge(*ready)
                if i >= 2:
                    pool.wait_ge(s_st, i - 1)
                y = ln_source(i)
                pool.tensor_tensor(ysum[i % 2], y[:, 0, :], y[:, 1, :], ALU.add).then_inc(s_pre, 1)

            def add_squares(i):
                pool.wait_ge(s_sq, i + 1)
                pool.tensor_tensor(sq[i % 2][:, 0, :], sq[i % 2][:, 0, :], sq[i % 2][:, 1, :], ALU.add).then_inc(s_pre, 1)

            def pair(i, ready, step=1):
                for n in range(2):
                    add_input(i + n, (ready, (n + 1) * step))
                    add_squares(i + n)
                for n in range(2):
                    power(i + n)

            pair(LN_IN, s_h0, 2)
            for s in range(STEPS + 2):
                if s >= 2:
                    power(LN_GRU + s - 2)
                if 1 <= s <= STEPS:
                    add_input(LN_GRU + s - 1, (s_y, s))
                if s < STEPS:
                    d, y = s % 2, aa[s % 2]
                    first = 0 if d == 0 else S - 1
                    pool.wait_ge(s_clip, s + 1)
                    pool.memset(both(y)[:, first::S], 0.0).then_inc(s_edge, 1)
                if 1 <= s <= STEPS:
                    add_squares(LN_GRU + s - 1)
            pair(LN_MOE, s_hf)
            pair(LN_ATT, s_add)
            for n in range(2):
                add_input(LN_MLP + n, (s_ha, n + 1))
                add_squares(LN_MLP + n)
                power(LN_MLP + n)
            for n in range(2):
                i = LN_OUT + n
                pool.wait_ge(s_st, i - 1)
                to = sq[i % 2][:, 0, :]
                for m in range(1, KI):
                    pool.wait_ge(s_gsq, n * KI + m + 1)
                    if m > 1:
                        pool.wait_ge(s_acc, n * (KI - 1) + m - 1)
                    pool.tensor_tensor(to, gsq[n][:, 0, :] if m == 1 else to, gsq[n][:, m, :], ALU.add)\
                        .then_inc(s_acc, 1)
                power(i)

        @block.tensor
        def _(pe):
            def ln_sums(i, mean=mean_h):
                if mean is mean_h:
                    pe.wait_ge(s_pre, 2 * (i + 1))
                if i >= 1:
                    pe.wait_ge(s_stc, i)
                for c, src in enumerate((ysum[i % 2], sq[i % 2][:, 0, :])):
                    for j in range(JT):
                        last = pe.matmul(bank[0:TT, 4, c * JT + j:c * JT + j + 1], src[:, j * TT:(j + 1) * TT], mean[:],
                                         start=True, stop=True)
                last.then_inc(s_st, 1)

            def stay_warm(count, b=7, rows=P):
                for _ in range(count):
                    pe.matmul(bank[0:rows, b, 0:NT], zero16[:, 0:rows], zero16[:], start=True, stop=True)

            def ln_spread(i):
                pe.wait_ge(s_rm, i + 1)
                if i >= 2:
                    pe.wait_ge(s_norm, i if LN_GRU < i < LN_MOE or i > LN_OUT else i - 1)
                place = spread_place(i)
                for c in range(2):
                    for j in range(JT):
                        last = pe.matmul(place[c][:, j * TT:(j + 1) * TT],
                                         rm[i % 2][:, c * JT + j:c * JT + j + 1].broadcast_to([TT, P]),
                                         ident[0:TT, 0:TT], start=True, stop=True)
                last.then_inc(s_bc, 1)

            def ln_pair(i):
                stay_warm(10)
                ln_sums(i)
                stay_warm(9)
                ln_sums(i + 1)
                stay_warm(6)
                ln_spread(i)
                ln_spread(i + 1)
                stay_warm(10)

            for k in range(KF):
                pe.wait_ge(s_in[k], 32)
                for n in range(2):
                    for m in range(KH):
                        last = pe.matmul(bank[:, 2 * n + m, 0:NT], wt[:, k, m * P:(m + 1) * P],
                                         xp[:, k, half(n)], start=(k == 0), stop=(k == KF - 1))
                        if k == KF - 1:
                            last.then_inc(s_tok, 1)
            pe.wait_ge(s_const, 12)
            pe.wait_ge(s_vconst, 6)
            ln_pair(LN_IN)

            def fuse(n):
                pe.wait_ge((s_gz, s_gt)[n], STEPS)
                for k in range(4):
                    if n == 1 and k == 2:
                        stay_warm(14)
                    if k % 2 == 0:
                        pe.wait_ge(s_aff, STEPS - UNITS + 2 * n + k // 2 + 1)
                    for m in range(KH):
                        last = pe.matmul(bank[:, 2 * n + m, 0:NT], wf[:, k, m * P:(m + 1) * P],
                                         xx[2 * n + k // 2][:, k % 2, :], start=(k == 0), stop=(k == 3))
                last.then_inc(s_fus, 1)

            def products(s, g):
                l, u, d, n = unit(s)
                if g == 0:
                    if l == 0:
                        pe.wait_ge(s_norm, n + 1)
                    else:
                        pe.wait_ge(s_aff, s - UNITS + 1)
                    if u == 0:
                        pe.wait_ge(s_load[f"wg{l}"], 16)
                if s == 0 and g == 1:
                    pe.wait_ge(s_norm, 2)
                if s >= 1:
                    pe.wait_ge((s_gz, s_gt)[g], s)
                for m in range(KH):
                    for k in range(KH):
                        src = xn[:, k, half(n)] if l == 0 else xx[u][:, k, :]
                        last = pe.matmul(bank[:, 2 * g + m, 0:NT], wg[:, l, d, g, k, m * P:(m + 1) * P], src,
                                         start=(k == 0), stop=(k == KH - 1))
                last.then_inc((s_zmm, s_hmm)[g], 1)

            for s in range(STEPS + 2):
                if s < STEPS:
                    products(s, 0)
                if s == STEPS + 1:
                    stay_warm(9)
                if s >= 2:
                    ln_sums(LN_GRU + s - 2)
                if s < STEPS:
                    products(s, 1)
                if s == STEPS:
                    stay_warm(25)
                if s == STEPS + 1:
                    pe.wait_ge(s_load["wf"], 16)
                    fuse(0)
                if s >= 2:
                    ln_spread(LN_GRU + s - 2)
            fuse(1)
            ln_pair(LN_MOE)
            pe.wait_ge(s_load["wr"], 16)
            for j in range(6):
                pe.wait_ge(s_norm, LN_MOE + j // JT + 1)
                for k in range(KH):
                    last = pe.matmul(bank[0:TT, 7, j * E:(j + 1) * E], xn[:, k, j * TT:(j + 1) * TT], wr[:, k, :],
                                     start=(k == 0), stop=(k == KH - 1))
            last.then_inc(s_logit, 1)
            for j in range(6):
                for m in range(KH):
                    last = pe.transpose(bank[0:TT, TURN_BANKS[j], m * P:(m + 1) * P], xn[:, m, j * TT:(j + 1) * TT],
                                        ident[:])
                last.then_inc(s_xtp, 1)
            pe.wait_ge(s_stc, LN_MOE + 2)
            stay_warm(26, 4)
            pe.wait_ge(s_msk, 1)
            flat = lambda x: x[:].rearrange("p j e -> p (j e)")
            pe.matmul(bank[0:TT, 7, 0:6 * E], before[:], flat(msk), start=True, stop=False)
            pe.matmul(bank[0:TT, 7, 0:6 * E], ones[0:TT, 0:TT], flat(pre), start=False, stop=True).then_inc(s_rank, 1)
            stay_warm(22, 4)
            pe.wait_ge(s_xt, 6)
            pe.wait_ge(s_rk, 1)
            for j in range(6):
                last = pe.matmul(bank[0:E, j // JT, j % JT * TT:(j % JT + 1) * TT], rk[:, j, :], identr[:],
                                 start=True, stop=True)
            last.then_inc(s_rkp, 1)
            pe.wait_ge(s_rmx, 1)
            pe.transpose(bank[0:1, 7, 0:TT], rmx[:], ident[0:TT, 0:TT]).then_inc(s_rmt, 1)
            stay_warm(9, 4)

            def rank_rows():
                stay_warm(4, 4)
                pe.wait_ge(s_rkt, 1)
                for q in range(2 * E):
                    e, n = q // 2, q % 2
                    if q >= 4:
                        stay_warm(1, 4)
                        pe.wait_ge(s_rb[n], q // 2 - 1)
                    pe.matmul(bank[:, q % 4, 0:NT], identr[0:E, e:e + 1].broadcast_to([E, P]), rkt[:, half(n)],
                              start=True, stop=True).then_inc(s_rbp, 1)

            def clear_output():
                for n in range(2):
                    pe.wait_ge(s_rb[n], E)
                for b in range(4):
                    pe.matmul(bank[:, b, 0:NT], zero16[:, 0:P], zero16[:], start=True, stop=False, skip_group_check=True)

            def gather(c, x, i):
                pe.wait_ge(ps[c]["g"], x + 1)
                if i != 0 or not isinstance(x, int) or x > 0:
                    pe.wait_ge(ps[c]["xg"], x)
                for m in range(KH):
                    for part in (xth, xtl):
                        for j in range(6):
                            pe.matmul(bank[:, 6, m * C:(m + 1) * C], part[:, j, m * P:(m + 1) * P], G[i][:, j, :],
                                      start=(part is xth and j == 0), stop=(part is xtl and j == 5))
                for u in range(CT):
                    for j in range(6):
                        last = pe.matmul(bank[0:TT, 6, KH * C + 2 * u:KH * C + 2 * u + 2], G[i][:, j, u * TT:(u + 1) * TT],
                                         cur[i][:, j, :], start=(j == 0), stop=(j == 5))
                last.then_inc(ps[c]["gath"], 1)

            def turn_down(c, x):
                pe.wait_ge(ps[c]["yt"], x + 1)
                for u in range(CT):
                    for m in range(KH):
                        last = pe.transpose(bank[0:TT, 7, u * H + m * P:u * H + (m + 1) * P],
                                            down_out[:, m, u * TT:(u + 1) * TT], ident[:])
                last.then_inc(ps[c]["yp"], 1)

            def up(c, x, i, before=None):
                pe.wait_ge(s_upw[c][i], (x - i) * 8 + 16)
                pe.wait_ge(ps[c]["xg"], x + 1)
                for m in range(KI):
                    if m >= 2 or not (isinstance(x, int) and x == 0):
                        pe.wait_ge(ps[c]["act"], x * KI + m - 1)
                    for g in range(2):
                        for k in range(KH):
                            last = pe.matmul(bank[:, 4 + m % 2, g * 256:g * 256 + C],
                                             wup[i][:, k, g * I + m * P:g * I + (m + 1) * P], xg[i][:, k, :],
                                             start=(k == 0), stop=(k == KH - 1))
                    last.then_inc(ps[c]["gu"], 1)
                    if m == 0 and before is not None:
                        turn_down(c, before)

            def down(c, x, i):
                pe.wait_ge(s_dnw[c][i], (x - i) * 8 + 16)
                pe.wait_ge(ps[c]["act"], (x + 1) * KI)
                if not (isinstance(x, int) and x == 0):
                    pe.wait_ge(ps[c]["yw"], x)
                for m in range(KH):
                    for k in range(KI):
                        last = pe.matmul(bank[:, 7, m * C:(m + 1) * C], wdn[i][:, k, m * P:(m + 1) * P],
                                         act[i][:, k, :], start=(k == 0), stop=(k == KI - 1))
                last.then_inc(ps[c]["dmm"], 1)

            def scatter(c, x, i):
                pe.wait_ge(ps[c]["yw"], x + 1)
                pe.wait_ge(ps[c]["s"], x + 1)
                for m in range(KH):
                    for n in range(2):
                        for u in range(CT):
                            for part in (ywh, ywl):
                                last = pe.matmul(bank[:, 2 * m + n, 0:NT], part[:, u, m * P:(m + 1) * P],
                                                 Sm[i][:, u, half(n)], start=False, stop=False, skip_group_check=True)
                last.then_inc(ps[c]["scat"], 1)

            def experts(c):
                gather(c, 0, 0)
                if c == 0:
                    rank_rows()
                up(c, 0, 0)
                if c == 0:
                    clear_output()
                with pe.Fori(0, NP - 1) as pair:
                    x = pair * 2
                    gather(c, x + 1, 1)
                    down(c, x, 0)
                    up(c, x + 1, 1, x)
                    scatter(c, x, 0)
                    gather(c, x + 2, 0)
                    down(c, x + 1, 1)
                    up(c, x + 2, 0, x + 1)
                    scatter(c, x + 1, 1)
                gather(c, E - 1, 1)
                down(c, E - 2, 0)
                up(c, E - 1, 1, E - 2)
                scatter(c, E - 2, 0)
                down(c, E - 1, 1)
                stay_warm(5, 4)
                turn_down(c, E - 1)
                stay_warm(14, 4)
                scatter(c, E - 1, 1)

            experts(0)
            pe.wait_ge(s_flag, 1)
            with pe.If(pe.value_load(flag[0:1, 0:1]) > 0):
                for c in range(1, PASSES):
                    experts(c)

            stay_warm(18)
            pe.wait_ge(s_add, 2)
            ln_pair(LN_ATT)
            pe.wait_ge(s_load["wqkv"], 16)
            pe.wait_ge(s_load["wga"], 16)
            for q in range(16):
                n, c, m = q // 8, q % 8 // 4, q % 4
                if q % 8 == 0:
                    pe.wait_ge(s_aff, affine_count(LN_ATT + n))
                if q == 2:
                    pe.wait_ge(s_norm, LN_ATT + 2)
                if q >= 4:
                    pe.wait_ge(s_qkc, q - 3)
                for k in range(KH):
                    last = pe.matmul(bank[:, q % 4, 0:NT], wqkv[:, k, c * 512 + m * P:c * 512 + (m + 1) * P],
                                     xn[:, k, half(n)], start=(k == 0), stop=(k == KH - 1))
                last.then_inc(s_qk, 1)
            pe.wait_ge(s_qkc, 16)
            pe.wait_ge(s_abs, 2)
            pe.matmul(bank[:, 7, 0:2], ones[:], asum[:], start=True, stop=True).then_inc(s_absp, 1)
            for t in range(NAT):
                if t >= 2:
                    pe.wait_ge(s_vgc, t - 1)
                for k in range(KH):
                    pe.matmul(bank[0:AT, 2 * (t % 2), :], xn[:, k, t * AT:(t + 1) * AT], wqkv[:, k, 1024:1536],
                              start=(k == 0), stop=(k == KH - 1))
                for k in range(KH):
                    last = pe.matmul(bank[0:AT, 2 * (t % 2) + 1, 0:HEADS], xn[:, k, t * AT:(t + 1) * AT], wga[:, k, :],
                                     start=(k == 0), stop=(k == KH - 1))
                last.then_inc(s_vg, 1)
            pe.wait_ge(s_vgc, NAT)
            pe.wait_ge(s_ge, NAT)

            def scores(t):
                b = (0, 5)[t % 2]
                if t >= 2:
                    pe.wait_ge(s_scf, t - 1)
                    stay_warm(7, b, AT)
                for o in range(2):
                    pe.matmul(bank[0:AT, b + o, 0:4 * AT], identb[:], cmask4[:], start=True, stop=False,
                              skip_group_check=True)
                for e in range(HEADS):
                    r = slice(64 * (e % 2), 64 * (e % 2) + 64)
                    last = pe.matmul(bank[0:AT, b + e % 2, (e // 2) * AT:(e // 2 + 1) * AT],
                                     qt[r, e // 2, t * AT:(t + 1) * AT], kt[r, e // 2, t * AT:(t + 1) * AT],
                                     start=False, stop=True, skip_group_check=True)
                last.then_inc(s_sc, 1)

            def turn(t):
                pe.wait_ge(s_pn, t + 1)
                if t >= 1:
                    pe.wait_ge(s_pt, t)
                for e in range(HEADS):
                    last = pe.transpose(bank[0:AT, 2 + e // 4, (e % 4) * AT:(e % 4 + 1) * AT],
                                        sc[t % NSC][:, e, :], ident[0:AT, 0:AT])
                last.then_inc(s_ptp, 1)

            def values(t):
                pe.wait_ge(s_pt, t + 1)
                if t >= 2:
                    pe.wait_ge(s_oc, t - 1)
                if t == 1:
                    pe.wait_ge(s_gb, 1)
                for e in range(HEADS):
                    r = slice(64 * (e % 2), 64 * (e % 2) + 64)
                    last = pe.matmul(bank[r, (4, 7)[t % 2], (e // 2) * AT:(e // 2 + 1) * AT],
                                     vt[:, t, e * DH:(e + 1) * DH], pt[t % 2][:, (e % 2) * 4 + e // 2, :],
                                     start=True, stop=True)
                last.then_inc(s_o, 1)

            def project(n):
                pe.wait_ge(s_load["wo"], 16)
                pe.wait_ge(s_oc, (n + 1) * NAT // 2)
                for m in range(KH):
                    for k in range(4):
                        last = pe.matmul(bank[:, 2 * n + m, 0:NT], wo[:, k, m * P:(m + 1) * P],
                                         ot[:, k, half(n)], start=(k == 0), stop=(k == 3))
                last.then_inc(s_wo, 1)

            scores(0)
            scores(1)
            pe.wait_ge(s_q2, 1)
            for m in range(KH):
                for k in range(KI):
                    stay_warm(1, 2)
                    for part in (vh, vl):
                        last = pe.matmul(bank[:, 7, 2 * m:2 * m + 2], q2[:, k, m * P:(m + 1) * P], part[:, k, :],
                                         start=(k == 0 and part is vh), stop=(k == KI - 1 and part is vl))
            last.then_inc(s_gbp, 1)
            stay_warm(10, 2)
            for t in range(NAT):
                if t + 2 < NAT:
                    scores(t + 2)
                else:
                    pe.wait_ge(s_scf, t + 1)
                    stay_warm(7, (0, 5)[t % 2], AT)
                if t >= 1:
                    values(t - 1)
                turn(t)
                if t == NAT - 2:
                    project(0)
            stay_warm(6, 5)
            values(NAT - 1)
            pe.wait_ge(s_oc, NAT - 1)
            ln_sums(LN_MLP)
            project(1)

            ln_spread(LN_MLP)
            stay_warm(7)
            ln_sums(LN_MLP + 1)
            stay_warm(14)
            ln_spread(LN_MLP + 1)
            pe.wait_ge(s_stc, LN_MLP + 2)
            stay_warm(10, 4)

            def hidden(q):
                n, m = q // KI, q % KI
                if m == 0:
                    pe.wait_ge(s_xs, n + 1)
                if q >= 2:
                    pe.wait_ge(s_gel, q - 1)
                for k in range(KH):
                    for part in (xh[n], xl[n]):
                        last = pe.matmul(bank[:, m % 2, 0:NT], q1[:, k, m * P:(m + 1) * P], part[:, k, :],
                                         start=(k == 0 and part is xh[n]), stop=(k == KH - 1 and part is xl[n]))
                last.then_inc(s_u, 1)

            def outward(q):
                n, k = q // KI, q % KI
                pe.wait_ge(s_ys, q + 1)
                if q == 0:
                    pe.wait_ge(s_norm, LN_MLP + 2)
                if q == KI:
                    stay_warm(10)
                    pe.wait_ge(s_norm, LN_OUT + 1)
                yh_, yl_ = yh[q % YB], yl[q % YB]
                for m in range(KH):
                    for part in (yh_, yl_):
                        last = pe.matmul(bank[:, 2 + m, 0:NT], q2[:, k, m * P:(m + 1) * P], part,
                                         start=(k == 0 and part is yh_), stop=(k == KI - 1 and part is yl_))
                last.then_inc(s_w2, 1)

            def close(n):
                stay_warm(10)
                pe.wait_ge(s_acc, (n + 1) * (KI - 1))
                pe.wait_ge(s_accy, (n + 1) * (KI - 1))
                ln_sums(LN_OUT + n, mean_i)

            for q in range(2 * KI):
                hidden(q)
                if 2 <= q < KI + 2:
                    outward(q - 2)
                if q == KI + 1:
                    close(0)
                    stay_warm(14)
                    ln_spread(LN_OUT)
                if q >= KI + 4:
                    outward(q - 4)
            close(1)
            for q in range(2 * KI - 4, 2 * KI):
                outward(q)
            ln_spread(LN_OUT + 1)
            stay_warm(14)
            for n in range(2):
                pe.wait_ge(s_fin, n + 1)
                for j in range(JT):
                    t = n * JT + j
                    if t >= 2:
                        pe.wait_ge(s_trc, t - 1)
                    for m in range(KH):
                        last = pe.transpose(bank[0:TT, t % 2, m * P:(m + 1) * P],
                                            h[:, m, t * TT:(t + 1) * TT], ident[:])
                    last.then_inc(s_tr, 1)

        @block.scalar
        def _(sc_):
            def squares(i, ready):
                sc_.wait_ge(*ready)
                if i >= 2:
                    sc_.wait_ge(s_st, i - 1)
                sc_.activation(sq[i % 2][:], ln_source(i), ACT.Square).then_inc(s_sq, 1)

            def affine(i, gain, shift):
                sc_.wait_ge(s_norm, i + 1)
                for m in range(KH):
                    if LN_GRU <= i < LN_MOE:
                        src, dst = yy[(i - LN_GRU) % UNITS][:, m, :], xx[(i - LN_GRU) % UNITS][:, m, :]
                    else:
                        src = dst = xn[:, m, half(i % 2)]
                    last = sc_.activation(dst, src, ACT.Identity, scale=vec[:, gain + m:gain + m + 1],
                                          bias=vec[:, shift + m:shift + m + 1] if shift is not None else 0.0)
                last.then_inc(s_aff, 1)

            sc_.wait_ge(s_vconst, 2)
            sc_.activation(awake[:], mean_h[0:1, :], ACT.Sigmoid)
            for i in range(2):
                squares(i, (s_h0, 2 * i + 2))
            sc_.wait_ge(s_load["vec"], 16)
            sc_.wait_ge(s_vconst, 5)
            for s in range(STEPS + 3):
                if 1 <= s <= STEPS:
                    c = bias_column(s - 1)
                    sc_.wait_ge(s_hmm, s)
                    for m in range(KH):
                        last = sc_.activation(tt[(s - 1) % 2][:, m, :], bank[:, 2 + m, 0:NT], ACT.Tanh,
                                              bias=vec[:, V_BH + c + m:V_BH + c + m + 1])
                    last.then_inc(s_gt, 1)
                if s >= 3:
                    affine(LN_GRU + s - 3, V_GAM, V_BET)
                if s < STEPS:
                    c = bias_column(s)
                    if s >= 2:
                        sc_.wait_ge(s_y, s - 1)
                    sc_.wait_ge(s_zmm, s + 1)
                    for m in range(KH):
                        sc_.activation(aa[s % 2][:, m, :], bank[:, m, 0:NT], ACT.Sigmoid, scale=-1.0,
                                       bias=nbz[:, c + m:c + m + 1])
                        last = sc_.activation(zz[s % 2][:, m, :], bank[:, m, 0:NT], ACT.Sigmoid,
                                              bias=vec[:, V_BZ + c + m:V_BZ + c + m + 1])
                    last.then_inc(s_gz, 1)
                if 1 <= s <= STEPS:
                    squares(LN_GRU + s - 1, (s_y, s))
            for n in range(2):
                squares(LN_MOE + n, (s_hf, n + 1))
            sc_.wait_ge(s_max, 2)
            sc_.activation(pr[:], pr[:], ACT.Exp).then_inc(s_exp, 1)
            sc_.activation(awake[:], mean_h[0:1, :], ACT.Sigmoid)
            for j in range(6):
                sc_.wait_ge(s_xtp, j + 1)
                sc_.activation(xth[:, j, :], bank[0:TT, TURN_BANKS[j], 0:H], ACT.Copy).then_inc(s_xh, 1)

            def rank_rows():
                for e in range(E):
                    sc_.wait_ge(s_rbp, 2 * e + 1)
                    sc_.activation(rkb[:, e, half(0)], bank[:, 2 * e % 4, 0:NT], ACT.Copy).then_inc(s_rb[0], 1)

            def gathered(c, x, i):
                sc_.wait_ge(ps[c]["gath"], x + 1)
                if not (isinstance(x, int) and x < 2):
                    sc_.wait_ge(ps[c]["gu"], (x - 1) * KI)
                    sc_.wait_ge(ps[c]["yw"], x - 1)
                sc_.activation(wsl2[i][:], bank[0:TT, 6, KH * C:KH * C + 2 * CT].rearrange("p (u c) -> p u c", c=2),
                               ACT.Copy)
                sc_.activation(xg[i], bank[:, 6, 0:KH * C].rearrange("p (k t) -> p k t", t=C), ACT.Copy)\
                   .then_inc(ps[c]["xg"], 1)

            def copy_down(c, x):
                sc_.wait_ge(ps[c]["dmm"], x + 1)
                sc_.activation(down_out[:], bank[:, 7, 0:KH * C].rearrange("p (k t) -> p k t", t=C), ACT.Copy)\
                   .then_inc(ps[c]["yt"], 1)

            def sigmoids(c, x, i):
                for m in range(KI):
                    sc_.wait_ge(ps[c]["gu"], x * KI + m + 1)
                    if m >= 2 or not (isinstance(x, int) and x == 0):
                        sc_.wait_ge(ps[c]["act"], x * KI + m - 1)
                    sc_.activation(sg[m % 2], bank[:, 4 + m % 2, 0:C], ACT.Sigmoid).then_inc(ps[c]["sig"], 1)

            def experts(c):
                gathered(c, 0, 0)
                if c == 0:
                    rank_rows()
                sigmoids(c, 0, 0)
                with sc_.Fori(0, NP - 1) as pair:
                    for i in (1, 0):
                        gathered(c, pair * 2 + 2 - i, i)
                        copy_down(c, pair * 2 + 1 - i)
                        sigmoids(c, pair * 2 + 2 - i, i)
                gathered(c, E - 1, 1)
                copy_down(c, E - 2)
                sigmoids(c, E - 1, 1)
                copy_down(c, E - 1)

            experts(0)
            sc_.wait_ge(s_flag, 1)
            with sc_.If(sc_.value_load(flag[0:1, 0:1]) > 0):
                for c in range(1, PASSES):
                    sc_.wait_ge(ps[c - 1]["scat"], E)
                    experts(c)
            for n in range(2):
                squares(LN_ATT + n, (s_add, n + 1))
            for n in range(2):
                affine(LN_ATT + n, V_RMS, None)
            sc_.wait_ge(s_load["w1"], 16)
            sc_.wait_ge(s_load["w2"], 16)
            sc_.activation(qtmp[:, 0, :], w1.rearrange("p k n -> p (k n)"), ACT.Abs,
                           accum_out=asum[:, 0:1]).then_inc(s_abs, 1)
            sc_.activation(qtmp[:, 1, :], w2.rearrange("p k n -> p (k n)"), ACT.Abs,
                           accum_out=asum[:, 1:2]).then_inc(s_abs, 1)
            for q in range(16):
                n, c, m = q // 8, q % 8 // 4, q % 4
                sc_.wait_ge(s_qk, q + 1)
                sc_.activation((qt, kt)[c][:, m, half(n)], bank[:, q % 4, 0:NT], ACT.Copy,
                               scale=DH ** -0.5 if c == 0 else 1.0).then_inc(s_qkc, 1)
            for t in range(NAT):
                sc_.wait_ge(s_vg, t + 1)
                sc_.activation(gex[:, t, :], bank[0:AT, 2 * (t % 2) + 1, 0:HEADS], ACT.Exp, scale=-1.0).then_inc(s_ge, 1)
                sc_.activation(vt[:, t, :], bank[0:AT, 2 * (t % 2), :], ACT.Copy).then_inc(s_vgc, 1)
            def keep_out(t):
                sc_.wait_ge(s_o, t + 1)
                sc_.activation(ot[:, :, t * AT:(t + 1) * AT],
                               bank[:, (4, 7)[t % 2], 0:4 * AT].rearrange("p (e t) -> p e t", e=4),
                               ACT.Copy).then_inc(s_oc, 1)

            for t in range(NAT + 1):
                if t < NAT:
                    sc_.wait_ge(s_scf, t + 1)
                    sc_.activation(sc[t % NSC][:], sc[t % NSC][:], ACT.Exp).then_inc(s_ex, 1)
                if t >= 1:
                    sc_.wait_ge(s_ptp, t)
                    if t >= 3:
                        sc_.wait_ge(s_o, t - 2)
                    sc_.activation(pt[(t - 1) % 2][:].rearrange("p (b e) t -> p b (e t)", b=2),
                                   bank[0:AT, 2:4, 0:4 * AT], ACT.Copy).then_inc(s_pt, 1)
                if t >= 2:
                    keep_out(t - 2)
            squares(LN_MLP, (s_ha, 1))
            keep_out(NAT - 1)
            squares(LN_MLP + 1, (s_ha, 2))
            sc_.activation(awake[:], mean_h[0:1, :], ACT.Gelu)
            for n in range(2):
                affine(LN_MLP + n, V_L1G, V_L1B)
            def mean_part(n):
                sc_.wait_ge(s_gb, 1)
                sc_.wait_ge(s_bc, LN_OUT + n + 1)
                for m in range(KH):
                    last = sc_.activation((zz, tt)[n][1][:, m, :], bank[:, 6, 0:NT], ACT.Identity, scale=gb[:, m, 0:1],
                                          bias=gbn[:, m:m + 1])
                last.then_inc(s_mg, 1)

            for n in range(2):
                for m in range(KI):
                    q = n * KI + m
                    if q == KI + 4:
                        mean_part(0)
                    sc_.wait_ge(s_u, q + 1)
                    sc_.activation(gy[n][:, m, :], bank[:, m % 2, 0:NT], ACT.Gelu, scale=wsi[:, 0:1],
                                   bias=vec[:, V_B1 + m:V_B1 + m + 1]).then_inc(s_gel, 1)
                    sc_.wait_ge(s_gel, q + 1)
                    sc_.activation(gsq[n][:, m, :], gy[n][:, m, :], ACT.Square).then_inc(s_gsq, 1)
            mean_part(1)
            for t in range(6):
                sc_.wait_ge(s_tr, t + 1)
                sc_.activation(oc[:, t, :], bank[0:TT, t % 2, 0:H], ACT.Copy).then_inc(s_trc, 1)

        @block.vector
        def _(dve):
            dve.memset(ones[:], 1.0).then_inc(s_vconst, 1)
            dve.memset(mean_h[:], 1.0 / H).then_inc(s_vconst, 1)
            dve.memset(mean_i[:], 1.0 / I).then_inc(s_vconst, 1)
            dve.memset(asum[:], 0.0).then_inc(s_vconst, 1)
            dve.wait_ge(s_load["vec"], 16)
            dve.tensor_scalar(nbz[:], vec[:, V_BZ:V_BZ + 16], -1.0, None, ALU.mult).then_inc(s_vconst, 1)

            def ln_var(i):
                e2 = {LN_ATT: RMS_EPS, LN_MLP: EPS}.get(i - i % 2)
                stat_, msq_, var_, ve_ = (x[i % 2] for x in (stat, msq, var, ve))
                dve.wait_ge(s_st, i + 1)
                dve.tensor_copy(stat_[:], bank[0:TT, 4, 0:6]).then_inc(s_stc, 1)
                dve.wait_ge(s_stc, i + 1)
                link(dve, dve.tensor_tensor(msq_[:], stat_[:, 0:3], stat_[:, 0:3], ALU.mult))
                link(dve, dve.tensor_tensor(var_[:], stat_[:, 3:6], msq_[:], ALU.subtract))
                if e2 is None:
                    dve.tensor_scalar(ve_[:], var_[:], 0.0, EPS, ALU.max, ALU.add).then_inc(s_ve, 1)
                else:
                    link(dve, dve.tensor_scalar(var_[:], var_[:], 0.0, 1.0 + e2, ALU.max, ALU.mult))
                    dve.tensor_scalar(ve_[:], var_[:], e2 * EPS, None, ALU.add).then_inc(s_ve, 1)

            def ln_root(i):
                x = rm[i % 2]
                dve.wait_ge(s_pow, i + 1)
                dve.tensor_tensor(x[:, 3:6], stat[i % 2][:, 0:3], x[:, 0:3], ALU.mult).then_inc(s_rm, 1)

            def ln_norm(i):
                dve.wait_ge(s_bc, i + 1)
                src, dst = ln_source(i), ln_target(i)
                root, shift = [x.rearrange("p (o t) -> p o t", o=1).broadcast_to([P, KH, NT]) for x in spread_place(i)]
                link(dve, dve.tensor_tensor(dst, src, root, ALU.mult))
                dve.tensor_tensor(dst, dst, shift, ALU.subtract).then_inc(s_norm, 1)

            def ln_pair(i):
                for n in range(2):
                    ln_var(i + n)
                for n in range(2):
                    ln_root(i + n)
                for n in range(2):
                    ln_norm(i + n)

            dve.wait_ge(s_const, 12)
            dve.tensor_copy(identr[:], ident[0:TT, 0:TT])
            dve.tensor_copy(identb[:], ident[0:AT, 0:AT])
            dve.tensor_copy(cmask4[:].rearrange("p (e t) -> p e t", e=4),
                            cmask[:].rearrange("p (o t) -> p o t", o=1).broadcast_to([AT, 4, AT])).then_inc(s_vconst, 1)

            for n in range(2):
                for m in range(KH):
                    dve.wait_ge(s_tok, 2 * n + m + 1)
                    dve.tensor_copy(h[:, m, half(n)], bank[:, 2 * n + m, 0:NT]).then_inc(s_h0, 1)
            ln_pair(LN_IN)

            for s in range(STEPS + 3):
                i = LN_GRU + s - 3
                if s >= 3:
                    dve.wait_ge(s_bc, i + 1)
                    scaled = dve.tensor_tensor(ln_target(i), ln_source(i),
                                               bank[:, 5:6, 0:NT].broadcast_to([P, KH, NT]), ALU.mult)
                    scaled.then_inc(s_v, 1)
                    chain[0] += 1
                    scaled = chain[0]
                if 1 <= s <= STEPS:
                    l, u, d, n = unit(s - 1)
                    z, a, t, y = zz[(s - 1) % 2], aa[(s - 1) % 2], tt[(s - 1) % 2], yy[u]
                    dve.wait_ge(s_gt, s)
                    dve.tensor_tensor(z[:], z[:], t[:], ALU.mult).then_inc(s_v, 1)
                    chain[0] += 1
                    taken = chain[0]
                if s >= 3:
                    dve.wait_ge(s_v, scaled)
                    dve.tensor_tensor(ln_target(i), ln_target(i), bank[:, 6:7, 0:NT].broadcast_to([P, KH, NT]),
                                      ALU.subtract).then_inc(s_norm, 1)
                if 1 <= s <= STEPS:
                    dve.wait_ge(s_v, taken)
                    dve.wait_ge(s_edge, s)
                    if s >= 5:
                        dve.wait_ge(s_aff, s - 4)
                    to = y if l == 0 else t
                    rev = slice(None) if d == 0 else slice(None, None, -1)
                    scan = dve.tensor_tensor_scan(both(to)[:, rev], both(a)[:, rev], both(z)[:, rev], 0.0,
                                                  ALU.mult, ALU.add)
                    if l == 0:
                        scan.then_inc(s_y, 1)
                    else:
                        scan.then_inc(s_v, 1)
                        chain[0] += 1
                        scan = chain[0]
                if 2 <= s < STEPS + 2:
                    ln_var(LN_GRU + s - 2)
                if 1 <= s <= STEPS and l > 0:
                    dve.wait_ge(s_v, scan)
                    dve.tensor_tensor(y[:], t[:], xx[u], ALU.add).then_inc(s_y, 1)
                if 2 <= s < STEPS + 2:
                    ln_root(LN_GRU + s - 2)
                if s < STEPS:
                    dve.wait_ge(s_gz, s + 1)
                    dve.tensor_scalar(aa[s % 2][:], aa[s % 2][:], 1e-8, 1.0, ALU.max, ALU.min).then_inc(s_clip, 1)

            for n in range(2):
                dve.wait_ge(s_fus, n + 1)
                for m in range(KH):
                    last = dve.scalar_tensor_tensor(out=h[:, m, half(n)], in0=bank[:, 2 * n + m, 0:NT],
                                                    scalar=vec[:, V_FB + m:V_FB + m + 1], in1=h[:, m, half(n)],
                                                    op0=ALU.add, op1=ALU.add)
                last.then_inc(s_hf, 1)
            ln_pair(LN_MOE)

            def over(x):
                return x.broadcast_to([TT, 6, E])
            lg = bank[0:TT, 7, 0:6 * E].rearrange("p (j e) -> p j e", e=E)
            dve.wait_ge(s_logit, 1)
            link(dve, dve.tensor_reduce(mx1[:], lg, AX_X, ALU.max))
            dve.tensor_tensor(pr[:], lg, over(mx1[:]), ALU.subtract).then_inc(s_max, 2)
            dve.wait_ge(s_exp, 1)
            link(dve, dve.tensor_reduce(mx1[:], pr[:], AX_X, ALU.add))
            link(dve, dve.reciprocal(mx1[:], mx1[:]))
            link(dve, dve.tensor_tensor(pr[:], pr[:], over(mx1[:]), ALU.mult))
            dve.wait_ge(s_const, 12)
            prefer = ranks[0:TT, :].rearrange("p (o e) -> p o e", o=1).broadcast_to([TT, 6, E])
            def rows_low(j):
                dve.wait_ge(s_xh, j + 1)
                dve.tensor_tensor(xtl[:, j, :], bank[0:TT, TURN_BANKS[j], 0:H], xth[:, j, :].bitcast(F32),
                                  ALU.subtract).then_inc(s_xt, 1)

            def beside(ins, j):
                chain[0] += 1
                ins.then_inc(s_v, 1)
                rows_low(j)
                dve.wait_ge(s_v, chain[0])

            for c in range(2):
                link(dve, dve.tensor_reduce(top[:, c, :], pr[:], AX_X, ALU.max))
                tc = top[:, c, :].rearrange("p (j o) -> p j o", o=1)
                link(dve, dve.tensor_tensor(eq[:], pr[:], over(tc), ALU.is_equal))
                link(dve, dve.tensor_tensor(keys[:], eq[:], prefer, ALU.mult))
                link(dve, dve.tensor_reduce(mx1[:], keys[:], AX_X, ALU.max))
                link(dve, dve.tensor_tensor(sel[:, c], keys[:], over(mx1[:]), ALU.is_equal))
                if c == 0:
                    link(dve, dve.scalar_tensor_tensor(out=pr[:], in0=sel[:, c], scalar=-2.0, in1=pr[:],
                                                       op0=ALU.mult, op1=ALU.add))
            link(dve, dve.tensor_tensor(msk[:], sel[:, 0], sel[:, 1], ALU.add))
            link(dve, dve.memset(pre[:, 0, :], 0.0))
            for j in range(1, 6):
                ins = dve.tensor_tensor(pre[:, j, :], pre[:, j - 1, :], msk[:, j - 1, :], ALU.add)
                link(dve, ins) if j < 5 else ins.then_inc(s_msk, 1)
            beside(dve.tensor_tensor(den[:], top[:, 0, :], top[:, 1, :], ALU.add), 0)
            dve.wait_ge(s_rank, 1)
            beside(dve.scalar_tensor_tensor(out=keys[:], in0=bank[0:TT, 7, 0:6 * E].rearrange("p (j e) -> p j e", e=E),
                                            scalar=1.0, in1=msk[:], op0=ALU.add, op1=ALU.mult), 1)
            dve.tensor_scalar(rk[:], keys[:], -1.0, None, ALU.add).then_inc(s_rk, 1)
            dve.tensor_reduce(rmx[:], keys[:].rearrange("p j e -> p (j e)"), AX_X, ALU.max).then_inc(s_rmx, 1)
            beside(dve.reciprocal(den[:], den[:]), 2)
            for c in range(2):
                beside(dve.tensor_tensor(top[:, c, :], top[:, c, :], den[:], ALU.mult), 3 + c)
                link(dve, dve.tensor_tensor(sel[:, c], sel[:, c],
                                            over(top[:, c, :].rearrange("p (j o) -> p j o", o=1)), ALU.mult))
            beside(dve.tensor_tensor(comb[:], sel[:, 0], sel[:, 1], ALU.add), 5)
            link(dve, dve.tensor_copy(combs[:, :, :, 0], comb[:]))
            link(dve, dve.tensor_tensor(combs[:, :, :, 1], comb[:], combs[:, :, :, 0].bitcast(F32), ALU.subtract))

            def rank_rows():
                dve.wait_ge(s_rkp, 1)
                dve.tensor_copy(rkt[:].rearrange("p (n t) -> p n t", n=2), bank[0:E, 0:2, 0:NT]).then_inc(s_rkt, 1)
                dve.wait_ge(s_rmt, 1)
                link(dve, dve.tensor_reduce(rone[:], bank[0:1, 7, 0:TT], AX_X, ALU.max))
                dve.tensor_scalar(flag[:], rone[:], float(C) + 0.5, None, ALU.is_gt).then_inc(s_flag, 1)
                for e in range(E):
                    dve.wait_ge(s_rbp, 2 * e + 2)
                    dve.tensor_copy(rkb[:, e, half(1)], bank[:, (2 * e + 1) % 4, 0:NT]).then_inc(s_rb[1], 1)
                dve.wait_ge(s_rb[0], E)

            dve.wait_ge(s_rk, 1)

            def matrix_g(c, x, i):
                if not (isinstance(x, int) and x < 2):
                    dve.wait_ge(ps[c]["gath"], x - 1)
                dve.tensor_copy(cur[i][:], combs[:, :, x, :].bitcast(F32))
                dve.tensor_tensor(G[i],
                                  slot_row[:, c * C:(c + 1) * C].rearrange("p (o s) -> p o s", o=1).broadcast_to([TT, 6, C]),
                                  rk[:, :, x].bitcast(F32).rearrange("p (j o) -> p j o", o=1).broadcast_to([TT, 6, C]),
                                  ALU.is_equal).then_inc(ps[c]["g"], 1)

            def matrix_s(c, x, i):
                if not (isinstance(x, int) and x < 2):
                    dve.wait_ge(ps[c]["scat"], x - 1)
                for u in range(CT):
                    last = dve.tensor_scalar(Sm[i][:, u, :], rkb[0:TT, x, :], slot_col[:, c * CT + u:c * CT + u + 1], None,
                                             ALU.is_equal)
                last.then_inc(ps[c]["s"], 1)

            def activate(c, x, i, chunks=range(KI)):
                if 0 in chunks and not (isinstance(x, int) and x < 2):
                    dve.wait_ge(ps[c]["dmm"], x - 1)
                for m in chunks:
                    dve.wait_ge(ps[c]["sig"], x * KI + m + 1)
                    dve.tensor_tensor(gt[m % 2], bank[:, 4 + m % 2, 0:C], sg[m % 2], ALU.mult).then_inc(s_vact[c], 1)
                    dve.wait_ge(s_vact[c], x * KI + m + 1)
                    dve.tensor_tensor(act[i][:, m, :], bank[:, 4 + m % 2, 256:256 + C], gt[m % 2],
                                      ALU.mult).then_inc(ps[c]["act"], 1)

            def outputs_high(c, x, i):
                dve.wait_ge(ps[c]["xg"], x + 1)
                dve.tensor_reduce(wsum[:], wsl2[i][:], AX_X, ALU.add).then_inc(s_vy[c], 1)
                dve.wait_ge(s_vy[c], x * (1 + CT) + 1)
                dve.wait_ge(ps[c]["yp"], x + 1)
                if not (isinstance(x, int) and x == 0):
                    dve.wait_ge(ps[c]["scat"], x)
                for u in range(CT):
                    dve.tensor_scalar(ywh[:, u, :], bank[0:TT, 7, u * H:(u + 1) * H], wsum[:, u:u + 1], None,
                                      ALU.mult).then_inc(s_vy[c], 1)

            def outputs_low(c, x):
                for u in range(CT):
                    dve.wait_ge(s_vy[c], x * (1 + CT) + 2 + u)
                    last = dve.scalar_tensor_tensor(out=ywl[:, u, :], in0=bank[0:TT, 7, u * H:(u + 1) * H],
                                                    scalar=wsum[:, u:u + 1], in1=ywh[:, u, :].bitcast(F32),
                                                    op0=ALU.mult, op1=ALU.subtract)
                last.then_inc(ps[c]["yw"], 1)

            def experts(c):
                matrix_g(c, 0, 0)
                if c == 0:
                    rank_rows()
                matrix_g(c, 1, 1)
                matrix_s(c, 0, 0)
                activate(c, 0, 0)
                with dve.Fori(0, NP - 1) as pair:
                    x = pair * 2
                    for i in range(2):
                        matrix_g(c, x + 2 + i, i)
                        matrix_s(c, x + 1 + i, 1 - i)
                        activate(c, x + 1 + i, 1 - i, range(1))
                        outputs_high(c, x + i, i)
                        activate(c, x + 1 + i, 1 - i, range(1, 2))
                        outputs_low(c, x + i)
                        activate(c, x + 1 + i, 1 - i, range(2, KI))
                matrix_s(c, E - 1, 1)
                activate(c, E - 1, 1, range(1))
                outputs_high(c, E - 2, 0)
                activate(c, E - 1, 1, range(1, 2))
                outputs_low(c, E - 2)
                activate(c, E - 1, 1, range(2, KI))
                outputs_high(c, E - 1, 1)
                outputs_low(c, E - 1)

            experts(0)
            dve.wait_ge(ps[0]["scat"], E)
            dve.wait_ge(s_flag, 1)
            with dve.If(dve.value_load(flag[0:1, 0:1]) > 0):
                for c in range(1, PASSES):
                    experts(c)
                    dve.wait_ge(ps[c]["scat"], E)
            for n in range(2):
                for m in range(KH):
                    last = dve.tensor_tensor(h[:, m, half(n)], bank[:, 2 * m + n, 0:NT], h[:, m, half(n)], ALU.add)
                last.then_inc(s_add, 1)

            ln_pair(LN_ATT)

            dve.wait_ge(s_absp, 1)
            link(dve, dve.tensor_scalar(wsi[:], bank[:, 7, 0:2], 1.0 / (H * I), 1e-5, ALU.mult, ALU.max))
            link(dve, dve.reciprocal(ws[:], wsi[:]))
            link(dve, dve.reciprocal(wsi[:], ws[:]))
            for c, (w, q) in enumerate(((w1, q1), (w2, q2))):
                flat = w.rearrange("p k n -> p (k n)")
                dve.tensor_scalar(qtmp[:, 0, :], flat, ws[:, c:c + 1], -0.5, ALU.mult, ALU.is_lt).then_inc(s_v, 1)
                dve.tensor_scalar(qtmp[:, 1, :], flat, ws[:, c:c + 1], 0.5, ALU.mult, ALU.is_gt).then_inc(s_v, 1)
                chain[0] += 2
                dve.wait_ge(s_v, chain[0])
                ins = dve.tensor_tensor(q[:].rearrange("p k n -> p (k n)"), qtmp[:, 1, :], qtmp[:, 0, :], ALU.subtract)
                link(dve, ins)
            gbv = vec[:, V_GB2:V_GB2 + 16].rearrange("p (k c) -> p k c", c=2)
            link(dve, dve.tensor_copy(vh[:], gbv))
            dve.tensor_tensor(vl[:], gbv, vh[:].bitcast(F32), ALU.subtract).then_inc(s_q2, 1)

            def softmax_in(t):
                dve.wait_ge(s_sc, t + 1)
                if t >= NSC:
                    dve.wait_ge(s_ptp, t - NSC + 1)
                x, b = sc[t % NSC], (0, 5)[t % 2]
                s4 = bank[0:AT, b:b + 2, 0:4 * AT].rearrange("p b (e t) -> p b e t", e=4)
                link(dve, dve.tensor_reduce(rmax[t % 2][:].rearrange("p (b e) -> p b e", b=2), s4, AX_X, ALU.max))
                dve.tensor_tensor(x.rearrange("p (b e) t -> p b e t", b=2), s4,
                                  rmax[t % 2][:].rearrange("p (b e o) -> p b e o", b=2, o=1).broadcast_to([AT, 2, 4, AT]),
                                  ALU.subtract).then_inc(s_scf, 1)

            def softmax_out(t):
                x = sc[t % NSC]
                dve.wait_ge(s_ex, t + 1)
                link(dve, dve.tensor_reduce(rsum[:], x[:], AX_X, ALU.add))
                link(dve, dve.scalar_tensor_tensor(out=rden[:], in0=gex[:, t, :], scalar=1.0, in1=rsum[:],
                                                   op0=ALU.add, op1=ALU.mult))
                link(dve, dve.reciprocal(rden[:], rden[:]))
                dve.tensor_tensor(x[:], x[:], rden[:].rearrange("p (e o) -> p e o", o=1).broadcast_to([AT, HEADS, AT]),
                                  ALU.mult).then_inc(s_pn, 1)

            softmax_in(0)
            for t in range(NAT):
                if t + 1 < NAT:
                    softmax_in(t + 1)
                softmax_out(t)
                if t == 0:
                    dve.wait_ge(s_gbp, 1)
                    link(dve, dve.tensor_scalar(gb[:], bank[:, 7, 0:4].rearrange("p (m c) -> p m c", c=2), wsi[:, 1:2],
                                                None, ALU.mult))
                    for m in range(KH):
                        link(dve, dve.tensor_tensor(gb[:, m, 1:2], gb[:, m, 1:2], vec[:, V_B2 + m:V_B2 + m + 1], ALU.add))
                    dve.tensor_scalar(gbn[:], gb[:, :, 1], -1.0, None, ALU.mult).then_inc(s_gb, 1)
            def add_attention(n):
                dve.wait_ge(s_wo, n + 1)
                dve.tensor_tensor(h[:, :, half(n)], bank[:, 2 * n:2 * n + 2, 0:NT], h[:, :, half(n)],
                                  ALU.add).then_inc(s_ha, 1)

            def split_rows(n):
                dve.wait_ge(s_aff, affine_count(LN_MLP + n))
                link(dve, dve.tensor_copy(xh[n], xn[:, :, half(n)]))
                dve.tensor_tensor(xl[n], xn[:, :, half(n)], xh[n].bitcast(F32), ALU.subtract).then_inc(s_xs, 1)

            add_attention(0)
            ln_var(LN_MLP)
            ln_root(LN_MLP)
            add_attention(1)
            ln_norm(LN_MLP)
            ln_var(LN_MLP + 1)
            split_rows(0)
            ln_root(LN_MLP + 1)
            ln_norm(LN_MLP + 1)
            split_rows(1)

            def split_hidden(q):
                n, k = q // KI, q % KI
                dve.wait_ge(s_gel, q + 1)
                if q >= YB:
                    dve.wait_ge(s_w2, q - YB + 1)
                g2 = vec[:, V_GB2 + 2 * k:V_GB2 + 2 * k + 1]
                high = dve.tensor_scalar(yh[q % YB], gy[n][:, k, :], g2, None, ALU.mult)
                high.then_inc(s_v, 1)
                chain[0] += 1
                if k >= 1:
                    to, i = ysum[n], LN_OUT + n
                    if k == 1:
                        dve.wait_ge(s_st, i - 1)
                    else:
                        dve.wait_ge(s_accy, n * (KI - 1) + k - 1)
                    dve.tensor_tensor(to, gy[n][:, 0, :] if k == 1 else to, gy[n][:, k, :], ALU.add).then_inc(s_accy, 1)
                dve.wait_ge(s_v, chain[0])
                dve.scalar_tensor_tensor(out=yl[q % YB], in0=gy[n][:, k, :], scalar=g2, in1=yh[q % YB].bitcast(F32),
                                         op0=ALU.mult, op1=ALU.subtract).then_inc(s_ys, 1)

            def take_product(n):
                dve.wait_ge(s_w2, (n + 1) * KI)
                dve.wait_ge(s_bc, LN_OUT + n + 1)
                tmp, root = zz[0] if n == 0 else tt[0], aa[n]
                link(dve, dve.tensor_copy(root[:, 0, :], bank[:, 5, 0:NT]))
                dve.scalar_tensor_tensor(out=tmp[:], in0=bank[:, 2:4, 0:NT], scalar=wsi[:, 1:2],
                                         in1=root[:, 0:1, :].broadcast_to([P, KH, NT]), op0=ALU.mult,
                                         op1=ALU.mult).then_inc(s_norm, 1)

            def close(n):
                tmp, tmp2 = (zz, tt)[n]
                dve.wait_ge(s_norm, LN_OUT + n + 1)
                dve.wait_ge(s_mg, n + 1)
                link(dve, dve.tensor_tensor(tmp[:], tmp[:], tmp2[:], ALU.subtract))
                dve.tensor_tensor(h[:, :, half(n)], h[:, :, half(n)], tmp[:], ALU.add).then_inc(s_fin, 1)

            for q in range(2 * KI):
                split_hidden(q)
                if q == KI + 1:
                    ln_var(LN_OUT)
                    ln_root(LN_OUT)
                    take_product(0)
            ln_var(LN_OUT + 1)
            close(0)
            ln_root(LN_OUT + 1)
            take_product(1)
            close(1)


def kernel(**inputs):
    import numpy as np
    import concourse.bacc as bacc
    from concourse.bass_utils import run_bass_kernel_spmd

    a = {k: np.asarray(v) for k, v in inputs.items()}
    c = np.ascontiguousarray
    px = a["x"].reshape(B, 3, 6, 16, 6, 16).transpose(0, 1, 3, 5, 2, 4).reshape(T, FLAT)

    def cols(v):
        return v.reshape(-1, P).T

    gru = np.stack([np.stack([a[f"L0_attn_{d}_W{g}"] for g in "zh"], 1) for d in ("fwd", "bwd")], 1)
    bias = [np.stack([a["L0_attn_fwd_b" + g], a["L0_attn_bwd_b" + g]], 1) for g in "zh"]
    gb2 = np.stack([cols(a["L1_ffn_ln2_g"]), cols(a["L1_ffn_ln2_b"])], 2).reshape(P, 16)
    vecs = np.concatenate([cols(bias[0]), cols(bias[1]), cols(a["L0_attn_ln_gamma"]), cols(a["L0_attn_ln_beta"]),
                           cols(a["L0_attn_fusion_b"]), cols(a["L1_attn_rms_w"]), cols(a["L1_ffn_ln1_g"]),
                           cols(a["L1_ffn_ln1_b"]), cols(a["L1_ffn_b1"]), gb2, cols(a["L1_ffn_b2"])], 1)
    qkv = np.concatenate([a[f"L1_attn_w{n}"].transpose(1, 0, 2).reshape(H, HEADS * DH) for n in "qkv"], 1)
    arrays = {
        "patches": px.T, "w_tok": a["L0_tok_W"], "w_gru": gru.transpose(0, 1, 2, 4, 3),
        "w_fus": a["L0_attn_fusion_W"].T, "vecs": vecs, "w_gate": a["L0_ffn_gate_w"].T,
        "w_up": a["L0_ffn_gate_up_proj"].transpose(0, 2, 1), "w_down": a["L0_ffn_down_proj"].transpose(0, 2, 1),
        "w_qkv": qkv, "w_gates": a["L1_attn_w_gates"][:, [0, 2, 4, 6, 1, 3, 5, 7]], "w_o": a["L1_attn_wo"].reshape(HEADS * DH, H),
        "w_1": a["L1_ffn_w1"].T, "w_2": a["L1_ffn_w2"].T,
    }
    arrays = {k: c(v) for k, v in arrays.items()}
    nc = bacc.Bacc("TRN2", target_bir_lowering=False, num_devices=1)
    args = [nc.dram_tensor(k, v.shape, mybir.dt.from_np(v.dtype), kind="ExternalInput").ap() for k, v in arrays.items()]
    out = nc.dram_tensor("tower_out", (T, H), F32, kind="ExternalOutput").ap()
    tower(nc, *args, out)
    r = run_bass_kernel_spmd(nc, [arrays], core_ids=[0])
    return r.results[0]["tower_out"].reshape(B, S, H)
```
